# Optimizing a Trainium2 kernel written in Bass

```python
import numpy as np
import jax
import jax.numpy as jnp

def _softmax(x, axis=-1):
    return jax.nn.softmax(x, axis=axis)

def _gelu(x):
    return jax.nn.gelu(x, approximate=True)

def _silu(x):
    return jax.nn.silu(x)

def _sigmoid(x):
    return jax.nn.sigmoid(x)

def _layernorm(x, axis=-1, eps=1e-05):
    m = jnp.mean(x, axis=axis, keepdims=True)
    v = jnp.var(x, axis=axis, keepdims=True)
    return (x - m) / jnp.sqrt(v + eps)

def _scatter_add(tgt, idx, src, axis=0):
    return tgt.at[idx].add(src)

def _segment_sum(src, seg, n):
    return jax.ops.segment_sum(src, seg, n)
kernel_name = 'mk_recurrent_d1_jaxref_r4_e8a0e9'

def setup_inputs(seed: int=0):
    np.random.seed(seed)
    _w = jnp.asarray

    def _L0_attn_setup():
        import jax, jax.numpy as jnp
        import numpy as np
        N_HEAD = 16
        WINDOW = 128
        CAUSAL = False

        def _window_attention(x, w_in, b_in, w_out, b_out):
            B, T, D = x.shape
            H = N_HEAD
            hd = D // H
            scale = 1.0 / jnp.sqrt(jnp.float32(hd))
            qkv = jnp.einsum('btd,ed->bte', x, w_in) + b_in
            q, k, v = jnp.split(qkv, 3, axis=-1)
            q = q.reshape(B, T, H, hd).transpose(0, 2, 1, 3)
            k = k.reshape(B, T, H, hd).transpose(0, 2, 1, 3)
            v = v.reshape(B, T, H, hd).transpose(0, 2, 1, 3)
            scores = jnp.einsum('bhqd,bhkd->bhqk', q, k) * scale
            idx = jnp.arange(T)
            diff = idx[:, None] - idx[None, :]
            if CAUSAL:
                allowed = (diff >= 0) & (diff <= WINDOW)
            else:
                allowed = jnp.abs(diff) <= WINDOW
            NEG = jnp.float32(-1e+30)
            scores = jnp.where(allowed[None, None, :, :], scores, NEG)
            attn = jax.nn.softmax(scores, axis=-1)
            ctx = jnp.einsum('bhqk,bhkd->bhqd', attn, v)
            ctx = ctx.transpose(0, 2, 1, 3).reshape(B, T, D)
            out = jnp.einsum('btd,ed->bte', ctx, w_out) + b_out
            return x + out
        key = jax.random.key(seed)
        ks = jax.random.split(key, 5)
        B, T, D = (1, 1024, 256)
        x = jax.random.normal(ks[0], (B, T, D), dtype=jnp.float32)
        w_in = jax.random.normal(ks[1], (3 * D, D), dtype=jnp.float32) * 0.02
        b_in = jax.random.normal(ks[2], (3 * D,), dtype=jnp.float32) * 0.02
        w_out = jax.random.normal(ks[3], (D, D), dtype=jnp.float32) * 0.02
        b_out = jax.random.normal(ks[4], (D,), dtype=jnp.float32) * 0.02
        return {'x': x, 'w_in': w_in, 'b_in': b_in, 'w_out': w_out, 'b_out': b_out}
    _L0_attn_in = _L0_attn_setup()

    def _L0_ffn_setup():
        import jax, jax.numpy as jnp
        import numpy as np
        B, S, H, I, E = (2, 1024, 256, 128, 8)
        key = jax.random.key(seed)
        ks = jax.random.split(key, 5)
        scale_h = 1.0 / np.sqrt(H)
        scale_i = 1.0 / np.sqrt(I)
        return {'hidden_states': jax.random.normal(ks[0], (B, S, H), dtype=jnp.float32), 'gate_w': jax.random.normal(ks[1], (E, H), dtype=jnp.float32) * scale_h, 'w_gate': jax.random.normal(ks[2], (E, I, H), dtype=jnp.float32) * scale_h, 'w_up': jax.random.normal(ks[3], (E, I, H), dtype=jnp.float32) * scale_h, 'w_down': jax.random.normal(ks[4], (E, H, I), dtype=jnp.float32) * scale_i}
    _L0_ffn_in = _L0_ffn_setup()
    _d = {'L0_attn_x': _L0_attn_in['x'], 'L0_attn_w_in': _L0_attn_in['w_in'], 'L0_attn_b_in': _L0_attn_in['b_in'], 'L0_attn_w_out': _L0_attn_in['w_out'], 'L0_attn_b_out': _L0_attn_in['b_out'], 'L0_ffn_gate_w': _L0_ffn_in['gate_w'], 'L0_ffn_w_gate': _L0_ffn_in['w_gate'], 'L0_ffn_w_up': _L0_ffn_in['w_up'], 'L0_ffn_w_down': _L0_ffn_in['w_down']}
    _x0 = _d['L0_attn_x']
    _d['L0_attn_x'] = jax.random.normal(jax.random.fold_in(jax.random.key(seed), 1), (16, 512, 256), dtype=_x0.dtype)
    del _x0
    return _d

def reference(L0_attn_x, L0_attn_w_in, L0_attn_b_in, L0_attn_w_out, L0_attn_b_out, L0_ffn_gate_w, L0_ffn_w_gate, L0_ffn_w_up, L0_ffn_w_down):

    def _L0_attn_ref(x, w_in, b_in, w_out, b_out):
        import jax, jax.numpy as jnp
        import numpy as np
        N_HEAD = 16
        WINDOW = 128
        CAUSAL = False

        def _window_attention(x, w_in, b_in, w_out, b_out):
            B, T, D = x.shape
            H = N_HEAD
            hd = D // H
            scale = 1.0 / jnp.sqrt(jnp.float32(hd))
            qkv = jnp.einsum('btd,ed->bte', x, w_in) + b_in
            q, k, v = jnp.split(qkv, 3, axis=-1)
            q = q.reshape(B, T, H, hd).transpose(0, 2, 1, 3)
            k = k.reshape(B, T, H, hd).transpose(0, 2, 1, 3)
            v = v.reshape(B, T, H, hd).transpose(0, 2, 1, 3)
            scores = jnp.einsum('bhqd,bhkd->bhqk', q, k) * scale
            idx = jnp.arange(T)
            diff = idx[:, None] - idx[None, :]
            if CAUSAL:
                allowed = (diff >= 0) & (diff <= WINDOW)
            else:
                allowed = jnp.abs(diff) <= WINDOW
            NEG = jnp.float32(-1e+30)
            scores = jnp.where(allowed[None, None, :, :], scores, NEG)
            attn = jax.nn.softmax(scores, axis=-1)
            ctx = jnp.einsum('bhqk,bhkd->bhqd', attn, v)
            ctx = ctx.transpose(0, 2, 1, 3).reshape(B, T, D)
            out = jnp.einsum('btd,ed->bte', ctx, w_out) + b_out
            return x + out
        return _window_attention(x, w_in, b_in, w_out, b_out)

    def _L0_ffn_ref(hidden_states, gate_w, w_gate, w_up, w_down):
        import jax, jax.numpy as jnp
        import numpy as np
        B, S, H, I, E = (2, 1024, 256, 128, 8)
        b, s, h = hidden_states.shape
        x = hidden_states.reshape(-1, h)
        logits = x @ gate_w.T
        top_v = jnp.max(logits, axis=-1)
        sel = jnp.argmax(logits, axis=-1)
        rw = jax.nn.sigmoid(top_v)
        out = jnp.zeros_like(x)
        n_exp = gate_w.shape[0]
        for e in range(n_exp):
            mask = (sel == e).astype(x.dtype)
            xs = x * (rw * mask)[:, None]
            g = xs @ w_gate[e].T
            u = xs @ w_up[e].T
            out = out + u * jax.nn.silu(g) @ w_down[e].T
        return out.reshape(b, s, h)
    x = L0_attn_x
    xn = _layernorm(x, axis=-1)
    s = _L0_attn_ref(xn, L0_attn_w_in, L0_attn_b_in, L0_attn_w_out, L0_attn_b_out)
    g = _silu(_L0_ffn_ref(xn, L0_ffn_gate_w, L0_ffn_w_gate, L0_ffn_w_up, L0_ffn_w_down))
    x = x + s * g
    return x

_drawn_inputs = setup_inputs


def setup_inputs(seed=0):
    import zlib

    import numpy as np

    out = dict(_drawn_inputs(seed))
    spreads = {}
    factors = {'L0_attn_w_in': 8.0, 'L0_attn_b_in': 8.0, 'L0_attn_w_out': 8.0, 'L0_attn_b_out': 8.0}
    for name, (base, spread) in spreads.items():
        noise = np.random.default_rng([zlib.crc32(name.encode()), seed]).standard_normal(out[name].shape)
        drawn = base * np.exp(spread * noise) if base else spread * noise
        out[name] = jnp.asarray(drawn.astype(out[name].dtype))
    for name, factor in factors.items():
        out[name] = (out[name] * factor).astype(out[name].dtype)
    return out
```

```python
from contextlib import ExitStack

import concourse.bass as bass
from concourse import mybir

ALU = mybir.AluOpType
ACT = mybir.ActivationFunctionType
F32 = mybir.dt.float32
F32R = mybir.dt.float32r
BF16 = mybir.dt.bfloat16
I32 = mybir.dt.int32
U32 = mybir.dt.uint32
AX_X = mybir.AxisListType.X

P = 128
NEG = -1e30
EPS = 1e-5
PRODUCTS = ((0, 0), (0, 1), (1, 0))


def build(nc, x, w_qkv_t, b_in, w_out_t, b_out, gate_t, w_gate_t, w_up_t, w_down_t, out):
    SEQS, T, D = x.shape
    E, _, I = w_gate_t.shape
    HEADS = 16
    HD = D // HEADS
    N = SEQS * T
    TILES = N // P
    QT = T // P
    DC = D // P
    UNIT_HEADS = HEADS // 2
    PAIRS = UNIT_HEADS // 2
    SCALE = 1.0 / HD ** 0.5
    FT = TILES + E
    FG = FT // 4
    ROWS = FT * P
    DUMP = ROWS
    assert (T, D, I, HD, QT, FT % 4) == (512, 256, 128, 16, 4, 0)

    x_g = x.rearrange("s (t p) d -> s p t d", p=P)
    out_g = out.rearrange("s (t p) d -> s p t d", p=P)
    xn_dram = nc.dram_tensor("xn_scratch", [SEQS, P, QT, D], F32).ap()
    sorted_dram = nc.dram_tensor("sorted_scratch", [ROWS + 2 * E * P, D], F32).ap()
    y_dram = nc.dram_tensor("expert_out_scratch", [ROWS, D], F32).ap()
    parts_dram = nc.dram_tensor("parts_scratch", [2, 4, P, T], F32).ap()
    max_dram = nc.dram_tensor("max_scratch", [2, UNIT_HEADS, T], F32).ap()

    with ExitStack() as ctx:
        def sb(name, shape, dt=F32):
            return ctx.enter_context(nc.sbuf_tensor(name, shape, dt))

        ident = sb("ident", [P, P])
        ident_b = sb("ident_b", [P, P], BF16)
        upper_b = sb("upper_b", [P, P], BF16)
        ones_b = sb("ones_b", [P, P], BF16)
        mask_b = sb("mask_b", [P, 2, P], BF16)
        ones64 = sb("ones64", [P, TILES])
        eps_t = sb("eps_t", [P, 1])
        b_qk = sb("b_qk", [P, 4])
        b_v = sb("b_v", [P, D])
        b_o = sb("b_o", [P, D])
        stage = sb("stage", [P, E * 3 * D])
        stage_qkv = stage[:, 0:DC * 3 * D].rearrange("p (c n) -> p c n", c=DC)
        stage_o = stage[:, DC * 3 * D:DC * 4 * D].rearrange("p (c n) -> p c n", c=DC)
        stage_gate = stage[:, DC * 4 * D:DC * (4 * D + E)].rearrange("p (c e) -> p c e", c=DC)
        w_qkv = sb("w_qkv", [P, 2, DC, 3 * D], F32R)
        w_o = sb("w_o", [P, 2, DC, D], F32R)
        w_gl = sb("w_gl", [P, 2, DC, E], F32R)
        w_gu = sb("w_gu", [P, 2, E * DC * 2 * I], F32R)
        w_dn = sb("w_dn", [P, 2, E * D], F32R)

        scores_and_values = sb("scores_and_values", [P, 2, TILES * E])
        logits, route_a = (scores_and_values[:, n].rearrange("p (t e) -> p t e", e=E) for n in range(2))
        one_hot = sb("one_hot", [P, TILES, E])
        one_hot_b = sb("one_hot_b", [P, TILES, E], BF16)
        top = sb("top", [P, TILES])
        weight = sb("weight", [P, TILES])
        rev = sb("rev", [P, E])
        iota_t = sb("iota_t", [P, TILES])
        iota_f = sb("iota_f", [P, FT])
        small = sb("small", [P, 16, E])
        position = sb("position", [P, TILES], I32)
        pad_position = sb("pad_position", [P, 2 * E], I32)
        expert_of = sb("expert_of", [P, FT], I32)
        pos4 = sb("pos4", [P, 2, 4], I32)

        x_in = sb("x_in", [P, 2, QT, D])
        bn = sb("bn", [P, 2, QT, 6])
        mv = sb("mv", [P, 2, QT, 2])
        sd = sb("sd", [P, 2, QT])
        rstd = sb("rstd", [P, 2, QT])
        xn = sb("xn", [P, 2, QT, D])
        cmp_f = x_in[:, 0].rearrange("p t d -> p (t d)")[:, 0:FT * E].rearrange("p (f e) -> p f e", e=E)
        by_e = x_in[:, 1, 0:2].rearrange("p t d -> p (t d)").rearrange("p (e t) -> p e t", e=E)
        cum = x_in[:, 1, 2:4].rearrange("p t d -> p (t d)").rearrange("p (e t) -> p e t", e=E)
        xt = [sb(f"xt{b}", [P, 2, DC, T], F32R) for b in range(2)]

        parts = sb("parts", [P, 4, T])
        stack = [sb(f"stack{c}", [P, 2, PAIRS, T], F32R) for c in range(2)]
        v_stage = scores_and_values[:].rearrange("p a n -> p (a n)").rearrange("p (t h d) -> p t h d", t=QT, d=HD)
        x_next = sb("x_next", [P, QT, D])
        v_aug = [sb(f"v_aug{c}", [P, QT, UNIT_HEADS, 32]) for c in range(2)]
        neg_max = sb("neg_max", [P, 2, QT, 4])
        max_parts = sb("max_parts", [P, QT, 4, 2])
        max_t = sb("max_t", [8, T])
        probs = stage[:, 0:16 * 3 * P].rearrange("p (r h q) -> p r h q", r=4, h=4)
        raw = sb("raw", [P, 4, T])
        recip = sb("recip", [P, HEADS])
        ctx_n = sb("ctx_n", [P, QT, HEADS, HD])
        s_sum = sb("s_sum", [P, D])
        gated = x_in[:, 1]
        y_in = xn[:, 1]

        xs = ctx_n[:].rearrange("p t h d -> p t (h d)")
        tanh_g, act_g, hid = (parts[:, n].rearrange("p (t i) -> p t i", t=4) for n in range(3))
        hid_t = sb("hid_t", [P, 2, 4 * P], F32R)
        ctx_t = hid_t[:, :, 0:DC * P].rearrange("p a (c t) -> p a c t", c=DC)
        tanh_y = raw[:, 0:2].rearrange("p a n -> p (a n)").rearrange("p (t d) -> p t d", t=4)
        y_out = raw[:, 2:4].rearrange("p a n -> p (a n)").rearrange("p (t d) -> p t d", t=4)

        ps = ctx.enter_context(nc.psum_tensor("ps", [P, 8, T], F32))

        names = """small_loaded weights_loaded weights_split consts_pool x_loaded0 x_loaded1 bn_done stats_done sd_done
            rstd_done xn_done xn_stored0 xn_stored1 rows_turned rows_hi rows_lo logits_done logits_kept routed route_link
            tanh_done onehot_ready counts_done positions_ready xn_again0 xn_again1 scaled padded pos_copied scattered0
            scattered1 experts_in experts_turned experts_hi experts_lo gu_done tanh_g_done act_g_done hid_done hid_turned
            hid_hi hid_lo y_done tanh_y_done y_ready y_stored next_loaded next_turned next_hi next_lo proj_done
            parts_hi parts_lo parts_written v_done v_staged v_copied stack_ready0 stack_ready1 s_done s_maxed max_hi
            max_lo max_turned max_evacuated max_written m_ready0 m_ready1 st_done ex_done masked pv_done raw_done
            raw_turned recip_done ctx_done ctx_turned ctx_hi ctx_lo o_done sum_done gated_done residual_loaded
            residual_ready y_gathered out_ready out_stored waits_passed""".split()
        sem = {name: ctx.enter_context(nc.semaphore(name)) for name in names}

        def carried(eng):
            eng.sem_inc(sem["waits_passed"], 1)

        def later(i, n):
            return not isinstance(i, int) or i >= n

        def product(dst, lhs, rhs, chunks, mm):
            todo = [(c, a, b) for c in range(chunks) for a, b in PRODUCTS]
            for n, (c, a, b) in enumerate(todo):
                last = mm(dst, lhs(a, c), rhs(b, c), start=(n == 0), stop=(n == len(todo) - 1))
            return last

        class Step:
            def __init__(self, i, c):
                inner = not isinstance(i, int)
                u = 2 * i + c
                self.u = u
                self.project = inner or i <= SEQS - 2
                self.load_next = c == 0 and (inner or i <= SEQS - 3)
                self.turn = c == 1 and (inner or i <= SEQS - 3)
                self.maxima = inner or -1 <= u <= 2 * SEQS - 2
                self.maxima_end = inner or 0 <= u <= 2 * SEQS - 1
                self.probs = inner or 0 <= u <= 2 * SEQS - 1
                self.probs_end = inner or 1 <= u <= 2 * SEQS
                self.output = inner or 1 <= i <= SEQS

        OUTPUT_JOBS = [
            {1: ("turn", 0), 2: ("turn", 1), 3: ("turn", 2), 4: ("turn", 3), 5: ("back", 0), 6: ("out", 0), 7: ("back", 1)},
            {0: ("out", 1), 1: ("back", 2), 2: ("out", 2), 3: ("back", 3), 4: ("out", 3)},
        ]
        none = (None, None)

        def attention(eng, step):
            for i in (-1, 0, 1):
                for c in range(2):
                    step(i, c, Step(i, c))
            with eng.Fori(2, SEQS - 2) as i:
                for c in range(2):
                    step(i, c, Step(i, c))
            for i in range(SEQS - 2, SEQS + 1):
                for c in range(2):
                    step(i, c, Step(i, c))

        def key_span(tile):
            lo, hi = max(0, tile - 1), min(QT - 1, tile + 1)
            return lo, hi - lo + 1

        block = ctx.enter_context(nc.Block())

        @block.sync
        def _(sp):
            sp.dma_start(stage_gate, gate_t.rearrange("(c p) e -> p c e", p=P)).then_inc(sem["weights_loaded"], 16)
            sp.dma_start(x_in[:, 0], x_g[0]).then_inc(sem["x_loaded0"], 16)
            sp.dma_start(stage_qkv, w_qkv_t.rearrange("(c p) n -> p c n", p=P)).then_inc(sem["weights_loaded"], 16)
            sp.dma_start(stage_o, w_out_t.rearrange("(c p) n -> p c n", p=P)).then_inc(sem["weights_loaded"], 16)
            for n in range(4):
                sp.dma_start(b_qk[:, n:n + 1], b_in[n * P:(n + 1) * P].rearrange("(p o) -> p o", o=1)).then_inc(
                    sem["small_loaded"], 16)
            sp.dma_start(b_v[:], b_in[2 * D:3 * D].partition_broadcast(P)).then_inc(sem["small_loaded"], 16)
            sp.dma_start(b_o[:], b_out.partition_broadcast(P)).then_inc(sem["small_loaded"], 16)

            def load_rows(i, b, first=False):
                if not first:
                    sp.wait_ge(sem["xn_done"], i - 1)
                    carried(sp)
                sp.dma_start(x_in[:, b], x_g[i]).then_inc(sem[f"x_loaded{b}"], 16)

            def store_rows(i, b):
                sp.wait_ge(sem["xn_done"], i + 1)
                carried(sp)
                sp.dma_start(xn_dram[i], xn[:, b]).then_inc(sem[f"xn_stored{b}"], 16)

            load_rows(1, 1, first=True)
            with sp.Fori(0, SEQS // 2 - 1) as pair:
                store_rows(2 * pair, 0)
                load_rows(2 * pair + 2, 0)
                store_rows(2 * pair + 1, 1)
                load_rows(2 * pair + 3, 1)
            store_rows(SEQS - 2, 0)
            store_rows(SEQS - 1, 1)

            sp.wait_ge(sem["weights_split"], 3)
            gu = stage[:, 0:E * DC * 2 * I].rearrange("p (e c g i) -> p g c e i", e=E, c=DC, g=2)
            for g, w in enumerate((w_gate_t, w_up_t)):
                for c in range(DC):
                    sp.dma_start(gu[:, g, c], w[:, c * P:(c + 1) * P, :].rearrange("e p i -> p e i")).then_inc(
                        sem["weights_loaded"], 16)
            dn = stage[:, E * DC * 2 * I:].rearrange("p (e n) -> p e n", e=E)
            sp.dma_start(dn, w_down_t.rearrange("e i n -> i e n")).then_inc(sem["weights_loaded"], 16)

            sp.wait_ge(sem["xn_stored0"], 8 * SEQS)
            sp.wait_ge(sem["xn_stored1"], 8 * SEQS)
            sp.wait_ge(sem["rows_turned"], SEQS)
            sp.dma_start(xn[:, 0], xn_dram[0]).then_inc(sem["xn_again0"], 16)
            sp.dma_start(xn[:, 1], xn_dram[1]).then_inc(sem["xn_again1"], 16)
            with sp.Fori(1, SEQS // 2) as pair:
                for b in range(2):
                    sp.wait_ge(sem["scaled"], 2 * pair + b - 1)
                    carried(sp)
                    sp.dma_start(xn[:, b], xn_dram[2 * pair + b]).then_inc(sem[f"xn_again{b}"], 16)

            sp.wait_ge(sem["scattered0"], 8 * TILES)
            sp.wait_ge(sem["scattered1"], 8 * TILES)
            sp.wait_ge(sem["padded"], 16 * 2 * E)
            xs_dram = sorted_dram[0:ROWS].rearrange("(k t p) d -> k p t d", p=P, t=4)
            ys_dram = y_dram.rearrange("(k t p) d -> k p t d", p=P, t=4)

            def experts_load(k, first=False):
                if not first:
                    sp.wait_ge(sem["experts_turned"], k)
                    carried(sp)
                sp.dma_start(xs, xs_dram[k]).then_inc(sem["experts_in"], 16)

            def experts_store(k):
                sp.wait_ge(sem["y_ready"], k + 1)
                carried(sp)
                sp.dma_start(ys_dram[k], y_out).then_inc(sem["y_stored"], 16)

            experts_load(0, first=True)
            experts_load(1)
            with sp.Fori(2, FG) as k:
                experts_load(k)
                experts_store(k - 2)
            experts_store(FG - 2)
            experts_store(FG - 1)

            def store_maxima(u, g, c):
                sp.wait_ge(sem["max_evacuated"], 2 * u + g + 1)
                carried(sp)
                sp.dma_start(max_dram[g], max_t[:]).then_inc(sem["max_written"], 16)
                sp.wait_ge(sem["max_written"], 16 * (2 * u + g + 1))
                carried(sp)
                src = max_dram[g].rearrange("(p j l) t -> j l p t", j=2, l=2)
                for j in range(2):
                    r = 64 * j + 3 * HD
                    sp.dma_start(stack[c][r:r + 2, 0, 2 * g:2 * g + 2, :].bitcast(F32),
                                 src[j]).then_inc(sem[f"m_ready{g}"], 16)

            def load_stack(u, g, c):
                src = parts_dram[c].rearrange("b (j d p) t -> j d b (p t)", j=2, d=HD)
                for j in range(2):
                    for t, blocks in enumerate((slice(1, 3), slice(0, 3, 2), slice(1, 4, 2))):
                        r = 64 * j + HD * t
                        dst = stack[c][r:r + HD, :, 2 * g:2 * g + 2, :].rearrange("d b p t -> d b (p t)").bitcast(F32)
                        sp.dma_start(dst, src[j][:, blocks, 2 * g * T:2 * (g + 1) * T]).then_inc(
                            sem[f"stack_ready{g}"], 16)

            sp.dma_start(x_next[:], xn_dram[0]).then_inc(sem["next_loaded"], 16)

            def step(i, c, has):
                u = has.u
                if has.load_next:
                    sp.wait_ge(sem["next_turned"], 2 * (i + 2))
                    carried(sp)
                    sp.dma_start(x_next[:], xn_dram[i + 2]).then_inc(sem["next_loaded"], 16)
                if has.maxima_end:
                    store_maxima(u, 1, c)
                if has.project:
                    sp.wait_ge(sem["parts_lo"], 2 * (u + 2) + 2)
                    carried(sp)
                    sp.dma_start(parts_dram[c].rearrange("b r t -> r b t"), parts[:]).then_inc(sem["parts_written"], 16)
                    sp.wait_ge(sem["parts_written"], 16 * (u + 3))
                    carried(sp)
                    if later(i, 0):
                        sp.wait_ge(sem["st_done"], 32 * u + 16)
                        carried(sp)
                        sp.wait_ge(sem["stack_ready0"], 96 * (u + 2))
                        carried(sp)
                    elif c == 1:
                        sp.wait_ge(sem["stack_ready0"], 96 * (u + 2))
                    load_stack(u + 2, 0, c)
                if has.maxima:
                    store_maxima(u + 1, 0, 1 - c)
                if has.project:
                    if later(i, 0):
                        sp.wait_ge(sem["st_done"], 32 * u + 32)
                        carried(sp)
                        sp.wait_ge(sem["stack_ready1"], 96 * (u + 2))
                        carried(sp)
                    elif c == 1:
                        sp.wait_ge(sem["stack_ready1"], 96 * (u + 2))
                    load_stack(u + 2, 1, c)
                if c == 1 and has.output:
                    sp.wait_ge(sem["out_ready"], 4 * i)
                    carried(sp)
                    sp.dma_start(out_g[i - 1], gated).then_inc(sem["out_stored"], 16)
                if c == 1 and has.probs:
                    sp.dma_start(xn[:, 0], xn_dram[i]).then_inc(sem["residual_loaded"], 16)
                    sp.dma_start(x_in[:, 0], x_g[i]).then_inc(sem["residual_loaded"], 16)

            attention(sp, step)
            sp.wait_ge(sem["out_stored"], 16 * SEQS)

        @block.gpsimd
        def _(pool):
            g = nc.gpsimd
            g.memset(ident[:], 0.0)
            g.memset(upper_b[:], 1.0)
            g.memset(mask_b[:], 0.0)
            g.memset(ones_b[:], 1.0)
            g.memset(eps_t[:], EPS).then_inc(sem["consts_pool"], 1)
            pool.wait_ge(sem["consts_pool"], 1)
            g.affine_select(out=ident[:], in_=ident[:], compare_op=ALU.not_equal, fill=1.0, base=0,
                            pattern=[[-1, P]], channel_multiplier=1)
            g.affine_select(out=upper_b[:], in_=upper_b[:], compare_op=ALU.is_gt, fill=0.0, base=0,
                            pattern=[[1, P]], channel_multiplier=-1)
            g.affine_select(out=mask_b[:, 0], in_=mask_b[:, 0], compare_op=ALU.is_ge, fill=NEG, base=0,
                            pattern=[[1, P]], channel_multiplier=-1)
            g.affine_select(out=mask_b[:, 1], in_=mask_b[:, 1], compare_op=ALU.is_ge, fill=NEG, base=0,
                            pattern=[[-1, P]], channel_multiplier=1)
            g.iota(rev[:], pattern=[[-1, E]], base=E, channel_multiplier=0, allow_small_or_imprecise_dtypes=True)
            g.iota(iota_t[:], pattern=[[P, TILES]], base=0, channel_multiplier=0, allow_small_or_imprecise_dtypes=True)
            g.iota(iota_f[:], pattern=[[1, FT]], base=0, channel_multiplier=0, allow_small_or_imprecise_dtypes=True)
            g.iota(small[:, 0], pattern=[[0, E]], base=0, channel_multiplier=1, allow_small_or_imprecise_dtypes=True)
            g.iota(small[:, 1], pattern=[[P, E]], base=DUMP, channel_multiplier=1, allow_small_or_imprecise_dtypes=True)
            g.iota(small[:, 2], pattern=[[P, E]], base=0, channel_multiplier=1,
                   allow_small_or_imprecise_dtypes=True).then_inc(sem["consts_pool"], 1)
            pool.wait_ge(sem["consts_pool"], 2)
            g.tensor_copy(ident_b[:], ident[:]).then_inc(sem["consts_pool"], 1)

            def rows_at(ap):
                return bass.IndirectOffsetOnAxis(ap=ap, axis=0)

            pool.wait_ge(sem["positions_ready"], 1)
            for n in range(2 * E):
                g.indirect_dma_start(out=sorted_dram[:, :], out_offset=rows_at(pad_position[:, n:n + 1]),
                                     in_=xs[:, 0, :], in_offset=None).then_inc(sem["padded"], 16)

            def scatter(i, b, first=False):
                if not first:
                    pool.wait_ge(sem[f"scattered{b}"], 32 * (i - b))
                    carried(pool)
                g.tensor_copy(pos4[:, b], position[:, bass.ds(i * 4, 4)]).then_inc(sem["pos_copied"], 1)
                pool.wait_ge(sem["pos_copied"], i + 1)
                carried(pool)
                pool.wait_ge(sem["scaled"], i + 1)
                carried(pool)
                for t in range(4):
                    g.indirect_dma_start(out=sorted_dram[:, :], out_offset=rows_at(pos4[:, b, t:t + 1]),
                                         in_=x_in[:, b, t, :], in_offset=None).then_inc(sem[f"scattered{b}"], 16)

            scatter(0, 0, first=True)
            scatter(1, 1, first=True)
            with pool.Fori(1, SEQS // 2) as pair:
                scatter(2 * pair, 0)
                scatter(2 * pair + 1, 1)

            pool.wait_ge(sem["small_loaded"], 96)
            pool.wait_ge(sem["y_stored"], 16 * FG)

            def step(i, c, has):
                u = has.u
                for n in range(8):
                    if has.probs:
                        item = n % 4
                        lo, span = key_span(item)
                        pool.wait_ge(sem["ex_done"], 32 * u + 4 * n + 4)
                        carried(pool)
                        if item > 0:
                            v = probs[:, item, :, 0:P]
                            last = g.affine_select(out=v, in_=v, compare_op=ALU.is_ge, fill=0.0, base=0,
                                                   pattern=[[0, 4], [1, P]], channel_multiplier=-1)
                        if item < QT - 1:
                            v = probs[:, item, :, (span - 1) * P:span * P]
                            last = g.affine_select(out=v, in_=v, compare_op=ALU.is_ge, fill=0.0, base=0,
                                                   pattern=[[0, 4], [-1, P]], channel_multiplier=1)
                        last.then_inc(sem["masked"], 1)
                    if n == 1 and has.maxima:
                        if c == 1 or not later(i, 0):
                            pool.wait_ge(sem["v_staged"], 2 * (i + 2))
                            carried(pool)
                        if later(u if isinstance(i, int) else i, 1):
                            pool.wait_ge(sem["pv_done"], 8 * u)
                            carried(pool)
                        half = (1 - c) * UNIT_HEADS
                        g.tensor_copy(v_aug[1 - c][:, :, :, 0:HD],
                                      v_stage[:, :, half:half + UNIT_HEADS, :]).then_inc(sem["v_copied"], 1)
                    if c == 0 and n in (2, 3, 4, 5) and has.output:
                        if n == 2:
                            pool.wait_ge(sem["residual_loaded"], 32 * i)
                            carried(pool)
                        g.tensor_tensor(xn[:, 0, n - 2], xn[:, 0, n - 2], b_o[:], ALU.add).then_inc(
                            sem["residual_ready"], 1)
                    kind, t = OUTPUT_JOBS[c].get(n - 1, none) if n else ((OUTPUT_JOBS[0][7]) if c else none)
                    if kind == "out" and has.output:
                        pool.wait_ge(sem["gated_done"], 4 * (i - 1) + t + 1)
                        carried(pool)
                        g.tensor_tensor(gated[:, t], gated[:, t], x_in[:, 0, t], ALU.add).then_inc(sem["out_ready"], 1)
                    if c == 1 and n >= 6 and has.probs:
                        if n == 6:
                            if later(i, 1):
                                pool.wait_ge(sem["y_gathered"], 64 * i)
                                carried(pool)
                            g.tensor_copy(pos4[:, 0], position[:, bass.ds(i * 4, 4)]).then_inc(sem["pos_copied"], 1)
                            pool.wait_ge(sem["pos_copied"], SEQS + i + 1)
                            carried(pool)
                            if later(i, 1):
                                pool.wait_ge(sem["gated_done"], 4 * i)
                                carried(pool)
                        for t in (0, 1) if n == 6 else (2, 3):
                            g.indirect_dma_start(out=y_in[:, t, :], out_offset=None, in_=y_dram[:, :],
                                                 in_offset=rows_at(pos4[:, 0, t:t + 1])).then_inc(sem["y_gathered"], 16)

            attention(pool, step)

        @block.scalar
        def _(act):
            a = nc.scalar

            def deviation(i, b):
                act.wait_ge(sem["stats_done"], i + 1)
                a.activation(sd[:, b, :], mv[:, b, :, 1], ACT.Sqrt, bias=eps_t[:]).then_inc(sem["sd_done"], 1)

            def rows_hi(i, b, first=False):
                act.wait_ge(sem["rows_turned"], i + 1)
                if not first:
                    act.wait_ge(sem["logits_done"], i - 1)
                a.activation(xt[b][:, 0], ps[:, 2 * b:2 * b + 2, :], ACT.Copy).then_inc(sem["rows_hi"], 1)

            act.wait_ge(sem["consts_pool"], 1)
            deviation(0, 0)
            deviation(1, 1)
            rows_hi(0, 0, first=True)
            deviation(2, 0)
            rows_hi(1, 1, first=True)
            with act.Fori(1, SEQS // 2 - 1) as pair:
                deviation(2 * pair + 1, 1)
                rows_hi(2 * pair, 0)
                deviation(2 * pair + 2, 0)
                rows_hi(2 * pair + 1, 1)
            deviation(SEQS - 1, 1)
            rows_hi(SEQS - 2, 0)
            rows_hi(SEQS - 1, 1)

            act.wait_ge(sem["routed"], 1)
            a.activation(weight[:], top[:], ACT.Tanh, scale=0.5).then_inc(sem["tanh_done"], 1)

            def two_banks(b):
                return ps[:, b:b + 2, :].rearrange("p b (t n) -> p (b t) n", t=2)

            def experts_hi(k, first=False):
                act.wait_ge(sem["experts_turned"], k + 1)
                if not first:
                    act.wait_ge(sem["gu_done"], k)
                a.activation(xt[1][:, 0], ps[:, 0:2, :], ACT.Copy).then_inc(sem["experts_hi"], 1)

            def gate_tanh(k, first=False):
                act.wait_ge(sem["gu_done"], k + 1)
                if not first:
                    act.wait_ge(sem["hid_done"], k)
                a.activation(tanh_g, two_banks(2)[:, :, 0:I], ACT.Tanh, scale=0.5).then_inc(sem["tanh_g_done"], 1)

            def hid_hi(k, first=False):
                act.wait_ge(sem["hid_turned"], k + 1)
                if not first:
                    act.wait_ge(sem["y_done"], k)
                a.activation(hid_t[:, 0], ps[:, 4, :], ACT.Copy).then_inc(sem["hid_hi"], 1)

            def result_tanh(k, first=False):
                act.wait_ge(sem["y_done"], k + 1)
                if not first:
                    act.wait_ge(sem["y_ready"], k)
                a.activation(tanh_y, two_banks(5), ACT.Tanh, scale=0.5).then_inc(sem["tanh_y_done"], 1)

            experts_hi(0, first=True)
            gate_tanh(0, first=True)
            experts_hi(1)
            hid_hi(0, first=True)
            gate_tanh(1)
            experts_hi(2)
            result_tanh(0, first=True)
            hid_hi(1)
            with act.Fori(2, FG - 1) as k:
                gate_tanh(k)
                experts_hi(k + 1)
                result_tanh(k - 1)
                hid_hi(k)
            gate_tanh(FG - 1)
            result_tanh(FG - 2)
            hid_hi(FG - 1)
            result_tanh(FG - 1)

            act.wait_ge(sem["small_loaded"], 96)

            def next_hi(job, ch):
                act.wait_ge(sem["next_turned"], job + 1)
                a.activation(xt[0][:, 0, ch], ps[:, 7, :], ACT.Copy).then_inc(sem["next_hi"], 1)

            next_hi(0, 0)
            next_hi(1, 1)

            def step(i, c, has):
                u = has.u

                def part_hi(n):
                    act.wait_ge(sem["proj_done"], 2 * (u + 2) + n + 1)
                    if n == 0 and (not isinstance(i, int) or u > -2):
                        act.wait_ge(sem["parts_written"], 16 * (u + 2))
                    col = 2 * n + c
                    a.activation(parts[:, 1 + n].bitcast(F32R), ps[:, 7, :], ACT.Identity,
                                 bias=b_qk[:, col:col + 1]).then_inc(sem["parts_hi"], 1)

                def exp(n, h):
                    lo, span = key_span(n % 4)
                    e = 4 * n + h
                    act.wait_ge(sem["st_done"], 32 * u + e + 1)
                    if h == 0 and (not isinstance(i, int) or 8 * u + n - 3 > 0):
                        act.wait_ge(sem["pv_done"], 8 * u + n - 3)
                    a.activation(probs[:, n % 4, h, 0:span * P], ps[:, 4 + e % 2, 0:span * P], ACT.Exp,
                                 scale=SCALE).then_inc(sem["ex_done"], 1)

                for n in range(8):
                    if has.project and n == 0:
                        part_hi(0)
                    if has.project and n == 2:
                        part_hi(1)
                    if has.turn and n in (3, 4):
                        next_hi(2 * (i + 2) + n - 3, n - 3)
                    if has.probs:
                        exp(n, 0)
                        exp(n, 1)
                        exp(n, 2)
                    kind, t = OUTPUT_JOBS[c].get(n, none)
                    if kind == "back" and has.output:
                        act.wait_ge(sem["ctx_turned"], 4 * (i - 1) + t + 1)
                        a.activation(ctx_t[:, 0], ps[:, 3, 0:DC * P].rearrange("p (c t) -> p c t", c=DC),
                                     ACT.Copy).then_inc(sem["ctx_hi"], 1)
                    if has.probs:
                        exp(n, 3)

            attention(act, step)

        @block.vector
        def _(dve):
            v = nc.vector
            links = [0]

            def link(ins):
                links[0] += 1
                ins.then_inc(sem["route_link"], 1)
                dve.wait_ge(sem["route_link"], links[0])

            v.memset(ones64[:], 1.0)
            v.memset(xs[:, 0, :], 0.0)
            for c in range(2):
                v.memset(v_aug[c][:], 1.0)
                for r in (32, 96):
                    v.memset(stack[c][r:r + 32, 1, :, :].bitcast(F32), 1.0)
            link(v.memset(small[:, 3], 0.0))

            def split(dst, src):
                link(v.tensor_copy(dst(0), src))
                return v.tensor_tensor(dst(1), src, dst(0).bitcast(F32), ALU.subtract)

            dve.wait_ge(sem["weights_loaded"], 48)
            split(lambda h: w_gl[:, h], stage_gate).then_inc(sem["weights_split"], 1)
            split(lambda h: w_qkv[:, h], stage_qkv).then_inc(sem["weights_split"], 1)
            split(lambda h: w_o[:, h], stage_o).then_inc(sem["weights_split"], 1)

            def statistics(i, b):
                dve.wait_ge(sem[f"x_loaded{b}"], 8 * (i - b) + 16)
                for t in range(QT):
                    last = v.bn_stats(bn[:, b, t], x_in[:, b, t])
                last.then_inc(sem["bn_done"], 1)
                dve.wait_ge(sem["bn_done"], i + 1)
                if not isinstance(i, int):
                    carried(dve)
                for t in range(QT):
                    last = v.bn_aggr(mv[:, b, t], bn[:, b, t])
                last.then_inc(sem["stats_done"], 1)

            def normalise(i, b, first=False):
                dve.wait_ge(sem["sd_done"], i + 1)
                v.reciprocal(rstd[:, b], sd[:, b]).then_inc(sem["rstd_done"], 1)
                dve.wait_ge(sem["rstd_done"], i + 1)
                if not first:
                    dve.wait_ge(sem[f"xn_stored{b}"], 8 * (i - b))
                    dve.wait_ge(sem["rows_turned"], i - 1)
                for t in range(QT):
                    last = v.tensor_scalar(xn[:, b, t], x_in[:, b, t], mv[:, b, t, 0:1], rstd[:, b, t:t + 1],
                                           ALU.subtract, ALU.mult)
                last.then_inc(sem["xn_done"], 1)

            def rows_lo(i, b):
                dve.wait_ge(sem["rows_hi"], i + 1)
                v.tensor_tensor(xt[b][:, 1], ps[:, 2 * b:2 * b + 2, :], xt[b][:, 0].bitcast(F32),
                                ALU.subtract).then_inc(sem["rows_lo"], 1)

            def keep_logits(i, b):
                dve.wait_ge(sem["logits_done"], i + 1)
                v.tensor_copy(logits[:, bass.ds(i * QT, QT), :],
                              ps[:, 4 + b, 0:QT * E].rearrange("p (t e) -> p t e", t=QT)).then_inc(sem["logits_kept"], 1)

            statistics(0, 0)
            normalise(0, 0, first=True)
            statistics(1, 1)
            normalise(1, 1, first=True)
            rows_lo(0, 0)
            with dve.Fori(1, SEQS // 2) as pair:
                statistics(2 * pair, 0)
                keep_logits(2 * pair - 2, 0)
                normalise(2 * pair, 0)
                rows_lo(2 * pair - 1, 1)
                statistics(2 * pair + 1, 1)
                keep_logits(2 * pair - 1, 1)
                normalise(2 * pair + 1, 1)
                rows_lo(2 * pair, 0)
            rows_lo(SEQS - 1, 1)
            keep_logits(SEQS - 2, 0)
            keep_logits(SEQS - 1, 1)
            dve.wait_ge(sem["logits_kept"], SEQS)

            tb = [P, TILES, E]
            dve.wait_ge(sem["consts_pool"], 3)
            link(v.reduce_max(top[:], logits, AX_X))
            v.tensor_tensor(route_a, logits, top[:].unsqueeze(2).to_broadcast(tb),
                            ALU.is_equal).then_inc(sem["routed"], 1)
            dve.wait_ge(sem["routed"], 1)
            link(v.tensor_tensor(route_a, route_a, rev[:].unsqueeze(1).to_broadcast(tb), ALU.mult))
            link(v.reduce_max(cum[:, 0, :], route_a, AX_X))
            link(v.tensor_tensor(one_hot[:], rev[:].unsqueeze(1).to_broadcast(tb),
                                 cum[:, 0, :].unsqueeze(2).to_broadcast(tb), ALU.is_equal))
            v.tensor_copy(one_hot_b[:], one_hot[:]).then_inc(sem["onehot_ready"], 1)
            dve.wait_ge(sem["tanh_done"], 1)
            link(v.tensor_scalar(weight[:], weight[:], 0.5, 0.5, ALU.mult, ALU.add))
            dve.wait_ge(sem["counts_done"], 1)
            before = ps[:, 0, :].rearrange("p (t e) -> p t e", e=E)
            total = ps[:, 1, :].rearrange("p (t e) -> p t e", e=E)
            for e in range(E):
                last = v.tensor_tensor_scan(cum[:, e, :], ones64[:], total[:, :, e], 0.0, ALU.mult, ALU.add)
            link(last)
            count, tiles, ends, base = (small[:, n] for n in (4, 5, 6, 7))
            link(v.tensor_copy(count, cum[:, :, TILES - 1]))
            link(v.tensor_tensor(by_e, count.unsqueeze(2).to_broadcast([P, E, TILES]),
                                 iota_t[:].unsqueeze(1).to_broadcast([P, E, TILES]), ALU.is_gt))
            link(v.reduce_sum(tiles, by_e, AX_X))
            link(v.tensor_tensor_scan(ends, ones64[:, 0:E], tiles, 0.0, ALU.mult, ALU.add))
            link(v.tensor_tensor(base, ends, tiles, ALU.subtract))
            link(v.tensor_scalar(base, base, float(P), None, ALU.mult))
            link(v.tensor_tensor(route_a, cum.rearrange("p e t -> p t e"), total, ALU.subtract))
            link(v.tensor_tensor(route_a, route_a, before, ALU.add))
            link(v.tensor_tensor(route_a, route_a, base.unsqueeze(1).to_broadcast(tb), ALU.add))
            link(v.tensor_tensor(route_a, route_a, one_hot[:], ALU.mult))
            link(v.reduce_sum(top[:], route_a, AX_X))
            link(v.tensor_copy(position[:], top[:]))
            pad, over, limit, tail = (small[:, n] for n in (9, 10, 11, 12))
            link(v.tensor_tensor(pad, base, count, ALU.add))
            link(v.tensor_tensor(pad, pad, small[:, 0], ALU.add))
            link(v.tensor_scalar(limit, ends, float(P), None, ALU.mult))

            def clip(idx, bound, dump_base, dst):
                link(v.tensor_tensor(over, idx, bound, ALU.is_ge))
                link(v.tensor_scalar(small[:, 13], small[:, 1], float(dump_base), None, ALU.add))
                link(v.tensor_tensor(small[:, 13], small[:, 13], idx, ALU.subtract))
                link(v.tensor_tensor(small[:, 13], small[:, 13], over, ALU.mult))
                link(v.tensor_tensor(small[:, 13], small[:, 13], idx, ALU.add))
                link(v.tensor_copy(dst, small[:, 13]))

            clip(pad, limit, 0, pad_position[:, 0:E])
            link(v.tensor_tensor(tail, small[:, 2], limit[:, E - 1:E].to_broadcast([P, E]), ALU.add))
            link(v.tensor_scalar(limit, small[:, 3], float(ROWS), None, ALU.add))
            clip(tail, limit, E * P, pad_position[:, E:2 * E])
            link(v.tensor_tensor(cmp_f, iota_f[:].unsqueeze(2).to_broadcast([P, FT, E]),
                                 ends.unsqueeze(1).to_broadcast([P, FT, E]), ALU.is_ge))
            link(v.reduce_sum(iota_f[:], cmp_f, AX_X))
            link(v.tensor_scalar(iota_f[:], iota_f[:], float(E - 1), None, ALU.min))
            v.tensor_copy(expert_of[:], iota_f[:]).then_inc(sem["positions_ready"], 1)

            def scale(i, b, first=False):
                dve.wait_ge(sem[f"xn_again{b}"], 8 * (i - b) + 16)
                if not first:
                    dve.wait_ge(sem[f"scattered{b}"], 32 * (i - b))
                w = weight[:, bass.ds(i * QT, QT)].unsqueeze(2).to_broadcast([P, QT, D])
                v.tensor_tensor(x_in[:, b], xn[:, b], w, ALU.mult).then_inc(sem["scaled"], 1)

            scale(0, 0, first=True)
            scale(1, 1, first=True)
            dve.wait_ge(sem["weights_loaded"], 16 * 8)
            split(lambda h: w_gu[:, h], stage[:, 0:E * DC * 2 * I]).then_inc(sem["weights_split"], 1)
            split(lambda h: w_dn[:, h], stage[:, E * DC * 2 * I:]).then_inc(sem["weights_split"], 1)
            with dve.Fori(1, SEQS // 2) as pair:
                scale(2 * pair, 0)
                scale(2 * pair + 1, 1)

            def two_banks(b):
                return ps[:, b:b + 2, :].rearrange("p b (t n) -> p (b t) n", t=2)

            def experts_lo(k):
                dve.wait_ge(sem["experts_hi"], k + 1)
                v.tensor_tensor(xt[1][:, 1], ps[:, 0:2, :], xt[1][:, 0].bitcast(F32), ALU.subtract).then_inc(
                    sem["experts_lo"], 1)

            def hid_lo(k):
                dve.wait_ge(sem["hid_hi"], k + 1)
                v.tensor_tensor(hid_t[:, 1], ps[:, 4, :], hid_t[:, 0].bitcast(F32), ALU.subtract).then_inc(sem["hid_lo"], 1)

            def gate(k, first=False):
                dve.wait_ge(sem["tanh_g_done"], k + 1)
                v.scalar_tensor_tensor(out=act_g, in0=tanh_g, scalar=1.0, in1=two_banks(2)[:, :, 0:I], op0=ALU.add,
                                       op1=ALU.mult).then_inc(sem["act_g_done"], 1)
                dve.wait_ge(sem["act_g_done"], k + 1)
                if not first:
                    dve.wait_ge(sem["hid_turned"], k)
                v.scalar_tensor_tensor(out=hid, in0=act_g, scalar=0.5, in1=two_banks(2)[:, :, I:2 * I], op0=ALU.mult,
                                       op1=ALU.mult).then_inc(sem["hid_done"], 1)

            def result(k, first=False):
                dve.wait_ge(sem["tanh_y_done"], k + 1)
                if not first:
                    dve.wait_ge(sem["y_stored"], 16 * k)
                v.scalar_tensor_tensor(out=y_out, in0=tanh_y, scalar=1.0, in1=two_banks(5), op0=ALU.add,
                                       op1=ALU.mult).then_inc(sem["y_ready"], 1)

            experts_lo(0)
            gate(0, first=True)
            experts_lo(1)
            hid_lo(0)
            gate(1)
            experts_lo(2)
            result(0, first=True)
            hid_lo(1)
            with dve.Fori(2, FG - 1) as k:
                gate(k)
                experts_lo(k + 1)
                result(k - 1)
                hid_lo(k)
            gate(FG - 1)
            result(FG - 2)
            hid_lo(FG - 1)
            result(FG - 1)

            def next_lo(job, ch):
                dve.wait_ge(sem["next_hi"], job + 1)
                v.tensor_tensor(xt[0][:, 1, ch], ps[:, 7, :], xt[0][:, 0, ch].bitcast(F32), ALU.subtract).then_inc(
                    sem["next_lo"], 1)

            next_lo(0, 0)
            next_lo(1, 1)

            def step(i, c, has):
                u = has.u

                def part_lo(n):
                    hi, lo = (1, 0) if n == 0 else (2, 3)
                    dve.wait_ge(sem["parts_hi"], 2 * (u + 2) + n + 1)
                    v.scalar_tensor_tensor(out=parts[:, lo].bitcast(F32R), in0=ps[:, 7, :],
                                           scalar=b_qk[:, 2 * n + c:2 * n + c + 1], in1=parts[:, hi], op0=ALU.add,
                                           op1=ALU.subtract).then_inc(sem["parts_lo"], 1)

                def stage_values(n):
                    dve.wait_ge(sem["v_done"], 2 * (i + 1) + n + 1)
                    if n == 0 and later(i, 0):
                        dve.wait_ge(sem["v_copied"], 2 * (i + 1))
                    bias = b_v[:].rearrange("p (h d) -> p h d", d=HD).unsqueeze(1).to_broadcast([P, 2, HEADS, HD])
                    v.tensor_tensor(v_stage[:, 2 * n:2 * n + 2], ps[:, 7, :].rearrange("p (t h d) -> p t h d", t=2, d=HD),
                                    bias, ALU.add).then_inc(sem["v_staged"], 1)

                def split_maxima(w, g):
                    m = 2 * w + g
                    dve.wait_ge(sem["s_maxed"], 32 * w + 16 * g + 16)
                    if not isinstance(m, int) or m > 0:
                        dve.wait_ge(sem["max_turned"], m)
                    v.tensor_copy(max_parts[:, :, :, 0].bitcast(F32R), neg_max[:, g]).then_inc(sem["max_hi"], 1)
                    dve.wait_ge(sem["max_hi"], m + 1)
                    v.tensor_tensor(max_parts[:, :, :, 1].bitcast(F32R), neg_max[:, g], max_parts[:, :, :, 0],
                                    ALU.subtract).then_inc(sem["max_lo"], 1)

                def evacuate_maxima(w, g):
                    m = 2 * w + g
                    dve.wait_ge(sem["max_turned"], m + 1)
                    if not isinstance(m, int) or m > 0:
                        dve.wait_ge(sem["max_written"], 16 * m)
                    v.tensor_copy(max_t[:], ps[0:8, 7, :]).then_inc(sem["max_evacuated"], 1)

                def row_max(n):
                    head, tile = n // 4, n % 4
                    lo, span = key_span(tile)
                    dve.wait_ge(sem["s_done"], 32 * (u + 1) + n + 1)
                    v.tensor_reduce(neg_max[:, head // 4, tile, head % 4:head % 4 + 1], ps[:, n % 3, 0:span * P], AX_X,
                                    ALU.max, negate=True).then_inc(sem["s_maxed"], 1)

                for n in range(8):
                    if has.project and n == 0:
                        part_lo(0)
                    if has.maxima_end and n == 1:
                        evacuate_maxima(u, 1)
                    if has.project and n == 2:
                        part_lo(1)
                    if has.project and c == 0 and n in (3, 4):
                        stage_values(n - 3)
                    if has.turn and n in (3, 4):
                        next_lo(2 * (i + 2) + n - 3, n - 3)
                    if has.maxima and n == 5:
                        evacuate_maxima(u + 1, 0)
                    if has.maxima:
                        row_max(4 * n)
                        row_max(4 * n + 1)
                    if n == 0 and has.probs_end or n == 4 and has.probs:
                        dve.wait_ge(sem["pv_done"], 8 * u + n)
                        if n == 4 and c == 0 and later(i, 1):
                            dve.wait_ge(sem["raw_turned"], 4 * i)
                        v.tensor_copy(raw[:, (2 * c + n // 4 - 1) % 4], ps[:, 6, :]).then_inc(sem["raw_done"], 1)
                    kind, t = OUTPUT_JOBS[c].get(n, none)
                    done = 4 * (i - 1) + t if kind and has.output else 0
                    if kind == "turn" and has.output:
                        view = ps[:, 3, :].rearrange("p (h d) -> p h d", d=32)
                        dve.wait_ge(sem["raw_turned"], done + 1)
                        v.reciprocal(recip[:], view[:, :, HD]).then_inc(sem["recip_done"], 1)
                        dve.wait_ge(sem["recip_done"], done + 1)
                        if t == 0 and later(i, 2):
                            dve.wait_ge(sem["ctx_turned"], done)
                        v.tensor_tensor(ctx_n[:, t], view[:, :, 0:HD],
                                        recip[:].unsqueeze(2).to_broadcast([P, HEADS, HD]), ALU.mult).then_inc(
                            sem["ctx_done"], 1)
                    if kind == "back" and has.output:
                        dve.wait_ge(sem["ctx_hi"], done + 1)
                        v.tensor_tensor(ctx_t[:, 1], ps[:, 3, 0:DC * P].rearrange("p (c t) -> p c t", c=DC),
                                        ctx_t[:, 0].bitcast(F32), ALU.subtract).then_inc(sem["ctx_lo"], 1)
                    if kind == "out" and has.output:
                        dve.wait_ge(sem["o_done"], done + 1)
                        dve.wait_ge(sem["residual_ready"], done + 1)
                        v.tensor_tensor(s_sum[:], ps[:, 3, 0:D], xn[:, 0, t], ALU.add).then_inc(sem["sum_done"], 1)
                        dve.wait_ge(sem["sum_done"], done + 1)
                        if t == 0:
                            dve.wait_ge(sem["y_gathered"], 64 * i)
                            if later(i, 2):
                                dve.wait_ge(sem["out_stored"], 16 * (i - 1))
                        v.scalar_tensor_tensor(out=gated[:, t], in0=y_in[:, t], scalar=0.5, in1=s_sum[:], op0=ALU.mult,
                                               op1=ALU.mult).then_inc(sem["gated_done"], 1)
                    if has.maxima:
                        row_max(4 * n + 2)
                        row_max(4 * n + 3)
                    if has.maxima and n == 3:
                        split_maxima(u + 1, 0)
                    if has.maxima and n == 7:
                        split_maxima(u + 1, 1)

            attention(dve, step)

        @block.tensor
        def _(pe):
            mm = nc.tensor.matmul
            tr = nc.tensor.transpose

            pe.wait_ge(sem["consts_pool"], 3)

            def turn(i, b, first=False):
                pe.wait_ge(sem["xn_done"], i + 1)
                if not first:
                    pe.wait_ge(sem["rows_lo"], i - 1)
                for c in range(DC):
                    for t in range(QT):
                        last = tr(ps[:, 2 * b + c, t * P:(t + 1) * P], xn[:, b, t, c * P:(c + 1) * P], ident[:])
                last.then_inc(sem["rows_turned"], 1)

            def gate_logits(i, b, first=False):
                pe.wait_ge(sem["rows_lo"], i + 1)
                if not first:
                    pe.wait_ge(sem["logits_kept"], i - 1)
                for t in range(QT):
                    last = product(ps[:, 4 + b, t * E:(t + 1) * E], lambda a, c: xt[b][:, a, c, t * P:(t + 1) * P],
                                   lambda a, c: w_gl[:, a, c, :], DC, mm)
                last.then_inc(sem["logits_done"], 1)

            turn(0, 0, first=True)
            turn(1, 1, first=True)
            pe.wait_ge(sem["weights_split"], 1)
            gate_logits(0, 0, first=True)
            turn(2, 0)
            gate_logits(1, 1, first=True)
            with pe.Fori(1, SEQS // 2 - 1) as pair:
                turn(2 * pair + 1, 1)
                gate_logits(2 * pair, 0)
                turn(2 * pair + 2, 0)
                gate_logits(2 * pair + 1, 1)
            turn(SEQS - 1, 1)
            gate_logits(SEQS - 2, 0)
            gate_logits(SEQS - 1, 1)

            pe.wait_ge(sem["onehot_ready"], 1)
            oh = one_hot_b[:].rearrange("p t e -> p (t e)")
            mm(ps[:, 0, :], upper_b[:], oh, start=True, stop=True)
            mm(ps[:, 1, :], ones_b[:], oh, start=True, stop=True).then_inc(sem["counts_done"], 1)

            pe.wait_ge(sem["positions_ready"], 1)
            pe.wait_ge(sem["weights_split"], 5)

            def front_turn(k, first=False):
                pe.wait_ge(sem["experts_in"], 16 * (k + 1))
                if not first:
                    pe.wait_ge(sem["experts_lo"], k)
                for c in range(DC):
                    for t in range(4):
                        last = tr(ps[:, c, t * P:(t + 1) * P], xs[:, t, c * P:(c + 1) * P], ident[:])
                last.then_inc(sem["experts_turned"], 1)

            def expert_at(k, t):
                return pe.value_load(expert_of[0:1, bass.ds(k * 4 + t, 1)], min_val=0, max_val=E - 1)

            def front_products(k, first=False):
                pe.wait_ge(sem["experts_lo"], k + 1)
                if not first:
                    pe.wait_ge(sem["hid_done"], k)
                for t in range(4):
                    e = expert_at(k, t)
                    last = product(ps[:, 2 + t // 2, (t % 2) * 2 * I:(t % 2 + 1) * 2 * I],
                                   lambda a, c: xt[1][:, a, c, t * P:(t + 1) * P],
                                   lambda a, c: w_gu[:, a, bass.ds(e * (DC * 2 * I) + c * 2 * I, 2 * I)], DC, mm)
                last.then_inc(sem["gu_done"], 1)

            def back_turn(k, first=False):
                pe.wait_ge(sem["hid_done"], k + 1)
                if not first:
                    pe.wait_ge(sem["hid_lo"], k)
                for t in range(4):
                    last = tr(ps[:, 4, t * P:(t + 1) * P], hid[:, t, :], ident[:])
                last.then_inc(sem["hid_turned"], 1)

            def back_products(k, first=False):
                pe.wait_ge(sem["hid_lo"], k + 1)
                if not first:
                    pe.wait_ge(sem["y_ready"], k)
                for t in range(4):
                    e = expert_at(k, t)
                    last = product(ps[:, 5 + t // 2, (t % 2) * D:(t % 2 + 1) * D],
                                   lambda a, c: hid_t[:, a, t * P:(t + 1) * P],
                                   lambda a, c: w_dn[:, a, bass.ds(e * D, D)], 1, mm)
                last.then_inc(sem["y_done"], 1)

            front_turn(0, first=True)
            front_products(0, first=True)
            front_turn(1)
            back_turn(0, first=True)
            front_products(1)
            front_turn(2)
            back_products(0, first=True)
            back_turn(1)
            with pe.Fori(2, FG - 1) as k:
                front_products(k)
                front_turn(k + 1)
                back_products(k - 1)
                back_turn(k)
            front_products(FG - 1)
            back_products(FG - 2)
            back_turn(FG - 1)
            back_products(FG - 1)

            def turn_next(job, ch):
                if ch == 0:
                    pe.wait_ge(sem["next_loaded"], 8 * (job + 2))
                for t in range(QT):
                    last = tr(ps[:, 7, t * P:(t + 1) * P], x_next[:, t, ch * P:(ch + 1) * P], ident[:])
                last.then_inc(sem["next_turned"], 1)

            turn_next(0, 0)
            pe.wait_ge(sem["next_lo"], 1)
            turn_next(1, 1)
            pe.wait_ge(sem["y_ready"], FG)

            def step(i, c, has):
                u = has.u

                def project(n):
                    off = n * D + c * P
                    product(ps[:, 7, :], lambda a, ch: w_qkv[:, a, ch, off:off + P],
                            lambda a, ch: xt[0][:, a, ch, :], DC, mm).then_inc(sem["proj_done"], 1)

                def project_values(n):
                    for h in range(2):
                        t = 2 * n + h
                        last = product(ps[:, 7, h * D:(h + 1) * D], lambda a, ch: xt[0][:, a, ch, t * P:(t + 1) * P],
                                       lambda a, ch: w_qkv[:, a, ch, 2 * D:3 * D], DC, mm)
                    last.then_inc(sem["v_done"], 1)

                def turn_maxima(w, g):
                    pe.wait_ge(sem["max_lo"], 2 * w + g + 1)
                    for t in range(QT):
                        last = tr(ps[0:8, 7, t * P:(t + 1) * P], max_parts[:, t].rearrange("p h l -> p (h l)"), ident[:])
                    last.then_inc(sem["max_turned"], 1)

                def spare_job(n):
                    if has.project and n == 0:
                        if has.maxima_end:
                            pe.wait_ge(sem["max_evacuated"], 2 * u + 1)
                        if c == 0:
                            pe.wait_ge(sem["next_lo"], 2 * (i + 2))
                        elif not has.maxima_end:
                            pe.wait_ge(sem["v_staged"], 2 * (i + 2))
                        project(0)
                    if has.maxima_end and n == 1:
                        if has.project:
                            pe.wait_ge(sem["parts_lo"], 2 * (u + 2) + 1)
                        else:
                            pe.wait_ge(sem["max_evacuated"], 2 * u + 1)
                        turn_maxima(u, 1)
                    if has.project and n == 2:
                        if has.maxima_end:
                            pe.wait_ge(sem["max_evacuated"], 2 * u + 2)
                        else:
                            pe.wait_ge(sem["parts_lo"], 2 * (u + 2) + 1)
                        project(1)
                    if has.project and c == 0 and n == 3:
                        pe.wait_ge(sem["parts_lo"], 2 * (u + 2) + 2)
                        project_values(0)
                    if has.project and c == 0 and n == 4:
                        pe.wait_ge(sem["v_staged"], 2 * (i + 1) + 1)
                        project_values(1)
                    if has.turn and n == 3:
                        pe.wait_ge(sem["parts_lo"], 2 * (u + 2) + 2)
                        turn_next(2 * (i + 2), 0)
                    if has.turn and n == 4:
                        pe.wait_ge(sem["next_lo"], 2 * (i + 2) + 1)
                        turn_next(2 * (i + 2) + 1, 1)
                    if has.maxima and n == 5:
                        if has.project and c == 0:
                            pe.wait_ge(sem["v_staged"], 2 * (i + 2))
                        elif has.turn:
                            pe.wait_ge(sem["next_lo"], 2 * (i + 3))
                        elif has.project:
                            pe.wait_ge(sem["parts_lo"], 2 * (u + 2) + 2)
                        else:
                            pe.wait_ge(sem["max_evacuated"], 2 * u + 2)
                        turn_maxima(u + 1, 0)

                def output_job(n):
                    kind, t = OUTPUT_JOBS[c].get(n, none)
                    if not kind or not has.output:
                        return
                    done = 4 * (i - 1) + t
                    if kind == "turn":
                        if t == 0:
                            pe.wait_ge(sem["raw_done"], 4 * i)
                            if later(i, 2):
                                pe.wait_ge(sem["sum_done"], done)
                        else:
                            pe.wait_ge(sem["ctx_done"], done)
                        for g in range(4):
                            last = tr(ps[:, 3, g * P:(g + 1) * P], raw[:, g, t * P:(t + 1) * P], ident[:])
                        last.then_inc(sem["raw_turned"], 1)
                    elif kind == "back":
                        if t == 0:
                            pe.wait_ge(sem["ctx_done"], 4 * i)
                        else:
                            pe.wait_ge(sem["sum_done"], done)
                        flat = ctx_n[:, t].rearrange("p h d -> p (h d)")
                        for ch in range(DC):
                            last = tr(ps[:, 3, ch * P:(ch + 1) * P], flat[:, ch * P:(ch + 1) * P], ident[:])
                        last.then_inc(sem["ctx_turned"], 1)
                    else:
                        pe.wait_ge(sem["ctx_lo"], done + 1)
                        product(ps[:, 3, 0:D], lambda a, ch: ctx_t[:, a, ch, :], lambda a, ch: w_o[:, a, ch, :], DC,
                                mm).then_inc(sem["o_done"], 1)

                def scores_t(n, h):
                    g, item = n // 4, n % 4
                    lo, span = key_span(item)
                    pair, j = 2 * g + h // 2, h % 2
                    e = 4 * n + h
                    if item == 0 and h == 0:
                        pe.wait_ge(sem[f"m_ready{g}"], 32 * (u + 1))
                    if not isinstance(i, int) or 32 * u + e >= 2:
                        pe.wait_ge(sem["ex_done"], 32 * u + e - 1)
                    r = slice(64 * j, 64 * j + 3 * HD + 2)
                    mm(ps[:, 4 + e % 2, 0:span * P], stack[c][r, 1, pair, item * P:(item + 1) * P],
                       stack[c][r, 0, pair, lo * P:(lo + span) * P], start=True, stop=True).then_inc(sem["st_done"], 1)

                def scores(n):
                    head, tile = n // 4, n % 4
                    pair, j = head // 2, head % 2
                    lo, span = key_span(tile)
                    if n % 16 == 0:
                        pe.wait_ge(sem[f"stack_ready{head // 4}"], 96 * (u + 2))
                    if not isinstance(i, int) or 32 * (u + 1) + n >= 3:
                        pe.wait_ge(sem["s_maxed"], 32 * (u + 1) + (n - 2 if n >= 2 else n - 1))
                    r = slice(64 * j, 64 * j + 3 * HD)
                    dst = ps[:, n % 3, 0:span * P]
                    mm(dst, stack[1 - c][r, 0, pair, tile * P:(tile + 1) * P],
                       stack[1 - c][r, 1, pair, lo * P:(lo + span) * P], start=True, stop=False, skip_group_check=True)
                    if span == 3:
                        edge = dst.rearrange("p (b k) -> p b k", k=P)[:, 0:3:2, :]
                        last = mm(edge, ident_b[:], mask_b[:], start=False, stop=True, skip_group_check=True)
                    elif tile == 0:
                        last = mm(dst[:, P:2 * P], ident_b[:], mask_b[:, 1], start=False, stop=True,
                                  skip_group_check=True)
                    else:
                        last = mm(dst[:, 0:P], ident_b[:], mask_b[:, 0], start=False, stop=True, skip_group_check=True)
                    last.then_inc(sem["s_done"], 1)

                def context(w, half, n):
                    g, item = n // 4, n % 4
                    lo, span = key_span(item)
                    pe.wait_ge(sem["masked"], 8 * w + n + 1)
                    if item == 0:
                        if not isinstance(i, int) or 2 * w + g > 0:
                            pe.wait_ge(sem["raw_done"], 2 * w + g)
                        if g == 0:
                            pe.wait_ge(sem["v_copied"], w + 1)
                    for h in range(4):
                        last = mm(ps[32 * h:32 * h + 32, 6, lo * P:(lo + span) * P], v_aug[half][:, item, 4 * g + h, :],
                                  probs[:, item, h, 0:span * P], start=(item == 0), stop=(item == QT - 1),
                                  tile_position=(0, 32 * h), skip_group_check=True)
                    last.then_inc(sem["pv_done"], 1)

                for n in range(8):
                    spare_job(n)
                    if has.probs:
                        scores_t(n, 0)
                        scores_t(n, 1)
                    if has.maxima:
                        scores(4 * n)
                        scores(4 * n + 1)
                    if n == 0 and has.probs_end:
                        context(u - 1, 1 - c, 7)
                    elif n > 0 and has.probs:
                        context(u, c, n - 1)
                    if has.probs:
                        scores_t(n, 2)
                    output_job(n)
                    if has.probs:
                        scores_t(n, 3)
                    if has.maxima:
                        scores(4 * n + 2)
                        scores(4 * n + 3)

            attention(pe, step)


def kernel(**inputs):
    import numpy as np
    import concourse.bacc as bacc
    from concourse.bass_utils import run_bass_kernel_spmd

    get = {k: np.asarray(v) for k, v in inputs.items()}

    def by_unit(a):
        qk, v = a[:512], a[512:]
        qk = qk.reshape((2, 2, 4, 2, 16) + a.shape[1:])
        qk = np.moveaxis(qk, 2, 4).reshape((512,) + a.shape[1:])
        return np.concatenate([qk, v])

    arrays = {
        "x": get["L0_attn_x"],
        "w_qkv_t": by_unit(get["L0_attn_w_in"]).T,
        "b_in": by_unit(get["L0_attn_b_in"]),
        "w_out_t": get["L0_attn_w_out"].T,
        "b_out": get["L0_attn_b_out"],
        "gate_t": get["L0_ffn_gate_w"].T,
        "w_gate_t": get["L0_ffn_w_gate"].transpose(0, 2, 1),
        "w_up_t": get["L0_ffn_w_up"].transpose(0, 2, 1),
        "w_down_t": get["L0_ffn_w_down"].transpose(0, 2, 1),
    }
    arrays = {k: np.ascontiguousarray(v) for k, v in arrays.items()}
    nc = bacc.Bacc("TRN2", target_bir_lowering=False, num_devices=1)
    args = [nc.dram_tensor(k, list(a.shape), mybir.dt.from_np(a.dtype), kind="ExternalInput").ap()
            for k, a in arrays.items()]
    shape = list(arrays["x"].shape)
    args.append(nc.dram_tensor("out", shape, F32, kind="ExternalOutput").ap())
    build(nc, *args)
    r = run_bass_kernel_spmd(nc, [arrays], core_ids=[0])
    return r.results[0]["out"]
```

```python
from contextlib import ExitStack

import concourse.bass as bass
from concourse import mybir

ALU = mybir.AluOpType
ACT = mybir.ActivationFunctionType
F32 = mybir.dt.float32
F32R = mybir.dt.float32r
BF16 = mybir.dt.bfloat16
I32 = mybir.dt.int32
U32 = mybir.dt.uint32
AX_X = mybir.AxisListType.X

P = 128
NEG = -1e30
EPS = 1e-5
PRODUCTS = ((0, 0), (0, 1), (1, 0))


def build(nc, x, w_qkv_t, b_in, w_out_t, b_out, gate_t, w_gate_t, w_up_t, w_down_t, out):
    SEQS, T, D = x.shape
    E, _, I = w_gate_t.shape
    HEADS = 16
    HD = D // HEADS
    N = SEQS * T
    TILES = N // P
    QT = T // P
    DC = D // P
    UNIT_HEADS = HEADS // 2
    PAIRS = UNIT_HEADS // 2
    SCALE = 1.0 / HD ** 0.5
    FT = TILES + E
    FG = FT // 4
    ROWS = FT * P
    assert (T, D, I, HD, QT, FT % 4) == (512, 256, 128, 16, 4, 0)

    x_g = x.rearrange("s (t p) d -> s p t d", p=P)
    out_g = out.rearrange("s (t p) d -> s p t d", p=P)
    xn_dram = nc.dram_tensor("xn_scratch", [SEQS, P, QT, D], F32).ap()
    sorted_dram = nc.dram_tensor("sorted_scratch", [ROWS, D], F32).ap()
    y_dram = nc.dram_tensor("expert_out_scratch", [ROWS, D], F32).ap()
    parts_dram = nc.dram_tensor("parts_scratch", [2, 4, P, T], F32).ap()

    with ExitStack() as ctx:
        def sb(name, shape, dt=F32):
            return ctx.enter_context(nc.sbuf_tensor(name, shape, dt))

        ident = sb("ident", [P, P])
        upper_b = sb("upper_b", [P, P], BF16)
        ones_b = sb("ones_b", [P, P], BF16)
        mask = sb("mask", [P, 3, P])
        ones64 = sb("ones64", [P, TILES])
        eps_t = sb("eps_t", [P, 1])
        b_qk = sb("b_qk", [P, 4])
        b_v = sb("b_v", [P, D])
        b_o = sb("b_o", [P, D])
        stage = sb("stage", [P, E * 3 * D])
        stage_qkv = stage[:, 0:DC * 3 * D].rearrange("p (c n) -> p c n", c=DC)
        stage_o = stage[:, DC * 3 * D:DC * 4 * D].rearrange("p (c n) -> p c n", c=DC)
        stage_gate = stage[:, DC * 4 * D:DC * (4 * D + E)].rearrange("p (c e) -> p c e", c=DC)
        w_qkv = sb("w_qkv", [P, 2, DC, 3 * D], F32R)
        w_o = sb("w_o", [P, 2, DC, D], F32R)
        w_gl = sb("w_gl", [P, 2, DC, E], F32R)
        w_gu = sb("w_gu", [P, 2, E * DC * 2 * I], F32R)
        w_dn = sb("w_dn", [P, 2, E * D], F32R)

        scores_and_values = sb("scores_and_values", [P, 2, TILES * E])
        logits, route_a = (scores_and_values[:, n].rearrange("p (t e) -> p t e", e=E) for n in range(2))
        one_hot = sb("one_hot", [P, TILES, E])
        one_hot_b = sb("one_hot_b", [P, TILES, E], BF16)
        top = sb("top", [P, TILES])
        weight = sb("weight", [P, TILES])
        rev = sb("rev", [P, E])
        iota_t = sb("iota_t", [P, TILES])
        iota_f = sb("iota_f", [P, FT])
        small = sb("small", [P, 16, E])
        position = sb("position", [P, TILES], I32)
        pad_position = sb("pad_position", [P, E], I32)
        experts_word = sb("experts_word", [P, FG], I32)
        pos4 = sb("pos4", [P, 2, 4], I32)

        x_in = sb("x_in", [P, 2, QT, D])
        bn = sb("bn", [P, 2, QT, 6])
        mv = sb("mv", [P, 2, QT, 2])
        sd = sb("sd", [P, 2, QT])
        rstd = sb("rstd", [P, 2, QT])
        xn = sb("xn", [P, 2, QT, D])
        cmp_f = x_in[:, 0].rearrange("p t d -> p (t d)")[:, 0:FT * E].rearrange("p (f e) -> p f e", e=E)
        by_e = x_in[:, 1, 0:2].rearrange("p t d -> p (t d)").rearrange("p (e t) -> p e t", e=E)
        cum = x_in[:, 1, 2:4].rearrange("p t d -> p (t d)").rearrange("p (e t) -> p e t", e=E)
        xt = [sb(f"xt{b}", [P, 2, DC, T], F32R) for b in range(2)]

        parts = sb("parts", [P, 4, T])
        q_stack = [sb(f"q_stack{c}", [P, UNIT_HEADS, T], F32R) for c in range(2)]
        k_stack = [w_gu[:, 0, c * PAIRS * T:(c + 1) * PAIRS * T].rearrange("p (a t) -> p a t", t=T) for c in range(2)]
        KEY_ROWS = slice(0, 6 * HD)
        MAX_ROWS = slice(6 * HD, 6 * HD + 2)
        v_stage = scores_and_values[:].rearrange("p a n -> p (a n)").rearrange("p (t h d) -> p t h d", t=QT, d=HD)
        x_next = sb("x_next", [P, QT, D])
        v_aug = [sb(f"v_aug{c}", [P, QT, UNIT_HEADS, 32]) for c in range(2)]
        neg_max = sb("neg_max", [P, 2, QT, 4])
        max_parts = sb("max_parts", [P, QT, 4, 2])
        max_t = sb("max_t", [8, T])
        probs = stage[:, 0:16 * 3 * P].rearrange("p (r h q) -> p r h q", r=4, h=4)
        raw = sb("raw", [P, 4, T])
        recip = sb("recip", [P, HEADS])
        ctx_n = sb("ctx_n", [P, QT, HEADS, HD])
        s_sum = sb("s_sum", [P, D])
        gated = x_in[:, 1]
        y_in = xn[:, 1]

        logits_t = parts
        zero_rows = ctx_n[:, 0].rearrange("p h d -> p (h d)")
        xs = [xn[:, b] for b in range(2)]
        y_out = [x_in[:, b] for b in range(2)]
        tanh_g, act_g, hid = (parts[:, n].rearrange("p (t i) -> p t i", t=4) for n in range(3))
        hid_t = sb("hid_t", [P, 2, 4 * P], F32R)
        ctx_t = hid_t[:, :, 0:DC * P].rearrange("p a (c t) -> p a c t", c=DC)
        tanh_y = raw[:, 0:2].rearrange("p a n -> p (a n)").rearrange("p (t d) -> p t d", t=4)

        ps = ctx.enter_context(nc.psum_tensor("ps", [P, 8, T], F32))

        names = """small_loaded weights_loaded weights_split consts_pool x_loaded0 x_loaded1 bn_done stats_done sd_done
            rstd_done xn_done xn_stored0 xn_stored1 rows_turned rows_hi rows_lo logits_done logits_copied logits_turned logits_kept routed route_link
            tanh_done onehot_ready counts_done positions_ready xn_again0 xn_again1 scaled padded pos_copied scattered0
            scattered1 experts_in0 experts_in1 experts_turned experts_hi experts_lo gu_done tanh_g_done act_g_done hid_done hid_turned
            hid_hi hid_lo y_done tanh_y_done y_ready y_stored0 y_stored1 next_loaded next_turned next_hi next_lo proj_done
            parts_hi parts_lo parts_written v_done v_staged v_copied stack_ready0 stack_ready1 s_done s_maxed max_hi
            max_lo max_turned max_evacuated m_ready0 m_ready1 st_done ex_done masked pv_done raw_done
            raw_turned recip_done ctx_done ctx_turned ctx_hi ctx_lo o_done sum_done gated_done residual_loaded
            residual_ready y_gathered out_ready out_stored ones_ready waits_passed""".split()
        sem = {name: ctx.enter_context(nc.semaphore(name)) for name in names}

        def carried(eng):
            eng.sem_inc(sem["waits_passed"], 1)

        def later(i, n):
            return not isinstance(i, int) or i >= n

        def product(dst, lhs, rhs, chunks, mm):
            todo = [(c, a, b) for c in range(chunks) for a, b in PRODUCTS]
            for n, (c, a, b) in enumerate(todo):
                last = mm(dst, lhs(a, c), rhs(b, c), start=(n == 0), stop=(n == len(todo) - 1))
            return last

        class Step:
            def __init__(self, i, c):
                inner = not isinstance(i, int)
                u = 2 * i + c
                self.u = u
                self.project = inner or i <= SEQS - 2
                self.load_next = c == 0 and (inner or i <= SEQS - 3)
                self.turn = c == 1 and (inner or i <= SEQS - 3)
                self.maxima = inner or -1 <= u <= 2 * SEQS - 2
                self.maxima_end = inner or 0 <= u <= 2 * SEQS - 1
                self.probs = inner or 0 <= u <= 2 * SEQS - 1
                self.probs_end = inner or 1 <= u <= 2 * SEQS
                self.output = inner or 1 <= i <= SEQS

        OUTPUT_JOBS = [
            {1: ("turn", 0), 2: ("turn", 1), 3: ("turn", 2), 4: ("turn", 3), 5: ("back", 0), 6: ("out", 0), 7: ("back", 1)},
            {0: ("out", 1), 1: ("back", 2), 2: ("out", 2), 3: ("back", 3), 4: ("out", 3)},
        ]
        none = (None, None)

        def attention(eng, step):
            for i in (-1, 0, 1):
                for c in range(2):
                    step(i, c, Step(i, c))
            with eng.Fori(2, SEQS - 2) as i:
                for c in range(2):
                    step(i, c, Step(i, c))
            for i in range(SEQS - 2, SEQS + 1):
                for c in range(2):
                    step(i, c, Step(i, c))

        def key_span(tile):
            lo, hi = max(0, tile - 1), min(QT - 1, tile + 1)
            return lo, hi - lo + 1

        block = ctx.enter_context(nc.Block())

        @block.sync
        def _(sp):
            sp.dma_start(stage_gate, gate_t.rearrange("(c p) e -> p c e", p=P)).then_inc(sem["weights_loaded"], 16)
            sp.dma_start(x_in[:, 0], x_g[0]).then_inc(sem["x_loaded0"], 16)
            sp.dma_start(stage_qkv, w_qkv_t.rearrange("(c p) n -> p c n", p=P)).then_inc(sem["weights_loaded"], 16)
            sp.dma_start(stage_o, w_out_t.rearrange("(c p) n -> p c n", p=P)).then_inc(sem["weights_loaded"], 16)
            for n in range(4):
                sp.dma_start(b_qk[:, n:n + 1], b_in[n * P:(n + 1) * P].rearrange("(p o) -> p o", o=1)).then_inc(
                    sem["small_loaded"], 16)
            sp.dma_start(b_v[:], b_in[2 * D:3 * D].partition_broadcast(P)).then_inc(sem["small_loaded"], 16)
            sp.dma_start(b_o[:], b_out.partition_broadcast(P)).then_inc(sem["small_loaded"], 16)

            def load_rows(i, b, first=False):
                if not first:
                    sp.wait_ge(sem["xn_done"], i - 1)
                    carried(sp)
                sp.dma_start(x_in[:, b], x_g[i]).then_inc(sem[f"x_loaded{b}"], 16)

            def store_rows(i, b):
                sp.wait_ge(sem["xn_done"], i + 1)
                carried(sp)
                sp.dma_start(xn_dram[i], xn[:, b]).then_inc(sem[f"xn_stored{b}"], 16)

            load_rows(1, 1, first=True)
            with sp.Fori(0, SEQS // 2 - 1) as pair:
                store_rows(2 * pair, 0)
                load_rows(2 * pair + 2, 0)
                store_rows(2 * pair + 1, 1)
                load_rows(2 * pair + 3, 1)
            store_rows(SEQS - 2, 0)
            store_rows(SEQS - 1, 1)

            sp.wait_ge(sem["weights_split"], 3)
            gu = stage[:, 0:E * DC * 2 * I].rearrange("p (e c g i) -> p g c e i", e=E, c=DC, g=2)
            for g, w in enumerate((w_gate_t, w_up_t)):
                for c in range(DC):
                    sp.dma_start(gu[:, g, c], w[:, c * P:(c + 1) * P, :].rearrange("e p i -> p e i")).then_inc(
                        sem["weights_loaded"], 16)
            dn = stage[:, E * DC * 2 * I:].rearrange("p (e n) -> p e n", e=E)
            sp.dma_start(dn, w_down_t.rearrange("e i n -> i e n")).then_inc(sem["weights_loaded"], 16)

            sp.wait_ge(sem["xn_stored0"], 8 * SEQS)
            sp.wait_ge(sem["xn_stored1"], 8 * SEQS)
            sp.wait_ge(sem["rows_turned"], SEQS)
            sp.dma_start(xn[:, 0], xn_dram[0]).then_inc(sem["xn_again0"], 16)
            sp.dma_start(xn[:, 1], xn_dram[1]).then_inc(sem["xn_again1"], 16)
            with sp.Fori(1, SEQS // 2) as pair:
                for b in range(2):
                    sp.wait_ge(sem["scaled"], 2 * pair + b - 1)
                    carried(sp)
                    sp.dma_start(xn[:, b], xn_dram[2 * pair + b]).then_inc(sem[f"xn_again{b}"], 16)

            sp.wait_ge(sem["scattered0"], 8 * TILES)
            sp.wait_ge(sem["scattered1"], 8 * TILES)
            sp.wait_ge(sem["padded"], 16 * E)
            xs_dram = sorted_dram.rearrange("(k t p) d -> k p t d", p=P, t=4)
            ys_dram = y_dram.rearrange("(k t p) d -> k p t d", p=P, t=4)

            def experts_load(k, b, first=False):
                if not first:
                    sp.wait_ge(sem["experts_turned"], k - 1)
                    carried(sp)
                sp.dma_start(xs[b], xs_dram[k]).then_inc(sem[f"experts_in{b}"], 16)

            def experts_store(k, b):
                sp.wait_ge(sem["y_ready"], k + 1)
                carried(sp)
                sp.dma_start(ys_dram[k], y_out[b]).then_inc(sem[f"y_stored{b}"], 16)

            experts_load(0, 0, first=True)
            experts_load(1, 1, first=True)
            for k in range(2, 5):
                experts_load(k, k % 2)
            with sp.Fori(0, FG // 2 - 3) as pair:
                for b in range(2):
                    experts_store(2 * pair + b, b)
                    experts_load(2 * pair + b + 5, 1 - b)
            experts_store(FG - 6, 0)
            experts_load(FG - 1, 1)
            for k in range(FG - 5, FG):
                experts_store(k, k % 2)
            sp.wait_ge(sem["y_stored0"], 8 * FG)
            sp.wait_ge(sem["y_stored1"], 8 * FG)

            def store_maxima(u, g, c):
                sp.wait_ge(sem["max_evacuated"], 2 * u + g + 1)
                carried(sp)
                for h in range(4):
                    stacked = PAIRS * (h % 2) + 2 * g + h // 2
                    sp.dma_start(q_stack[c][MAX_ROWS, stacked, :].bitcast(F32), max_t[2 * h:2 * h + 2, :]).then_inc(
                        sem[f"m_ready{g}"], 16)

            def load_stack(u, g, c):
                src = parts_dram[c].rearrange("b (j d p) t -> j d b (p t)", j=2, d=HD)[:, :, :, 2 * g * T:2 * (g + 1) * T]
                for j in range(2):
                    r, h = 3 * HD * j, PAIRS * j + 2 * g
                    q_dst = q_stack[c][:, h:h + 2, :].rearrange("r p t -> r (p t)").bitcast(F32)
                    k_dst = k_stack[c][:, 2 * g:2 * g + 2, :].rearrange("r p t -> r (p t)").bitcast(F32)
                    done = sem[f"stack_ready{g}"]
                    sp.dma_start(q_dst[r:r + 2 * HD], src[j][:, 0:2].rearrange("d b n -> b d n")).then_inc(done, 16)
                    sp.dma_start(q_dst[r + 2 * HD:r + 3 * HD], src[j][:, 1]).then_inc(done, 16)
                    sp.dma_start(k_dst[r:r + HD], src[j][:, 2]).then_inc(done, 16)
                    sp.dma_start(k_dst[r + HD:r + 3 * HD], src[j][:, 2:4].rearrange("d b n -> b d n")).then_inc(done, 16)

            sp.dma_start(x_next[:], xn_dram[0]).then_inc(sem["next_loaded"], 16)

            def step(i, c, has):
                u = has.u
                if has.load_next:
                    sp.wait_ge(sem["next_turned"], 2 * (i + 2))
                    carried(sp)
                    sp.dma_start(x_next[:], xn_dram[i + 2]).then_inc(sem["next_loaded"], 16)
                if has.maxima_end:
                    store_maxima(u, 1, c)
                if has.project:
                    sp.wait_ge(sem["parts_lo"], 2 * (u + 2) + 2)
                    carried(sp)
                    sp.dma_start(parts_dram[c].rearrange("b r t -> r b t"), parts[:]).then_inc(sem["parts_written"], 16)
                    sp.wait_ge(sem["parts_written"], 16 * (u + 3))
                    carried(sp)
                    if later(i, 0):
                        sp.wait_ge(sem["st_done"], 32 * u + 16)
                        carried(sp)
                        sp.wait_ge(sem["stack_ready0"], 128 * (u + 2))
                        carried(sp)
                    elif c == 1:
                        sp.wait_ge(sem["stack_ready0"], 128 * (u + 2))
                    load_stack(u + 2, 0, c)
                if has.maxima:
                    store_maxima(u + 1, 0, 1 - c)
                if has.project:
                    if later(i, 0):
                        sp.wait_ge(sem["st_done"], 32 * u + 32)
                        carried(sp)
                        sp.wait_ge(sem["stack_ready1"], 128 * (u + 2))
                        carried(sp)
                    elif c == 1:
                        sp.wait_ge(sem["stack_ready1"], 128 * (u + 2))
                    load_stack(u + 2, 1, c)
                if c == 1 and has.output:
                    sp.wait_ge(sem["out_ready"], 4 * i)
                    carried(sp)
                    sp.dma_start(out_g[i - 1], gated).then_inc(sem["out_stored"], 16)
                if c == 1 and has.probs:
                    sp.dma_start(xn[:, 0], xn_dram[i]).then_inc(sem["residual_loaded"], 16)
                    sp.dma_start(x_in[:, 0], x_g[i]).then_inc(sem["residual_loaded"], 16)

            attention(sp, step)
            sp.wait_ge(sem["out_stored"], 16 * SEQS)

        @block.gpsimd
        def _(pool):
            g = nc.gpsimd
            g.memset(ident[:], 0.0)
            g.memset(upper_b[:], 1.0)
            g.memset(mask[:], 0.0)
            g.memset(ones_b[:], 1.0)
            for c in range(2):
                g.memset(q_stack[c][:].bitcast(F32), 0.0)
            g.memset(eps_t[:], EPS).then_inc(sem["consts_pool"], 1)
            pool.wait_ge(sem["consts_pool"], 1)
            g.affine_select(out=ident[:], in_=ident[:], compare_op=ALU.not_equal, fill=1.0, base=0,
                            pattern=[[-1, P]], channel_multiplier=1)
            g.affine_select(out=upper_b[:], in_=upper_b[:], compare_op=ALU.is_gt, fill=0.0, base=0,
                            pattern=[[1, P]], channel_multiplier=-1)
            g.affine_select(out=mask[:, 0], in_=mask[:, 0], compare_op=ALU.is_ge, fill=NEG, base=0,
                            pattern=[[1, P]], channel_multiplier=-1)
            g.affine_select(out=mask[:, 2], in_=mask[:, 2], compare_op=ALU.is_ge, fill=NEG, base=0,
                            pattern=[[-1, P]], channel_multiplier=1)
            g.iota(rev[:], pattern=[[-1, E]], base=E, channel_multiplier=0, allow_small_or_imprecise_dtypes=True)
            g.iota(iota_t[:], pattern=[[P, TILES]], base=0, channel_multiplier=0, allow_small_or_imprecise_dtypes=True)
            g.iota(iota_f[:], pattern=[[1, FT]], base=0, channel_multiplier=0, allow_small_or_imprecise_dtypes=True)
            g.iota(small[:, 0], pattern=[[P, E]], base=0, channel_multiplier=1,
                   allow_small_or_imprecise_dtypes=True).then_inc(sem["consts_pool"], 1)

            def rows_at(ap):
                return bass.IndirectOffsetOnAxis(ap=ap, axis=0)

            pool.wait_ge(sem["positions_ready"], 1)
            for n in range(E):
                g.indirect_dma_start(out=sorted_dram[:, :], out_offset=rows_at(pad_position[:, n:n + 1]),
                                     in_=zero_rows, in_offset=None).then_inc(sem["padded"], 16)

            def scatter(i, b, first=False):
                if not first:
                    pool.wait_ge(sem[f"scattered{b}"], 32 * (i - b))
                    carried(pool)
                g.tensor_copy(pos4[:, b], position[:, bass.ds(i * 4, 4)]).then_inc(sem["pos_copied"], 1)
                pool.wait_ge(sem["pos_copied"], i + 1)
                carried(pool)
                pool.wait_ge(sem["scaled"], i + 1)
                carried(pool)
                for t in range(4):
                    g.indirect_dma_start(out=sorted_dram[:, :], out_offset=rows_at(pos4[:, b, t:t + 1]),
                                         in_=x_in[:, b, t, :], in_offset=None).then_inc(sem[f"scattered{b}"], 16)

            scatter(0, 0, first=True)
            scatter(1, 1, first=True)
            with pool.Fori(1, SEQS // 2) as pair:
                scatter(2 * pair, 0)
                scatter(2 * pair + 1, 1)

            pool.wait_ge(sem["gu_done"], FG)
            for c in range(2):
                last = g.memset(k_stack[c][P - 32:P].bitcast(F32), 1.0)
            last.then_inc(sem["ones_ready"], 1)
            pool.wait_ge(sem["small_loaded"], 96)
            pool.wait_ge(sem["y_stored0"], 8 * FG)
            pool.wait_ge(sem["y_stored1"], 8 * FG)

            def step(i, c, has):
                u = has.u
                for n in range(8):
                    if has.probs:
                        item = n % 4
                        lo, span = key_span(item)
                        pool.wait_ge(sem["ex_done"], 32 * u + 4 * n + 4)
                        carried(pool)
                        if item > 0:
                            v = probs[:, item, :, 0:P]
                            last = g.affine_select(out=v, in_=v, compare_op=ALU.is_ge, fill=0.0, base=0,
                                                   pattern=[[0, 4], [1, P]], channel_multiplier=-1)
                        if item < QT - 1:
                            v = probs[:, item, :, (span - 1) * P:span * P]
                            last = g.affine_select(out=v, in_=v, compare_op=ALU.is_ge, fill=0.0, base=0,
                                                   pattern=[[0, 4], [-1, P]], channel_multiplier=1)
                        last.then_inc(sem["masked"], 1)
                    if n == 1 and has.maxima:
                        if c == 1 or not later(i, 0):
                            pool.wait_ge(sem["v_staged"], 2 * (i + 2))
                            carried(pool)
                        if later(u if isinstance(i, int) else i, 1):
                            pool.wait_ge(sem["pv_done"], 8 * u)
                            carried(pool)
                        half = (1 - c) * UNIT_HEADS
                        g.tensor_copy(v_aug[1 - c][:, :, :, 0:HD],
                                      v_stage[:, :, half:half + UNIT_HEADS, :]).then_inc(sem["v_copied"], 1)
                    if c == 0 and n in (2, 3, 4, 5) and has.output:
                        if n == 2:
                            pool.wait_ge(sem["residual_loaded"], 32 * i)
                            carried(pool)
                        g.tensor_tensor(xn[:, 0, n - 2], xn[:, 0, n - 2], b_o[:], ALU.add).then_inc(
                            sem["residual_ready"], 1)
                    kind, t = OUTPUT_JOBS[c].get(n - 1, none) if n else ((OUTPUT_JOBS[0][7]) if c else none)
                    if kind == "out" and has.output:
                        pool.wait_ge(sem["gated_done"], 4 * (i - 1) + t + 1)
                        carried(pool)
                        g.tensor_tensor(gated[:, t], gated[:, t], x_in[:, 0, t], ALU.add).then_inc(sem["out_ready"], 1)
                    if c == 1 and n >= 6 and has.probs:
                        if n == 6:
                            if later(i, 1):
                                pool.wait_ge(sem["y_gathered"], 64 * i)
                                carried(pool)
                            g.tensor_copy(pos4[:, 0], position[:, bass.ds(i * 4, 4)]).then_inc(sem["pos_copied"], 1)
                            pool.wait_ge(sem["pos_copied"], SEQS + i + 1)
                            carried(pool)
                            if later(i, 1):
                                pool.wait_ge(sem["gated_done"], 4 * i)
                                carried(pool)
                        for t in (0, 1) if n == 6 else (2, 3):
                            g.indirect_dma_start(out=y_in[:, t, :], out_offset=None, in_=y_dram[:, :],
                                                 in_offset=rows_at(pos4[:, 0, t:t + 1])).then_inc(sem["y_gathered"], 16)

            attention(pool, step)

        @block.scalar
        def _(act):
            a = nc.scalar

            def deviation(i, b):
                act.wait_ge(sem["stats_done"], i + 1)
                a.activation(sd[:, b, :], mv[:, b, :, 1], ACT.Sqrt, bias=eps_t[:]).then_inc(sem["sd_done"], 1)

            def rows_hi(i, b, first=False):
                act.wait_ge(sem["rows_turned"], i + 1)
                if not first:
                    act.wait_ge(sem["logits_done"], i - 1)
                a.activation(xt[b][:, 0], ps[:, 2 * b:2 * b + 2, :], ACT.Copy).then_inc(sem["rows_hi"], 1)

            def copy_logits(i, b, first=False):
                act.wait_ge(sem["logits_done"], i + 1)
                if not first:
                    act.wait_ge(sem["logits_turned"], i - 1)
                a.activation(logits_t[0:E, b], ps[0:E, 4 + b, :], ACT.Copy).then_inc(sem["logits_copied"], 1)

            act.wait_ge(sem["consts_pool"], 1)
            deviation(0, 0)
            deviation(1, 1)
            rows_hi(0, 0, first=True)
            deviation(2, 0)
            copy_logits(0, 0, first=True)
            rows_hi(1, 1, first=True)
            deviation(3, 1)
            copy_logits(1, 1, first=True)
            rows_hi(2, 0)
            with act.Fori(2, SEQS // 2) as pair:
                deviation(2 * pair, 0)
                copy_logits(2 * pair - 2, 0)
                rows_hi(2 * pair - 1, 1)
                deviation(2 * pair + 1, 1)
                copy_logits(2 * pair - 1, 1)
                rows_hi(2 * pair, 0)
            copy_logits(SEQS - 2, 0)
            rows_hi(SEQS - 1, 1)
            copy_logits(SEQS - 1, 1)

            act.wait_ge(sem["routed"], 1)
            a.activation(weight[:], top[:], ACT.Tanh, scale=0.5).then_inc(sem["tanh_done"], 1)

            def two_banks(b):
                return ps[:, b:b + 2, :].rearrange("p b (t n) -> p (b t) n", t=2)

            def experts_hi(k, b, first=False):
                act.wait_ge(sem["experts_turned"], k + 1)
                if not first:
                    act.wait_ge(sem["gu_done"], k - 1)
                a.activation(xt[b][:, 0], ps[:, 0:2, :], ACT.Copy).then_inc(sem["experts_hi"], 1)

            def gate_tanh(k, first=False):
                act.wait_ge(sem["gu_done"], k + 1)
                if not first:
                    act.wait_ge(sem["hid_done"], k)
                a.activation(tanh_g, two_banks(2)[:, :, 0:I], ACT.Tanh, scale=0.5).then_inc(sem["tanh_g_done"], 1)

            def hid_hi(k, first=False):
                act.wait_ge(sem["hid_turned"], k + 1)
                if not first:
                    act.wait_ge(sem["y_done"], k)
                a.activation(hid_t[:, 0], ps[:, 4, :], ACT.Copy).then_inc(sem["hid_hi"], 1)

            def result_tanh(k, first=False):
                act.wait_ge(sem["y_done"], k + 1)
                if not first:
                    act.wait_ge(sem["y_ready"], k)
                a.activation(tanh_y, two_banks(5), ACT.Tanh, scale=0.5).then_inc(sem["tanh_y_done"], 1)

            experts_hi(0, 0, first=True)
            experts_hi(1, 1, first=True)
            gate_tanh(0, first=True)
            experts_hi(2, 0)
            hid_hi(0, first=True)
            gate_tanh(1)
            result_tanh(0, first=True)
            experts_hi(3, 1)
            hid_hi(1)
            with act.Fori(1, FG // 2 - 1) as pair:
                for b in range(2):
                    k = 2 * pair + b
                    gate_tanh(k)
                    result_tanh(k - 1)
                    experts_hi(k + 2, b)
                    hid_hi(k)
            for k in (FG - 2, FG - 1):
                gate_tanh(k)
                result_tanh(k - 1)
                hid_hi(k)
            result_tanh(FG - 1)

            act.wait_ge(sem["small_loaded"], 96)

            def next_hi(job, ch):
                act.wait_ge(sem["next_turned"], job + 1)
                a.activation(xt[0][:, 0, ch], ps[:, 7, :], ACT.Copy).then_inc(sem["next_hi"], 1)

            next_hi(0, 0)
            next_hi(1, 1)

            def step(i, c, has):
                u = has.u

                def part_hi(n):
                    act.wait_ge(sem["proj_done"], 2 * (u + 2) + n + 1)
                    if n == 0 and (not isinstance(i, int) or u > -2):
                        act.wait_ge(sem["parts_written"], 16 * (u + 2))
                    col = 2 * n + c
                    a.activation(parts[:, 1 + n].bitcast(F32R), ps[:, 7, :], ACT.Identity,
                                 bias=b_qk[:, col:col + 1]).then_inc(sem["parts_hi"], 1)

                def exp(n, h):
                    lo, span = key_span(n % 4)
                    e = 4 * n + h
                    act.wait_ge(sem["st_done"], 32 * u + e + 1)
                    if h == 0 and (not isinstance(i, int) or 8 * u + n - 3 > 0):
                        act.wait_ge(sem["pv_done"], 8 * u + n - 3)
                    a.activation(probs[:, n % 4, h, 0:span * P], ps[:, 4 + e % 2, 0:span * P], ACT.Exp,
                                 scale=SCALE).then_inc(sem["ex_done"], 1)

                for n in range(8):
                    if has.probs:
                        exp(n, 0)
                        exp(n, 1)
                    if has.project and n == 0:
                        part_hi(0)
                    if has.project and n == 2:
                        part_hi(1)
                    if has.turn and n in (3, 5):
                        next_hi(2 * (i + 2) + n // 5, n // 5)
                    if has.probs:
                        exp(n, 2)
                        exp(n, 3)
                    if n == 0 and has.probs_end or n == 4 and has.probs:
                        act.wait_ge(sem["pv_done"], 8 * u + n)
                        if n == 4 and c == 0 and later(i, 1):
                            act.wait_ge(sem["raw_turned"], 4 * i)
                        a.activation(raw[:, (2 * c + n // 4 - 1) % 4], ps[:, 6, :], ACT.Copy).then_inc(
                            sem["raw_done"], 1)
                    kind, t = OUTPUT_JOBS[c].get(n, none)
                    if kind == "back" and has.output:
                        act.wait_ge(sem["ctx_turned"], 4 * (i - 1) + t + 1)
                        a.activation(ctx_t[:, 0], ps[:, 3, 0:DC * P].rearrange("p (c t) -> p c t", c=DC),
                                     ACT.Copy).then_inc(sem["ctx_hi"], 1)

            attention(act, step)

        @block.vector
        def _(dve):
            v = nc.vector
            links = [0]

            def link(ins):
                links[0] += 1
                ins.then_inc(sem["route_link"], 1)
                dve.wait_ge(sem["route_link"], links[0])

            v.memset(ones64[:], 1.0)
            v.memset(zero_rows, 0.0)
            for c in range(2):
                v.memset(v_aug[c][:], 1.0)

            def split(dst, src):
                link(v.tensor_copy(dst(0), src))
                return v.tensor_tensor(dst(1), src, dst(0).bitcast(F32), ALU.subtract)

            dve.wait_ge(sem["weights_loaded"], 48)
            split(lambda h: w_gl[:, h], stage_gate).then_inc(sem["weights_split"], 1)
            split(lambda h: w_qkv[:, h], stage_qkv).then_inc(sem["weights_split"], 1)
            split(lambda h: w_o[:, h], stage_o).then_inc(sem["weights_split"], 1)

            def statistics(i, b):
                dve.wait_ge(sem[f"x_loaded{b}"], 8 * (i - b) + 16)
                for t in range(QT):
                    last = v.bn_stats(bn[:, b, t], x_in[:, b, t])
                last.then_inc(sem["bn_done"], 1)
                dve.wait_ge(sem["bn_done"], i + 1)
                if not isinstance(i, int):
                    carried(dve)
                for t in range(QT):
                    last = v.bn_aggr(mv[:, b, t], bn[:, b, t])
                last.then_inc(sem["stats_done"], 1)

            def normalise(i, b, first=False):
                dve.wait_ge(sem["sd_done"], i + 1)
                v.reciprocal(rstd[:, b], sd[:, b]).then_inc(sem["rstd_done"], 1)
                dve.wait_ge(sem["rstd_done"], i + 1)
                if not first:
                    dve.wait_ge(sem[f"xn_stored{b}"], 8 * (i - b))
                    dve.wait_ge(sem["rows_turned"], i - 1)
                for t in range(QT):
                    last = v.tensor_scalar(xn[:, b, t], x_in[:, b, t], mv[:, b, t, 0:1], rstd[:, b, t:t + 1],
                                           ALU.subtract, ALU.mult)
                last.then_inc(sem["xn_done"], 1)

            def rows_lo(i, b):
                dve.wait_ge(sem["rows_hi"], i + 1)
                v.tensor_tensor(xt[b][:, 1], ps[:, 2 * b:2 * b + 2, :], xt[b][:, 0].bitcast(F32),
                                ALU.subtract).then_inc(sem["rows_lo"], 1)

            def keep_logits(i, b):
                dve.wait_ge(sem["logits_turned"], i + 1)
                v.tensor_copy(logits[:, bass.ds(i * QT, QT), :],
                              ps[:, 6 + b, 0:QT * E].rearrange("p (t e) -> p t e", t=QT)).then_inc(sem["logits_kept"], 1)

            statistics(0, 0)
            normalise(0, 0, first=True)
            statistics(1, 1)
            normalise(1, 1, first=True)
            statistics(2, 0)
            rows_lo(0, 0)
            normalise(2, 0)
            statistics(3, 1)
            rows_lo(1, 1)
            normalise(3, 1)
            keep_logits(0, 0)
            with dve.Fori(2, SEQS // 2) as pair:
                statistics(2 * pair, 0)
                rows_lo(2 * pair - 2, 0)
                normalise(2 * pair, 0)
                keep_logits(2 * pair - 3, 1)
                statistics(2 * pair + 1, 1)
                rows_lo(2 * pair - 1, 1)
                normalise(2 * pair + 1, 1)
                keep_logits(2 * pair - 2, 0)
            rows_lo(SEQS - 2, 0)
            keep_logits(SEQS - 3, 1)
            rows_lo(SEQS - 1, 1)
            keep_logits(SEQS - 2, 0)
            keep_logits(SEQS - 1, 1)
            dve.wait_ge(sem["logits_kept"], SEQS)

            tb = [P, TILES, E]
            dve.wait_ge(sem["consts_pool"], 2)
            link(v.reduce_max(top[:], logits, AX_X))
            v.tensor_tensor(route_a, logits, top[:].unsqueeze(2).to_broadcast(tb),
                            ALU.is_equal).then_inc(sem["routed"], 1)
            dve.wait_ge(sem["routed"], 1)
            link(v.tensor_tensor(route_a, route_a, rev[:].unsqueeze(1).to_broadcast(tb), ALU.mult))
            link(v.reduce_max(cum[:, 0, :], route_a, AX_X))
            link(v.tensor_tensor(one_hot[:], rev[:].unsqueeze(1).to_broadcast(tb),
                                 cum[:, 0, :].unsqueeze(2).to_broadcast(tb), ALU.is_equal))
            v.tensor_copy(one_hot_b[:], one_hot[:]).then_inc(sem["onehot_ready"], 1)
            dve.wait_ge(sem["tanh_done"], 1)
            link(v.tensor_scalar(weight[:], weight[:], 0.5, 0.5, ALU.mult, ALU.add))
            dve.wait_ge(sem["counts_done"], 1)
            before = ps[:, 0, :].rearrange("p (t e) -> p t e", e=E)
            total = ps[:, 1, :].rearrange("p (t e) -> p t e", e=E)
            for e in range(E):
                last = v.tensor_tensor_scan(cum[:, e, :], ones64[:], total[:, :, e], 0.0, ALU.mult, ALU.add)
            link(last)
            count, tiles, ends, base = (small[:, n] for n in (4, 5, 6, 7))
            link(v.tensor_copy(count, cum[:, :, TILES - 1]))
            link(v.tensor_tensor(by_e, count.unsqueeze(2).to_broadcast([P, E, TILES]),
                                 iota_t[:].unsqueeze(1).to_broadcast([P, E, TILES]), ALU.is_gt))
            link(v.reduce_sum(tiles, by_e, AX_X))
            link(v.tensor_tensor_scan(ends, ones64[:, 0:E], tiles, 0.0, ALU.mult, ALU.add))
            link(v.tensor_tensor(base, ends, tiles, ALU.subtract))
            link(v.tensor_scalar(base, base, float(P), None, ALU.mult))
            link(v.tensor_tensor(route_a, cum.rearrange("p e t -> p t e"), total, ALU.subtract))
            link(v.tensor_tensor(route_a, route_a, before, ALU.add))
            link(v.tensor_tensor(route_a, route_a, base.unsqueeze(1).to_broadcast(tb), ALU.add))
            link(v.tensor_tensor(route_a, route_a, one_hot[:], ALU.mult))
            link(v.reduce_sum(top[:], route_a, AX_X))
            link(v.tensor_copy(position[:], top[:]))
            tokens, pads_before = small[:, 9], small[:, 10]
            link(v.tensor_tensor_scan(tokens, ones64[:, 0:E], count, 0.0, ALU.mult, ALU.add))
            link(v.tensor_tensor(tokens, tokens, count, ALU.subtract))
            link(v.tensor_tensor(pads_before, base, tokens, ALU.subtract))
            eb = [P, E, E]
            begun, place = by_e[:, :, 0:E], small[:, 11]
            link(v.tensor_tensor(begun, small[:, 0].unsqueeze(2).to_broadcast(eb),
                                 pads_before.unsqueeze(1).to_broadcast(eb), ALU.is_ge))
            link(v.tensor_tensor(begun, begun, count.unsqueeze(1).to_broadcast(eb), ALU.mult))
            link(v.reduce_sum(place, begun, AX_X))
            link(v.tensor_tensor(place, place, small[:, 0], ALU.add))
            link(v.tensor_copy(pad_position[:], place))
            link(v.tensor_tensor(cmp_f, iota_f[:].unsqueeze(2).to_broadcast([P, FT, E]),
                                 ends.unsqueeze(1).to_broadcast([P, FT, E]), ALU.is_ge))
            link(v.reduce_sum(iota_f[:], cmp_f, AX_X))
            link(v.tensor_scalar(iota_f[:], iota_f[:], float(E - 1), None, ALU.min))
            digit = iota_f[:].rearrange("p (k t) -> p t k", t=4)
            word = digit[:, 3]
            for t in (2, 1, 0):
                link(v.scalar_tensor_tensor(out=word, in0=word, scalar=float(E), in1=digit[:, t], op0=ALU.mult,
                                            op1=ALU.add))
            v.tensor_copy(experts_word[:], word).then_inc(sem["positions_ready"], 1)

            def scale(i, b, first=False):
                dve.wait_ge(sem[f"xn_again{b}"], 8 * (i - b) + 16)
                if not first:
                    dve.wait_ge(sem[f"scattered{b}"], 32 * (i - b))
                w = weight[:, bass.ds(i * QT, QT)].unsqueeze(2).to_broadcast([P, QT, D])
                v.tensor_tensor(x_in[:, b], xn[:, b], w, ALU.mult).then_inc(sem["scaled"], 1)

            scale(0, 0, first=True)
            scale(1, 1, first=True)
            dve.wait_ge(sem["weights_loaded"], 16 * 8)
            split(lambda h: w_gu[:, h], stage[:, 0:E * DC * 2 * I]).then_inc(sem["weights_split"], 1)
            split(lambda h: w_dn[:, h], stage[:, E * DC * 2 * I:]).then_inc(sem["weights_split"], 1)
            with dve.Fori(1, SEQS // 2) as pair:
                scale(2 * pair, 0)
                scale(2 * pair + 1, 1)

            def two_banks(b):
                return ps[:, b:b + 2, :].rearrange("p b (t n) -> p (b t) n", t=2)

            def experts_lo(k, b):
                dve.wait_ge(sem["experts_hi"], k + 1)
                v.tensor_tensor(xt[b][:, 1], ps[:, 0:2, :], xt[b][:, 0].bitcast(F32), ALU.subtract).then_inc(
                    sem["experts_lo"], 1)

            def hid_lo(k):
                dve.wait_ge(sem["hid_hi"], k + 1)
                v.tensor_tensor(hid_t[:, 1], ps[:, 4, :], hid_t[:, 0].bitcast(F32), ALU.subtract).then_inc(sem["hid_lo"], 1)

            def gate(k, first=False):
                dve.wait_ge(sem["tanh_g_done"], k + 1)
                v.scalar_tensor_tensor(out=act_g, in0=tanh_g, scalar=1.0, in1=two_banks(2)[:, :, 0:I], op0=ALU.add,
                                       op1=ALU.mult).then_inc(sem["act_g_done"], 1)
                dve.wait_ge(sem["act_g_done"], k + 1)
                if not first:
                    dve.wait_ge(sem["hid_turned"], k)
                v.scalar_tensor_tensor(out=hid, in0=act_g, scalar=0.5, in1=two_banks(2)[:, :, I:2 * I], op0=ALU.mult,
                                       op1=ALU.mult).then_inc(sem["hid_done"], 1)

            def result(k, b, first=False):
                dve.wait_ge(sem["tanh_y_done"], k + 1)
                if not first:
                    dve.wait_ge(sem[f"y_stored{b}"], 8 * (k - b))
                v.scalar_tensor_tensor(out=y_out[b], in0=tanh_y, scalar=1.0, in1=two_banks(5), op0=ALU.add,
                                       op1=ALU.mult).then_inc(sem["y_ready"], 1)

            experts_lo(0, 0)
            experts_lo(1, 1)
            gate(0, first=True)
            experts_lo(2, 0)
            hid_lo(0)
            gate(1)
            result(0, 0, first=True)
            experts_lo(3, 1)
            hid_lo(1)
            with dve.Fori(1, FG // 2 - 1) as pair:
                for b in range(2):
                    k = 2 * pair + b
                    gate(k)
                    result(k - 1, 1 - b)
                    experts_lo(k + 2, b)
                    hid_lo(k)
            gate(FG - 2)
            result(FG - 3, 1)
            hid_lo(FG - 2)
            gate(FG - 1)
            result(FG - 2, 0)
            hid_lo(FG - 1)
            result(FG - 1, 1)

            def next_lo(job, ch):
                dve.wait_ge(sem["next_hi"], job + 1)
                v.tensor_tensor(xt[0][:, 1, ch], ps[:, 7, :], xt[0][:, 0, ch].bitcast(F32), ALU.subtract).then_inc(
                    sem["next_lo"], 1)

            next_lo(0, 0)
            next_lo(1, 1)

            def step(i, c, has):
                u = has.u

                def part_lo(n):
                    hi, lo = (1, 0) if n == 0 else (2, 3)
                    dve.wait_ge(sem["parts_hi"], 2 * (u + 2) + n + 1)
                    v.scalar_tensor_tensor(out=parts[:, lo].bitcast(F32R), in0=ps[:, 7, :],
                                           scalar=b_qk[:, 2 * n + c:2 * n + c + 1], in1=parts[:, hi], op0=ALU.add,
                                           op1=ALU.subtract).then_inc(sem["parts_lo"], 1)

                def stage_values(n):
                    dve.wait_ge(sem["v_done"], 2 * (i + 1) + n + 1)
                    if n == 0 and later(i, 0):
                        dve.wait_ge(sem["v_copied"], 2 * (i + 1))
                    bias = b_v[:].rearrange("p (h d) -> p h d", d=HD).unsqueeze(1).to_broadcast([P, 2, HEADS, HD])
                    v.tensor_tensor(v_stage[:, 2 * n:2 * n + 2], ps[:, 7, :].rearrange("p (t h d) -> p t h d", t=2, d=HD),
                                    bias, ALU.add).then_inc(sem["v_staged"], 1)

                def split_maxima(w, g):
                    m = 2 * w + g
                    dve.wait_ge(sem["s_maxed"], 32 * w + 16 * g + 16)
                    if not isinstance(m, int) or m > 0:
                        dve.wait_ge(sem["max_turned"], m)
                    v.tensor_copy(max_parts[:, :, :, 0].bitcast(F32R), neg_max[:, g]).then_inc(sem["max_hi"], 1)
                    dve.wait_ge(sem["max_hi"], m + 1)
                    v.tensor_tensor(max_parts[:, :, :, 1].bitcast(F32R), neg_max[:, g], max_parts[:, :, :, 0],
                                    ALU.subtract).then_inc(sem["max_lo"], 1)

                def evacuate_maxima(w, g):
                    m = 2 * w + g
                    dve.wait_ge(sem["max_turned"], m + 1)
                    if not isinstance(m, int) or m > 0:
                        dve.wait_ge(sem[f"m_ready{1 - g}"], 64 * (w + g))
                    v.tensor_copy(max_t[:], ps[0:8, 7, :]).then_inc(sem["max_evacuated"], 1)

                def row_max(n):
                    head, tile = n // 4, n % 4
                    lo, span = key_span(tile)
                    dve.wait_ge(sem["s_done"], 32 * (u + 1) + n + 1)
                    carried(dve)
                    first = 1 if tile == 0 else 0
                    v.tensor_tensor_reduce(out=ps[:, n % 3, 0:span * P], in0=ps[:, n % 3, 0:span * P],
                                           in1=mask[:, first:first + span].rearrange("p b k -> p (b k)"),
                                           scale=-1.0, scalar=-NEG, op0=ALU.add, op1=ALU.min,
                                           accum_out=neg_max[:, head // 4, tile, head % 4:head % 4 + 1]).then_inc(
                        sem["s_maxed"], 1)

                for n in range(8):
                    if has.maxima:
                        row_max(4 * n)
                        row_max(4 * n + 1)
                        row_max(4 * n + 2)
                    if has.project and n == 0:
                        part_lo(0)
                    if has.maxima_end and n == 1:
                        evacuate_maxima(u, 1)
                    if has.project and n == 2:
                        part_lo(1)
                    if has.project and c == 0 and n in (3, 5):
                        stage_values(n // 5)
                    if has.turn and n in (3, 5):
                        next_lo(2 * (i + 2) + n // 5, n // 5)
                    if has.maxima and n == 4:
                        evacuate_maxima(u + 1, 0)
                    if has.maxima:
                        row_max(4 * n + 3)
                    if has.maxima and n == 3:
                        split_maxima(u + 1, 0)
                    if has.maxima and n == 7:
                        split_maxima(u + 1, 1)
                    kind, t = OUTPUT_JOBS[c].get(n, none)
                    done = 4 * (i - 1) + t if kind and has.output else 0
                    if kind == "turn" and has.output:
                        view = ps[:, 3, :].rearrange("p (h d) -> p h d", d=32)
                        dve.wait_ge(sem["raw_turned"], done + 1)
                        v.reciprocal(recip[:], view[:, :, HD]).then_inc(sem["recip_done"], 1)
                        dve.wait_ge(sem["recip_done"], done + 1)
                        if t == 0 and later(i, 2):
                            dve.wait_ge(sem["ctx_turned"], done)
                        v.tensor_tensor(ctx_n[:, t], view[:, :, 0:HD],
                                        recip[:].unsqueeze(2).to_broadcast([P, HEADS, HD]), ALU.mult).then_inc(
                            sem["ctx_done"], 1)
                    if kind == "back" and has.output:
                        dve.wait_ge(sem["ctx_hi"], done + 1)
                        v.tensor_tensor(ctx_t[:, 1], ps[:, 3, 0:DC * P].rearrange("p (c t) -> p c t", c=DC),
                                        ctx_t[:, 0].bitcast(F32), ALU.subtract).then_inc(sem["ctx_lo"], 1)
                    if kind == "out" and has.output:
                        dve.wait_ge(sem["o_done"], done + 1)
                        dve.wait_ge(sem["residual_ready"], done + 1)
                        v.tensor_tensor(s_sum[:], ps[:, 3, 0:D], xn[:, 0, t], ALU.add).then_inc(sem["sum_done"], 1)
                        dve.wait_ge(sem["sum_done"], done + 1)
                        if t == 0:
                            dve.wait_ge(sem["y_gathered"], 64 * i)
                            if later(i, 2):
                                dve.wait_ge(sem["out_stored"], 16 * (i - 1))
                        v.scalar_tensor_tensor(out=gated[:, t], in0=y_in[:, t], scalar=0.5, in1=s_sum[:], op0=ALU.mult,
                                               op1=ALU.mult).then_inc(sem["gated_done"], 1)

            attention(dve, step)

        @block.tensor
        def _(pe):
            mm = nc.tensor.matmul
            tr = nc.tensor.transpose

            pe.wait_ge(sem["consts_pool"], 2)

            def turn(i, b, first=False):
                pe.wait_ge(sem["xn_done"], i + 1)
                if not first:
                    pe.wait_ge(sem["rows_lo"], i - 1)
                for c in range(DC):
                    for t in range(QT):
                        last = tr(ps[:, 2 * b + c, t * P:(t + 1) * P], xn[:, b, t, c * P:(c + 1) * P], ident[:])
                last.then_inc(sem["rows_turned"], 1)

            def gate_logits(i, b, first=False):
                pe.wait_ge(sem["rows_lo"], i + 1)
                if not first:
                    pe.wait_ge(sem["logits_copied"], i - 1)
                product(ps[0:E, 4 + b, :], lambda a, c: w_gl[:, a, c, :], lambda a, c: xt[b][:, a, c, :], DC, mm).then_inc(
                    sem["logits_done"], 1)

            def logits_back(i, b, first=False):
                pe.wait_ge(sem["logits_copied"], i + 1)
                carried(pe)
                if not first:
                    pe.wait_ge(sem["logits_kept"], i - 1)
                    carried(pe)
                for t in range(QT):
                    last = tr(ps[:, 6 + b, t * E:(t + 1) * E], logits_t[0:E, b, t * P:(t + 1) * P], ident[0:E, 0:E])
                last.then_inc(sem["logits_turned"], 1)

            turn(0, 0, first=True)
            turn(1, 1, first=True)
            pe.wait_ge(sem["weights_split"], 1)
            gate_logits(0, 0, first=True)
            turn(2, 0)
            logits_back(0, 0, first=True)
            gate_logits(1, 1, first=True)
            turn(3, 1)
            logits_back(1, 1, first=True)
            gate_logits(2, 0)
            with pe.Fori(2, SEQS // 2) as pair:
                turn(2 * pair, 0)
                logits_back(2 * pair - 2, 0)
                gate_logits(2 * pair - 1, 1)
                turn(2 * pair + 1, 1)
                logits_back(2 * pair - 1, 1)
                gate_logits(2 * pair, 0)
            logits_back(SEQS - 2, 0)
            gate_logits(SEQS - 1, 1)
            logits_back(SEQS - 1, 1)

            pe.wait_ge(sem["onehot_ready"], 1)
            oh = one_hot_b[:].rearrange("p t e -> p (t e)")
            mm(ps[:, 0, :], upper_b[:], oh, start=True, stop=True)
            mm(ps[:, 1, :], ones_b[:], oh, start=True, stop=True).then_inc(sem["counts_done"], 1)

            pe.wait_ge(sem["positions_ready"], 1)
            pe.wait_ge(sem["weights_split"], 5)

            def front_turn(k, b, first=False):
                pe.wait_ge(sem[f"experts_in{b}"], 8 * (k - b) + 16)
                if not first:
                    pe.wait_ge(sem["experts_lo"], k)
                for c in range(DC):
                    for t in range(4):
                        last = tr(ps[:, c, t * P:(t + 1) * P], xs[b][:, t, c * P:(c + 1) * P], ident[:])
                last.then_inc(sem["experts_turned"], 1)

            def experts_of(k):
                word = pe.value_load(experts_word[0:1, bass.ds(k, 1)], min_val=0, max_val=E ** 4 - 1)
                return [word // E ** t % E for t in range(4)]

            def front_products(k, b, first=False):
                e = experts_of(k)
                pe.wait_ge(sem["experts_lo"], k + 1)
                if not first:
                    pe.wait_ge(sem["hid_done"], k)
                for t in range(4):
                    last = product(ps[:, 2 + t // 2, (t % 2) * 2 * I:(t % 2 + 1) * 2 * I],
                                   lambda a, c: xt[b][:, a, c, t * P:(t + 1) * P],
                                   lambda a, c: w_gu[:, a, bass.ds(e[t] * (DC * 2 * I) + c * 2 * I, 2 * I)], DC, mm)
                last.then_inc(sem["gu_done"], 1)

            def back_turn(k, first=False):
                pe.wait_ge(sem["hid_done"], k + 1)
                if not first:
                    pe.wait_ge(sem["hid_lo"], k)
                for t in range(4):
                    last = tr(ps[:, 4, t * P:(t + 1) * P], hid[:, t, :], ident[:])
                last.then_inc(sem["hid_turned"], 1)

            def back_products(k, first=False):
                e = experts_of(k)
                pe.wait_ge(sem["hid_lo"], k + 1)
                if not first:
                    pe.wait_ge(sem["y_ready"], k)
                for t in range(4):
                    last = product(ps[:, 5 + t // 2, (t % 2) * D:(t % 2 + 1) * D],
                                   lambda a, c: hid_t[:, a, t * P:(t + 1) * P],
                                   lambda a, c: w_dn[:, a, bass.ds(e[t] * D, D)], 1, mm)
                last.then_inc(sem["y_done"], 1)

            front_turn(0, 0, first=True)
            front_turn(1, 1)
            front_products(0, 0, first=True)
            front_turn(2, 0)
            back_turn(0, first=True)
            front_products(1, 1)
            back_products(0, first=True)
            front_turn(3, 1)
            back_turn(1)
            with pe.Fori(1, FG // 2 - 1) as pair:
                for b in range(2):
                    k = 2 * pair + b
                    front_products(k, b)
                    back_products(k - 1)
                    front_turn(k + 2, b)
                    back_turn(k)
            for b, k in enumerate((FG - 2, FG - 1)):
                front_products(k, b)
                back_products(k - 1)
                back_turn(k)
            back_products(FG - 1)

            def turn_next(job, ch):
                if ch == 0:
                    pe.wait_ge(sem["next_loaded"], 8 * (job + 2))
                for t in range(QT):
                    last = tr(ps[:, 7, t * P:(t + 1) * P], x_next[:, t, ch * P:(ch + 1) * P], ident[:])
                last.then_inc(sem["next_turned"], 1)

            turn_next(0, 0)
            pe.wait_ge(sem["next_lo"], 1)
            turn_next(1, 1)
            pe.wait_ge(sem["y_ready"], FG)

            def step(i, c, has):
                u = has.u

                def project(n):
                    off = n * D + c * P
                    product(ps[:, 7, :], lambda a, ch: w_qkv[:, a, ch, off:off + P],
                            lambda a, ch: xt[0][:, a, ch, :], DC, mm).then_inc(sem["proj_done"], 1)

                def project_values(n):
                    for h in range(2):
                        t = 2 * n + h
                        last = product(ps[:, 7, h * D:(h + 1) * D], lambda a, ch: xt[0][:, a, ch, t * P:(t + 1) * P],
                                       lambda a, ch: w_qkv[:, a, ch, 2 * D:3 * D], DC, mm)
                    last.then_inc(sem["v_done"], 1)

                def turn_maxima(w, g):
                    pe.wait_ge(sem["max_lo"], 2 * w + g + 1)
                    for t in range(QT):
                        last = tr(ps[0:8, 7, t * P:(t + 1) * P], max_parts[:, t].rearrange("p h l -> p (h l)"), ident[:])
                    last.then_inc(sem["max_turned"], 1)

                def spare_job(n):
                    if has.project and n == 0:
                        if c == 0:
                            pe.wait_ge(sem["next_lo"], 2 * (i + 2))
                        else:
                            pe.wait_ge(sem["v_staged"], 2 * (i + 2))
                        project(0)
                    if has.maxima_end and n == 1:
                        if has.project:
                            pe.wait_ge(sem["parts_lo"], 2 * (u + 2) + 1)
                        else:
                            pe.wait_ge(sem["max_evacuated"], 2 * u + 1)
                        turn_maxima(u, 1)
                    if has.project and n == 2:
                        if has.maxima_end:
                            pe.wait_ge(sem["max_evacuated"], 2 * u + 2)
                        else:
                            pe.wait_ge(sem["parts_lo"], 2 * (u + 2) + 1)
                        project(1)
                    if has.project and c == 0 and n == 3:
                        pe.wait_ge(sem["parts_lo"], 2 * (u + 2) + 2)
                        project_values(0)
                    if has.turn and n == 3:
                        pe.wait_ge(sem["parts_lo"], 2 * (u + 2) + 2)
                        turn_next(2 * (i + 2), 0)
                    if has.maxima and n == 4:
                        if has.project and c == 0:
                            pe.wait_ge(sem["v_staged"], 2 * (i + 1) + 1)
                        elif has.turn:
                            pe.wait_ge(sem["next_lo"], 2 * (i + 2) + 1)
                        elif has.project:
                            pe.wait_ge(sem["parts_lo"], 2 * (u + 2) + 2)
                        else:
                            pe.wait_ge(sem["max_evacuated"], 2 * u + 2)
                        turn_maxima(u + 1, 0)
                    if has.project and c == 0 and n == 5:
                        if has.maxima:
                            pe.wait_ge(sem["max_evacuated"], 2 * (u + 1) + 1)
                        else:
                            pe.wait_ge(sem["v_staged"], 2 * (i + 1) + 1)
                        project_values(1)
                    if has.turn and n == 5:
                        pe.wait_ge(sem["max_evacuated"], 2 * (u + 1) + 1)
                        turn_next(2 * (i + 2) + 1, 1)

                def output_job(n):
                    kind, t = OUTPUT_JOBS[c].get(n, none)
                    if not kind or not has.output:
                        return
                    done = 4 * (i - 1) + t
                    if kind == "turn":
                        if t == 0:
                            pe.wait_ge(sem["raw_done"], 4 * i)
                            if later(i, 2):
                                pe.wait_ge(sem["sum_done"], done)
                        else:
                            pe.wait_ge(sem["ctx_done"], done)
                        for g in range(4):
                            last = tr(ps[:, 3, g * P:(g + 1) * P], raw[:, g, t * P:(t + 1) * P], ident[:])
                        last.then_inc(sem["raw_turned"], 1)
                    elif kind == "back":
                        if t == 0:
                            pe.wait_ge(sem["ctx_done"], 4 * i)
                        else:
                            pe.wait_ge(sem["sum_done"], done)
                        flat = ctx_n[:, t].rearrange("p h d -> p (h d)")
                        for ch in range(DC):
                            last = tr(ps[:, 3, ch * P:(ch + 1) * P], flat[:, ch * P:(ch + 1) * P], ident[:])
                        last.then_inc(sem["ctx_turned"], 1)
                    else:
                        pe.wait_ge(sem["ctx_lo"], done + 1)
                        product(ps[:, 3, 0:D], lambda a, ch: ctx_t[:, a, ch, :], lambda a, ch: w_o[:, a, ch, :], DC,
                                mm).then_inc(sem["o_done"], 1)

                def scores_t(n, h):
                    g, item = n // 4, n % 4
                    lo, span = key_span(item)
                    pair, j = 2 * g + h // 2, h % 2
                    e = 4 * n + h
                    if item == 0 and h == 0:
                        pe.wait_ge(sem[f"m_ready{g}"], 64 * (u + 1))
                    if not isinstance(i, int) or 32 * u + e >= 2:
                        pe.wait_ge(sem["ex_done"], 32 * u + e - 1)
                    mm(ps[:, 4 + e % 2, 0:span * P], k_stack[c][0:MAX_ROWS.stop, pair, item * P:(item + 1) * P],
                       q_stack[c][0:MAX_ROWS.stop, PAIRS * j + pair, lo * P:(lo + span) * P], start=True,
                       stop=True).then_inc(sem["st_done"], 1)

                def scores(n):
                    head, tile = n // 4, n % 4
                    pair, j = head // 2, head % 2
                    lo, span = key_span(tile)
                    if n % 16 == 0:
                        pe.wait_ge(sem[f"stack_ready{head // 4}"], 128 * (u + 2))
                    if not isinstance(i, int) or 32 * (u + 1) + n >= 3:
                        pe.wait_ge(sem["s_maxed"], 32 * (u + 1) + (n - 2 if n >= 2 else n - 1))
                    mm(ps[:, n % 3, 0:span * P], q_stack[1 - c][KEY_ROWS, PAIRS * j + pair, tile * P:(tile + 1) * P],
                       k_stack[1 - c][KEY_ROWS, pair, lo * P:(lo + span) * P], start=True, stop=True).then_inc(
                        sem["s_done"], 1)

                def context(w, half, n):
                    g, item = n // 4, n % 4
                    lo, span = key_span(item)
                    pe.wait_ge(sem["masked"], 8 * w + n + 1)
                    if item == 0:
                        if not isinstance(i, int) or 2 * w + g > 0:
                            pe.wait_ge(sem["raw_done"], 2 * w + g)
                        if g == 0:
                            pe.wait_ge(sem["v_copied"], w + 1)
                    for h in range(4):
                        last = mm(ps[32 * h:32 * h + 32, 6, lo * P:(lo + span) * P], v_aug[half][:, item, 4 * g + h, :],
                                  probs[:, item, h, 0:span * P], start=(item == 0), stop=(item == QT - 1),
                                  tile_position=(0, 32 * h), skip_group_check=True)
                    last.then_inc(sem["pv_done"], 1)

                def score_items(n, h):
                    if has.probs:
                        scores_t(n, h)
                    if has.maxima:
                        scores(4 * n + h)

                for n in range(8):
                    score_items(n, 0)
                    score_items(n, 1)
                    spare_job(n)
                    score_items(n, 2)
                    score_items(n, 3)
                    if n == 0 and has.probs_end:
                        context(u - 1, 1 - c, 7)
                    elif n > 0 and has.probs:
                        context(u, c, n - 1)
                    output_job(n)

            pe.wait_ge(sem["ones_ready"], 1)
            attention(pe, step)


def kernel(**inputs):
    import numpy as np
    import concourse.bacc as bacc
    from concourse.bass_utils import run_bass_kernel_spmd

    get = {k: np.asarray(v) for k, v in inputs.items()}

    def by_unit(a):
        qk, v = a[:512], a[512:]
        qk = qk.reshape((2, 2, 4, 2, 16) + a.shape[1:])
        qk = np.moveaxis(qk, 2, 4).reshape((512,) + a.shape[1:])
        return np.concatenate([qk, v])

    arrays = {
        "x": get["L0_attn_x"],
        "w_qkv_t": by_unit(get["L0_attn_w_in"]).T,
        "b_in": by_unit(get["L0_attn_b_in"]),
        "w_out_t": get["L0_attn_w_out"].T,
        "b_out": get["L0_attn_b_out"],
        "gate_t": get["L0_ffn_gate_w"].T,
        "w_gate_t": get["L0_ffn_w_gate"].transpose(0, 2, 1),
        "w_up_t": get["L0_ffn_w_up"].transpose(0, 2, 1),
        "w_down_t": get["L0_ffn_w_down"].transpose(0, 2, 1),
    }
    arrays = {k: np.ascontiguousarray(v) for k, v in arrays.items()}
    nc = bacc.Bacc("TRN2", target_bir_lowering=False, num_devices=1)
    args = [nc.dram_tensor(k, list(a.shape), mybir.dt.from_np(a.dtype), kind="ExternalInput").ap()
            for k, a in arrays.items()]
    shape = list(arrays["x"].shape)
    args.append(nc.dram_tensor("out", shape, F32, kind="ExternalOutput").ap())
    build(nc, *args)
    r = run_bass_kernel_spmd(nc, [arrays], core_ids=[0])
    return r.results[0]["out"]
```

```python
from contextlib import ExitStack

import concourse.bass as bass
from concourse import mybir

ALU = mybir.AluOpType
ACT = mybir.ActivationFunctionType
F32 = mybir.dt.float32
F32R = mybir.dt.float32r
BF16 = mybir.dt.bfloat16
I32 = mybir.dt.int32
U32 = mybir.dt.uint32
AX_X = mybir.AxisListType.X

P = 128
NEG = -1e30
EPS = 1e-5
PRODUCTS = ((0, 0), (0, 1), (1, 0))


def build(nc, x, w_qkv_t, b_in, w_out_t, b_out, gate_t, w_gate_t, w_up_t, w_down_t, out):
    SEQS, T, D = x.shape
    E, _, I = w_gate_t.shape
    HEADS = 16
    HD = D // HEADS
    N = SEQS * T
    TILES = N // P
    QT = T // P
    DC = D // P
    UNIT_HEADS = HEADS // 2
    PAIRS = UNIT_HEADS // 2
    SCALE = 1.0 / HD ** 0.5
    FT = TILES + E
    FG = FT // 4
    ROWS = FT * P
    assert (T, D, I, HD, QT, FT % 4) == (512, 256, 128, 16, 4, 0)

    x_g = x.rearrange("s (t p) d -> s p t d", p=P)
    out_g = out.rearrange("s (t p) d -> s p t d", p=P)
    xn_dram = nc.dram_tensor("xn_scratch", [SEQS, P, QT, D], F32).ap()
    sorted_dram = nc.dram_tensor("sorted_scratch", [ROWS, D], F32).ap()
    y_dram = nc.dram_tensor("expert_out_scratch", [ROWS, D], F32).ap()
    parts_dram = nc.dram_tensor("parts_scratch", [2, 6, P, T], F32).ap()

    with ExitStack() as ctx:
        def sb(name, shape, dt=F32):
            return ctx.enter_context(nc.sbuf_tensor(name, shape, dt))

        ident = sb("ident", [P, P])
        upper_b = sb("upper_b", [P, P], BF16)
        ones_b = sb("ones_b", [P, P], BF16)
        mask = sb("mask", [P, 3, P])
        ones64 = sb("ones64", [P, TILES])
        eps_t = sb("eps_t", [P, 1])
        b_qk = sb("b_qk", [P, 4])
        b_v = sb("b_v", [P, D])
        b_o = sb("b_o", [P, D])
        stage = sb("stage", [P, E * 3 * D])
        stage_qkv = stage[:, 0:DC * 3 * D].rearrange("p (c n) -> p c n", c=DC)
        stage_o = stage[:, DC * 3 * D:DC * 4 * D].rearrange("p (c n) -> p c n", c=DC)
        stage_gate = stage[:, DC * 4 * D:DC * (4 * D + E)].rearrange("p (c e) -> p c e", c=DC)
        w_qkv = sb("w_qkv", [P, 2, DC, 3 * D], F32R)
        w_o = sb("w_o", [P, 2, DC, D], F32R)
        w_gl = sb("w_gl", [P, 2, DC, E], F32R)
        w_gu = sb("w_gu", [P, 2, E * DC * 2 * I], F32R)
        w_dn = sb("w_dn", [P, 2, E * D], F32R)

        logits_and_values = sb("logits_and_values", [P, 2, TILES * E])
        logits, route_a = (logits_and_values[:, n].rearrange("p (t e) -> p t e", e=E) for n in range(2))
        one_hot = sb("one_hot", [P, TILES, E])
        one_hot_b = sb("one_hot_b", [P, TILES, E], BF16)
        top = sb("top", [P, TILES])
        weight = sb("weight", [P, TILES])
        rev = sb("rev", [P, E])
        iota_t = sb("iota_t", [P, TILES])
        iota_f = sb("iota_f", [P, FT])
        small = sb("small", [P, 16, E])
        position = sb("position", [P, TILES], I32)
        pad_position = sb("pad_position", [P, E], I32)
        experts_word = sb("experts_word", [P, FG], I32)
        pos4 = sb("pos4", [P, 2, 4], I32)

        x_in = sb("x_in", [P, 2, QT, D])
        bn = sb("bn", [P, 2, QT, 6])
        mv = sb("mv", [P, 2, QT, 2])
        sd = sb("sd", [P, 2, QT])
        rstd = sb("rstd", [P, 2, QT])
        xn = sb("xn", [P, 2, QT, D])
        cmp_f = x_in[:, 0].rearrange("p t d -> p (t d)")[:, 0:FT * E].rearrange("p (f e) -> p f e", e=E)
        by_e = x_in[:, 1, 0:2].rearrange("p t d -> p (t d)").rearrange("p (e t) -> p e t", e=E)
        cum = x_in[:, 1, 2:4].rearrange("p t d -> p (t d)").rearrange("p (e t) -> p e t", e=E)
        xt = [sb(f"xt{b}", [P, 2, DC, T], F32R) for b in range(2)]

        parts = sb("parts", [P, 4, T])
        q_stack = [sb(f"q_stack{c}", [P, UNIT_HEADS, T], F32R) for c in range(2)]
        k_stack = [w_gu[:, 0, c * PAIRS * T:(c + 1) * PAIRS * T].rearrange("p (a t) -> p a t", t=T) for c in range(2)]
        k_first = xt[1][:].rearrange("p a c t -> p (a c) t")
        KEY_ROWS = slice(0, 6 * HD)
        MAX_ROWS = slice(6 * HD, 6 * HD + 2)
        v_stage = logits_and_values[:].rearrange("p a n -> p (a n)").rearrange("p (t h d) -> p t h d", t=QT, d=HD)
        x_next = sb("x_next", [P, QT, D])
        v_aug = [sb(f"v_aug{c}", [P, QT, UNIT_HEADS, 32]) for c in range(2)]
        neg_max = sb("neg_max", [P, 2, QT, 4])
        max_parts = sb("max_parts", [P, QT, 4, 2])
        max_t = sb("max_t", [8, T])
        probs = stage[:, 0:16 * 3 * P].rearrange("p (r h q) -> p r h q", r=4, h=4)
        raw = sb("raw", [P, 4, T])
        recip = sb("recip", [P, HEADS])
        ctx_n = sb("ctx_n", [P, QT, HEADS, HD])
        s_sum = sb("s_sum", [P, D])
        gated = x_in[:, 1]
        y_in = xn[:, 1]
        logits_t = parts

        zero_rows = ctx_n[:, 0].rearrange("p h d -> p (h d)")
        xs = [xn[:, b] for b in range(2)]
        y_out = [x_in[:, b] for b in range(2)]
        tanh_g, act_g, hid = (parts[:, n].rearrange("p (t i) -> p t i", t=4) for n in range(3))
        hid_t = sb("hid_t", [P, 2, 4 * P], F32R)
        ctx_t = hid_t[:, :, 0:DC * P].rearrange("p a (c t) -> p a c t", c=DC)
        tanh_y = raw[:, 0:2].rearrange("p a n -> p (a n)").rearrange("p (t d) -> p t d", t=4)

        ps = ctx.enter_context(nc.psum_tensor("ps", [P, 8, T], F32))

        names = """small_loaded weights_loaded weights_split consts_pool x_loaded0 x_loaded1 bn_done stats_done sd_done
            rstd_done xn_done xn_stored0 xn_stored1 rows_turned rows_hi rows_lo logits_done logits_copied
            logits_turned logits_kept routed route_link tanh_done onehot_ready counts_done positions_ready
            xn_again0 xn_again1 scaled padded pos_copied scattered0 scattered1 experts_in0 experts_in1
            experts_turned experts_hi experts_lo gu_done tanh_g_done act_g_done hid_done hid_turned hid_hi
            hid_lo y_done tanh_y_done y_ready y_stored0 y_stored1 next_loaded next_turned next_hi next_lo
            proj_done parts_hi parts_lo parts_written v_done v_staged v_copied stack_ready0 stack_ready1 s_done
            s_maxed max_hi max_lo max_turned max_evacuated m_ready0 m_ready1 st_done ex_done masked pv_done
            raw_done raw_turned recip_done ctx_done ctx_turned ctx_hi ctx_lo o_done sum_done gated_done
            residual_loaded residual_ready y_gathered out_ready out_stored ones_ready first_queries_ready
            first_stack_ready waits_passed""".split()
        sem = {name: ctx.enter_context(nc.semaphore(name)) for name in names}

        def carried(eng):
            eng.sem_inc(sem["waits_passed"], 1)

        def later(i, n):
            return not isinstance(i, int) or i >= n

        def product(dst, lhs, rhs, chunks, mm):
            todo = [(c, a, b) for c in range(chunks) for a, b in PRODUCTS]
            for n, (c, a, b) in enumerate(todo):
                last = mm(dst, lhs(a, c), rhs(b, c), start=(n == 0), stop=(n == len(todo) - 1))
            return last

        class Step:
            def __init__(self, i, c):
                inner = not isinstance(i, int)
                u = 2 * i + c
                self.u = u
                self.project = inner or 0 <= i <= SEQS - 2
                self.load_next = c == 0 and (inner or 0 <= i <= SEQS - 3)
                self.turn = c == 1 and (inner or i <= SEQS - 3)
                self.copy_values = inner or -1 <= u <= 2 * SEQS - 2
                self.maxima = inner or 0 <= u <= 2 * SEQS - 2
                self.maxima_end = inner or 1 <= u <= 2 * SEQS - 1
                self.probs = inner or 0 <= u <= 2 * SEQS - 1
                self.probs_end = inner or 1 <= u <= 2 * SEQS
                self.output = inner or 1 <= i <= SEQS

        OUTPUT_JOBS = [
            {1: ("turn", 0), 2: ("turn", 1), 3: ("turn", 2), 4: ("turn", 3), 5: ("back", 0), 6: ("out", 0), 7: ("back", 1)},
            {0: ("out", 1), 1: ("back", 2), 2: ("out", 2), 3: ("back", 3), 4: ("out", 3)},
        ]
        none = (None, None)

        def attention(eng, step):
            for i in (-1, 0, 1):
                for c in range(2):
                    step(i, c, Step(i, c))
            with eng.Fori(2, SEQS - 2) as i:
                for c in range(2):
                    step(i, c, Step(i, c))
            for i in range(SEQS - 2, SEQS + 1):
                for c in range(2):
                    step(i, c, Step(i, c))

        def key_span(tile):
            lo, hi = max(0, tile - 1), min(QT - 1, tile + 1)
            return lo, hi - lo + 1

        def store_parts(eng, c):
            for n in range(3):
                eng.dma_start(parts_dram[c, 2 * n:2 * n + 2].rearrange("b r t -> r b t"), parts[:, n:n + 2]).then_inc(
                    sem["parts_written"], 16)

        def load_stack(eng, g, c, n, done, stack=None):
            src = parts_dram[c].rearrange("b (j d p) t -> j b d (p t)", j=2, d=HD)[:, :, :, 2 * g * T:2 * (g + 1) * T]
            for j in range(2):
                rows, h = slice(3 * HD * j, 3 * HD * (j + 1)), PAIRS * j + 2 * g
                dst = (stack or k_stack[c])[rows, 2 * g:2 * g + 2, :] if n else q_stack[c][rows, h:h + 2, :]
                eng.dma_start(dst.rearrange("r p t -> r (p t)").bitcast(F32), src[j][3 * n:3 * n + 3]).then_inc(done, 16)

        def stack_maxima(eng, u, g, c):
            eng.wait_ge(sem["max_evacuated"], 2 * u + g + 1)
            carried(eng)
            for h in range(4):
                stacked = PAIRS * (h % 2) + 2 * g + h // 2
                eng.dma_start(q_stack[c][MAX_ROWS, stacked, :].bitcast(F32), max_t[2 * h:2 * h + 2, :]).then_inc(
                    sem[f"m_ready{g}"], 16)

        block = ctx.enter_context(nc.Block())

        @block.sync
        def _(sp):
            sp.dma_start(stage_gate, gate_t.rearrange("(c p) e -> p c e", p=P)).then_inc(sem["weights_loaded"], 16)
            sp.dma_start(x_in[:, 0], x_g[0]).then_inc(sem["x_loaded0"], 16)
            sp.dma_start(stage_qkv, w_qkv_t.rearrange("(c p) n -> p c n", p=P)).then_inc(sem["weights_loaded"], 16)
            sp.dma_start(stage_o, w_out_t.rearrange("(c p) n -> p c n", p=P)).then_inc(sem["weights_loaded"], 16)
            for n in range(4):
                sp.dma_start(b_qk[:, n:n + 1], b_in[n * P:(n + 1) * P].rearrange("(p o) -> p o", o=1)).then_inc(
                    sem["small_loaded"], 16)
            sp.dma_start(b_v[:], b_in[2 * D:3 * D].partition_broadcast(P)).then_inc(sem["small_loaded"], 16)
            sp.dma_start(b_o[:], b_out.partition_broadcast(P)).then_inc(sem["small_loaded"], 16)

            def load_rows(i, b, first=False):
                if not first:
                    sp.wait_ge(sem["xn_done"], i - 1)
                    carried(sp)
                sp.dma_start(x_in[:, b], x_g[i]).then_inc(sem[f"x_loaded{b}"], 16)

            def store_rows(i, b):
                sp.wait_ge(sem["xn_done"], i + 1)
                carried(sp)
                sp.dma_start(xn_dram[i], xn[:, b]).then_inc(sem[f"xn_stored{b}"], 16)

            load_rows(1, 1, first=True)
            with sp.Fori(0, SEQS // 2 - 1) as pair:
                store_rows(2 * pair, 0)
                load_rows(2 * pair + 2, 0)
                store_rows(2 * pair + 1, 1)
                load_rows(2 * pair + 3, 1)
            store_rows(SEQS - 2, 0)
            store_rows(SEQS - 1, 1)

            sp.wait_ge(sem["weights_split"], 3)
            gu = stage[:, 0:E * DC * 2 * I].rearrange("p (e c g i) -> p g c e i", e=E, c=DC, g=2)
            for g, w in enumerate((w_gate_t, w_up_t)):
                for c in range(DC):
                    sp.dma_start(gu[:, g, c], w[:, c * P:(c + 1) * P, :].rearrange("e p i -> p e i")).then_inc(
                        sem["weights_loaded"], 16)
            dn = stage[:, E * DC * 2 * I:].rearrange("p (e n) -> p e n", e=E)
            sp.dma_start(dn, w_down_t.rearrange("e i n -> i e n")).then_inc(sem["weights_loaded"], 16)

            sp.wait_ge(sem["xn_stored0"], 8 * SEQS)
            sp.wait_ge(sem["xn_stored1"], 8 * SEQS)
            sp.wait_ge(sem["rows_turned"], SEQS)
            sp.dma_start(xn[:, 0], xn_dram[0]).then_inc(sem["xn_again0"], 16)
            sp.dma_start(xn[:, 1], xn_dram[1]).then_inc(sem["xn_again1"], 16)
            sp.dma_start(x_next[:], xn_dram[0]).then_inc(sem["next_loaded"], 16)
            with sp.Fori(1, SEQS // 2) as pair:
                for b in range(2):
                    sp.wait_ge(sem["scaled"], 2 * pair + b - 1)
                    carried(sp)
                    sp.dma_start(xn[:, b], xn_dram[2 * pair + b]).then_inc(sem[f"xn_again{b}"], 16)

            sp.wait_ge(sem["next_turned"], 2)
            sp.dma_start(x_next[:], xn_dram[1]).then_inc(sem["next_loaded"], 16)
            sp.wait_ge(sem["parts_written"], 96)
            for g in range(2):
                load_stack(sp, g, 1, 0, sem["first_queries_ready"])

            sp.wait_ge(sem["scattered0"], 8 * TILES)
            sp.wait_ge(sem["scattered1"], 8 * TILES)
            sp.wait_ge(sem["padded"], 16 * E)
            xs_dram = sorted_dram.rearrange("(k t p) d -> k p t d", p=P, t=4)
            ys_dram = y_dram.rearrange("(k t p) d -> k p t d", p=P, t=4)

            def experts_load(k, b, first=False):
                if not first:
                    sp.wait_ge(sem["experts_turned"], k - 1)
                    carried(sp)
                sp.dma_start(xs[b], xs_dram[k]).then_inc(sem[f"experts_in{b}"], 16)

            def experts_store(k, b):
                sp.wait_ge(sem["y_ready"], k + 1)
                carried(sp)
                sp.dma_start(ys_dram[k], y_out[b]).then_inc(sem[f"y_stored{b}"], 16)

            experts_load(0, 0, first=True)
            experts_load(1, 1, first=True)
            for k in range(2, 5):
                experts_load(k, k % 2)
            with sp.Fori(0, FG // 2 - 3) as pair:
                for b in range(2):
                    experts_store(2 * pair + b, b)
                    experts_load(2 * pair + b + 5, 1 - b)
            experts_store(FG - 6, 0)
            experts_load(FG - 1, 1)
            for k in range(FG - 5, FG - 2):
                experts_store(k, k % 2)
            sp.wait_ge(sem["gu_done"], FG)
            for g in range(2):
                load_stack(sp, g, 0, 1, sem[f"stack_ready{g}"])
            experts_store(FG - 2, 0)
            experts_store(FG - 1, 1)

            def step(i, c, has):
                u = has.u
                if has.load_next:
                    sp.wait_ge(sem["next_turned"], 2 * (i + 2))
                    carried(sp)
                    sp.dma_start(x_next[:], xn_dram[i + 2]).then_inc(sem["next_loaded"], 16)
                if not later(i, 0) and c == 0:
                    for g in range(2):
                        sp.wait_ge(sem[f"stack_ready{g}"], 32)
                        load_stack(sp, g, 1, 1, sem[f"stack_ready{g}"])
                if has.maxima_end:
                    stack_maxima(sp, u, 1, c)
                if has.project:
                    sp.wait_ge(sem["parts_lo"], 2 * (u + 2) + 2)
                    carried(sp)
                    store_parts(sp, c)
                    sp.wait_ge(sem["parts_written"], 48 * (u + 3))
                    carried(sp)
                    sp.wait_ge(sem["st_done"], 32 * u + 16)
                    carried(sp)
                    sp.wait_ge(sem["stack_ready0"], 64 * (u + 1))
                    carried(sp)
                    load_stack(sp, 0, c, 0, sem["stack_ready0"])
                    load_stack(sp, 0, c, 1, sem["stack_ready0"])
                if has.maxima:
                    stack_maxima(sp, u + 1, 0, 1 - c)
                if has.project:
                    sp.wait_ge(sem["st_done"], 32 * u + 32)
                    carried(sp)
                    sp.wait_ge(sem["stack_ready1"], 64 * (u + 1))
                    carried(sp)
                    load_stack(sp, 1, c, 0, sem["stack_ready1"])
                    load_stack(sp, 1, c, 1, sem["stack_ready1"])
                if c == 1 and has.output:
                    sp.wait_ge(sem["out_ready"], 4 * i)
                    carried(sp)
                    sp.dma_start(out_g[i - 1], gated).then_inc(sem["out_stored"], 16)
                if c == 1 and has.probs:
                    if not later(i, 1):
                        sp.wait_ge(sem["y_stored0"], 8 * FG)
                        sp.wait_ge(sem["y_stored1"], 8 * FG)
                    sp.dma_start(xn[:, 0], xn_dram[i]).then_inc(sem["residual_loaded"], 16)
                    sp.dma_start(x_in[:, 0], x_g[i]).then_inc(sem["residual_loaded"], 16)

            attention(sp, step)
            sp.wait_ge(sem["out_stored"], 16 * SEQS)

        @block.gpsimd
        def _(pool):
            g = nc.gpsimd
            g.memset(ident[:], 0.0)
            g.memset(upper_b[:], 1.0)
            g.memset(mask[:], 0.0)
            g.memset(ones_b[:], 1.0)
            for c in range(2):
                g.memset(q_stack[c][:].bitcast(F32), 0.0)
            g.memset(eps_t[:], EPS).then_inc(sem["consts_pool"], 1)
            pool.wait_ge(sem["consts_pool"], 1)
            g.affine_select(out=ident[:], in_=ident[:], compare_op=ALU.not_equal, fill=1.0, base=0,
                            pattern=[[-1, P]], channel_multiplier=1)
            g.affine_select(out=upper_b[:], in_=upper_b[:], compare_op=ALU.is_gt, fill=0.0, base=0,
                            pattern=[[1, P]], channel_multiplier=-1)
            g.affine_select(out=mask[:, 0], in_=mask[:, 0], compare_op=ALU.is_ge, fill=NEG, base=0,
                            pattern=[[1, P]], channel_multiplier=-1)
            g.affine_select(out=mask[:, 2], in_=mask[:, 2], compare_op=ALU.is_ge, fill=NEG, base=0,
                            pattern=[[-1, P]], channel_multiplier=1)
            g.iota(rev[:], pattern=[[-1, E]], base=E, channel_multiplier=0, allow_small_or_imprecise_dtypes=True)
            g.iota(iota_t[:], pattern=[[P, TILES]], base=0, channel_multiplier=0, allow_small_or_imprecise_dtypes=True)
            g.iota(iota_f[:], pattern=[[1, FT]], base=0, channel_multiplier=0, allow_small_or_imprecise_dtypes=True)
            g.iota(small[:, 0], pattern=[[P, E]], base=0, channel_multiplier=1,
                   allow_small_or_imprecise_dtypes=True).then_inc(sem["consts_pool"], 1)

            def rows_at(ap):
                return bass.IndirectOffsetOnAxis(ap=ap, axis=0)

            pool.wait_ge(sem["positions_ready"], 1)
            for n in range(E):
                g.indirect_dma_start(out=sorted_dram[:, :], out_offset=rows_at(pad_position[:, n:n + 1]),
                                     in_=zero_rows, in_offset=None).then_inc(sem["padded"], 16)

            def scatter(i, b, first=False):
                if not first:
                    pool.wait_ge(sem[f"scattered{b}"], 32 * (i - b))
                    carried(pool)
                g.tensor_copy(pos4[:, b], position[:, bass.ds(i * 4, 4)]).then_inc(sem["pos_copied"], 1)
                pool.wait_ge(sem["pos_copied"], i + 1)
                carried(pool)
                pool.wait_ge(sem["scaled"], i + 1)
                carried(pool)
                for t in range(4):
                    g.indirect_dma_start(out=sorted_dram[:, :], out_offset=rows_at(pos4[:, b, t:t + 1]),
                                         in_=x_in[:, b, t, :], in_offset=None).then_inc(sem[f"scattered{b}"], 16)

            scatter(0, 0, first=True)
            scatter(1, 1, first=True)
            with pool.Fori(1, SEQS // 2) as pair:
                scatter(2 * pair, 0)
                scatter(2 * pair + 1, 1)

            pool.wait_ge(sem["gu_done"], FG)
            for c in range(2):
                last = g.memset(k_stack[c][P - 32:P].bitcast(F32), 1.0)
            last.then_inc(sem["ones_ready"], 1)
            pool.wait_ge(sem["ones_ready"], 1)
            pool.wait_ge(sem["small_loaded"], 96)
            pool.wait_ge(sem["y_stored0"], 8 * FG)
            pool.wait_ge(sem["y_stored1"], 8 * FG)

            def step(i, c, has):
                u = has.u
                for n in range(8):
                    if has.probs:
                        item = n % 4
                        lo, span = key_span(item)
                        pool.wait_ge(sem["ex_done"], 32 * u + 4 * n + 4)
                        carried(pool)
                        if item > 0:
                            v = probs[:, item, :, 0:P]
                            last = g.affine_select(out=v, in_=v, compare_op=ALU.is_ge, fill=0.0, base=0,
                                                   pattern=[[0, 4], [1, P]], channel_multiplier=-1)
                        if item < QT - 1:
                            v = probs[:, item, :, (span - 1) * P:span * P]
                            last = g.affine_select(out=v, in_=v, compare_op=ALU.is_ge, fill=0.0, base=0,
                                                   pattern=[[0, 4], [-1, P]], channel_multiplier=1)
                        last.then_inc(sem["masked"], 1)
                    if n == 1 and has.copy_values:
                        if c == 1 or not later(i, 0):
                            pool.wait_ge(sem["v_staged"], 2 * (i + 2))
                            carried(pool)
                        if later(u if isinstance(i, int) else i, 1):
                            pool.wait_ge(sem["pv_done"], 8 * u)
                            carried(pool)
                        half = (1 - c) * UNIT_HEADS
                        g.tensor_copy(v_aug[1 - c][:, :, :, 0:HD],
                                      v_stage[:, :, half:half + UNIT_HEADS, :]).then_inc(sem["v_copied"], 1)
                    if c == 0 and n in (2, 3, 4, 5) and has.output:
                        if n == 2:
                            pool.wait_ge(sem["residual_loaded"], 32 * i)
                            carried(pool)
                        g.tensor_tensor(xn[:, 0, n - 2], xn[:, 0, n - 2], b_o[:], ALU.add).then_inc(
                            sem["residual_ready"], 1)
                    kind, t = OUTPUT_JOBS[c].get(n - 1, none) if n else ((OUTPUT_JOBS[0][7]) if c else none)
                    if kind == "out" and has.output:
                        pool.wait_ge(sem["gated_done"], 4 * (i - 1) + t + 1)
                        carried(pool)
                        g.tensor_tensor(gated[:, t], gated[:, t], x_in[:, 0, t], ALU.add).then_inc(sem["out_ready"], 1)
                    if c == 1 and n >= 6 and has.probs:
                        if n == 6:
                            if later(i, 1):
                                pool.wait_ge(sem["y_gathered"], 64 * i)
                                carried(pool)
                            g.tensor_copy(pos4[:, 0], position[:, bass.ds(i * 4, 4)]).then_inc(sem["pos_copied"], 1)
                            pool.wait_ge(sem["pos_copied"], SEQS + i + 1)
                            carried(pool)
                            if later(i, 1):
                                pool.wait_ge(sem["gated_done"], 4 * i)
                                carried(pool)
                        for t in (0, 1) if n == 6 else (2, 3):
                            g.indirect_dma_start(out=y_in[:, t, :], out_offset=None, in_=y_dram[:, :],
                                                 in_offset=rows_at(pos4[:, 0, t:t + 1])).then_inc(sem["y_gathered"], 16)

            attention(pool, step)

        @block.scalar
        def _(act):
            a = nc.scalar

            def deviation(i, b):
                act.wait_ge(sem["stats_done"], i + 1)
                a.activation(sd[:, b, :], mv[:, b, :, 1], ACT.Sqrt, bias=eps_t[:]).then_inc(sem["sd_done"], 1)

            def rows_hi(i, b, first=False):
                act.wait_ge(sem["rows_turned"], i + 1)
                if not first:
                    act.wait_ge(sem["logits_done"], i - 1)
                a.activation(xt[b][:, 0], ps[:, 2 * b:2 * b + 2, :], ACT.Copy).then_inc(sem["rows_hi"], 1)

            def copy_logits(i, b, first=False):
                act.wait_ge(sem["logits_done"], i + 1)
                if not first:
                    act.wait_ge(sem["logits_turned"], i - 1)
                a.activation(logits_t[0:E, b], ps[0:E, 4 + b, :], ACT.Copy).then_inc(sem["logits_copied"], 1)

            act.wait_ge(sem["consts_pool"], 1)
            deviation(0, 0)
            deviation(1, 1)
            rows_hi(0, 0, first=True)
            deviation(2, 0)
            copy_logits(0, 0, first=True)
            rows_hi(1, 1, first=True)
            deviation(3, 1)
            copy_logits(1, 1, first=True)
            rows_hi(2, 0)
            with act.Fori(2, SEQS // 2) as pair:
                deviation(2 * pair, 0)
                copy_logits(2 * pair - 2, 0)
                rows_hi(2 * pair - 1, 1)
                deviation(2 * pair + 1, 1)
                copy_logits(2 * pair - 1, 1)
                rows_hi(2 * pair, 0)
            copy_logits(SEQS - 2, 0)
            rows_hi(SEQS - 1, 1)
            copy_logits(SEQS - 1, 1)

            act.wait_ge(sem["routed"], 1)
            a.activation(weight[:], top[:], ACT.Tanh, scale=0.5).then_inc(sem["tanh_done"], 1)

            def next_hi(job, ch):
                act.wait_ge(sem["next_turned"], job + 1)
                a.activation(xt[0][:, 0, ch], ps[:, 7, :], ACT.Copy).then_inc(sem["next_hi"], 1)

            def part_hi(w, c, n, first=False):
                act.wait_ge(sem["proj_done"], 2 * w + n + 1)
                if n == 0 and not first:
                    act.wait_ge(sem["parts_written"], 48 * w)
                col = 2 * n + c
                a.activation(parts[:, 1 + n].bitcast(F32R), ps[:, 7, :], ACT.Identity,
                             bias=b_qk[:, col:col + 1]).then_inc(sem["parts_hi"], 1)

            act.wait_ge(sem["small_loaded"], 96)
            next_hi(0, 0)
            next_hi(1, 1)
            for w in range(2):
                part_hi(w, w, 0, first=(w == 0))
                if w == 1:
                    for g in range(2):
                        load_stack(act, g, 0, 0, sem["first_stack_ready"])
                        load_stack(act, g, 0, 1, sem["first_stack_ready"], k_first)
                part_hi(w, w, 1)
                act.wait_ge(sem["parts_lo"], 2 * w + 2)
                store_parts(act, w)
            for g in range(2):
                stack_maxima(act, 0, g, 0)
            act.wait_ge(sem["parts_written"], 96)

            def two_banks(b):
                return ps[:, b:b + 2, :].rearrange("p b (t n) -> p (b t) n", t=2)

            def experts_hi(k, b, first=False):
                act.wait_ge(sem["experts_turned"], k + 1)
                if not first:
                    act.wait_ge(sem["gu_done"], k - 1)
                a.activation(xt[b][:, 0], ps[:, 0:2, :], ACT.Copy).then_inc(sem["experts_hi"], 1)

            def gate_tanh(k, first=False):
                act.wait_ge(sem["gu_done"], k + 1)
                if not first:
                    act.wait_ge(sem["hid_done"], k)
                a.activation(tanh_g, two_banks(2)[:, :, 0:I], ACT.Tanh, scale=0.5).then_inc(sem["tanh_g_done"], 1)

            def hid_hi(k, first=False):
                act.wait_ge(sem["hid_turned"], k + 1)
                if not first:
                    act.wait_ge(sem["y_done"], k)
                a.activation(hid_t[:, 0], ps[:, 4, :], ACT.Copy).then_inc(sem["hid_hi"], 1)

            def result_tanh(k, first=False):
                act.wait_ge(sem["y_done"], k + 1)
                if not first:
                    act.wait_ge(sem["y_ready"], k)
                a.activation(tanh_y, two_banks(5), ACT.Tanh, scale=0.5).then_inc(sem["tanh_y_done"], 1)

            experts_hi(0, 0, first=True)
            experts_hi(1, 1, first=True)
            gate_tanh(0, first=True)
            experts_hi(2, 0)
            hid_hi(0, first=True)
            gate_tanh(1)
            result_tanh(0, first=True)
            experts_hi(3, 1)
            hid_hi(1)
            with act.Fori(1, FG // 2 - 1) as pair:
                for b in range(2):
                    k = 2 * pair + b
                    gate_tanh(k)
                    result_tanh(k - 1)
                    experts_hi(k + 2, b)
                    hid_hi(k)
            for k in (FG - 2, FG - 1):
                gate_tanh(k)
                result_tanh(k - 1)
                hid_hi(k)
            result_tanh(FG - 1)

            def step(i, c, has):
                u = has.u

                def exp(n, h):
                    lo, span = key_span(n % 4)
                    e = 4 * n + h
                    act.wait_ge(sem["st_done"], 32 * u + e + 1)
                    if h == 0 and (not isinstance(i, int) or 8 * u + n - 3 > 0):
                        act.wait_ge(sem["pv_done"], 8 * u + n - 3)
                    a.activation(probs[:, n % 4, h, 0:span * P], ps[:, 4 + e % 2, 0:span * P], ACT.Exp,
                                 scale=SCALE).then_inc(sem["ex_done"], 1)

                for n in range(8):
                    if has.probs:
                        exp(n, 0)
                        exp(n, 1)
                    if has.project and n == 0:
                        part_hi(u + 2, c, 0)
                    if has.project and n == 2:
                        part_hi(u + 2, c, 1)
                    if has.turn and n in (3, 5):
                        next_hi(2 * (i + 2) + n // 5, n // 5)
                    if has.probs:
                        exp(n, 2)
                        exp(n, 3)
                    if n == 0 and has.probs_end or n == 4 and has.probs:
                        act.wait_ge(sem["pv_done"], 8 * u + n)
                        if n == 4 and c == 0 and later(i, 1):
                            act.wait_ge(sem["raw_turned"], 4 * i)
                        a.activation(raw[:, (2 * c + n // 4 - 1) % 4], ps[:, 6, :], ACT.Copy).then_inc(
                            sem["raw_done"], 1)
                    kind, t = OUTPUT_JOBS[c].get(n, none)
                    if kind == "back" and has.output:
                        act.wait_ge(sem["ctx_turned"], 4 * (i - 1) + t + 1)
                        a.activation(ctx_t[:, 0], ps[:, 3, 0:DC * P].rearrange("p (c t) -> p c t", c=DC),
                                     ACT.Copy).then_inc(sem["ctx_hi"], 1)

            attention(act, step)

        @block.vector
        def _(dve):
            v = nc.vector
            links = [0]

            def link(ins):
                links[0] += 1
                ins.then_inc(sem["route_link"], 1)
                dve.wait_ge(sem["route_link"], links[0])

            v.memset(ones64[:], 1.0)
            v.memset(zero_rows, 0.0)
            for c in range(2):
                v.memset(v_aug[c][:], 1.0)

            def split(dst, src):
                link(v.tensor_copy(dst(0), src))
                return v.tensor_tensor(dst(1), src, dst(0).bitcast(F32), ALU.subtract)

            dve.wait_ge(sem["weights_loaded"], 48)
            split(lambda h: w_gl[:, h], stage_gate).then_inc(sem["weights_split"], 1)
            split(lambda h: w_qkv[:, h], stage_qkv).then_inc(sem["weights_split"], 1)
            split(lambda h: w_o[:, h], stage_o).then_inc(sem["weights_split"], 1)

            def statistics(i, b):
                dve.wait_ge(sem[f"x_loaded{b}"], 8 * (i - b) + 16)
                for t in range(QT):
                    last = v.bn_stats(bn[:, b, t], x_in[:, b, t])
                last.then_inc(sem["bn_done"], 1)
                dve.wait_ge(sem["bn_done"], i + 1)
                if not isinstance(i, int):
                    carried(dve)
                for t in range(QT):
                    last = v.bn_aggr(mv[:, b, t], bn[:, b, t])
                last.then_inc(sem["stats_done"], 1)

            def normalise(i, b, first=False):
                dve.wait_ge(sem["sd_done"], i + 1)
                v.reciprocal(rstd[:, b], sd[:, b]).then_inc(sem["rstd_done"], 1)
                dve.wait_ge(sem["rstd_done"], i + 1)
                if not first:
                    dve.wait_ge(sem[f"xn_stored{b}"], 8 * (i - b))
                    dve.wait_ge(sem["rows_turned"], i - 1)
                for t in range(QT):
                    last = v.tensor_scalar(xn[:, b, t], x_in[:, b, t], mv[:, b, t, 0:1], rstd[:, b, t:t + 1],
                                           ALU.subtract, ALU.mult)
                last.then_inc(sem["xn_done"], 1)

            def rows_lo(i, b):
                dve.wait_ge(sem["rows_hi"], i + 1)
                v.tensor_tensor(xt[b][:, 1], ps[:, 2 * b:2 * b + 2, :], xt[b][:, 0].bitcast(F32),
                                ALU.subtract).then_inc(sem["rows_lo"], 1)

            def keep_logits(i, b):
                dve.wait_ge(sem["logits_turned"], i + 1)
                v.tensor_copy(logits[:, bass.ds(i * QT, QT), :],
                              ps[:, 6 + b, 0:QT * E].rearrange("p (t e) -> p t e", t=QT)).then_inc(sem["logits_kept"], 1)

            statistics(0, 0)
            normalise(0, 0, first=True)
            statistics(1, 1)
            normalise(1, 1, first=True)
            statistics(2, 0)
            rows_lo(0, 0)
            normalise(2, 0)
            statistics(3, 1)
            rows_lo(1, 1)
            normalise(3, 1)
            keep_logits(0, 0)
            with dve.Fori(2, SEQS // 2) as pair:
                statistics(2 * pair, 0)
                rows_lo(2 * pair - 2, 0)
                normalise(2 * pair, 0)
                keep_logits(2 * pair - 3, 1)
                statistics(2 * pair + 1, 1)
                rows_lo(2 * pair - 1, 1)
                normalise(2 * pair + 1, 1)
                keep_logits(2 * pair - 2, 0)
            rows_lo(SEQS - 2, 0)
            keep_logits(SEQS - 3, 1)
            rows_lo(SEQS - 1, 1)
            keep_logits(SEQS - 2, 0)
            keep_logits(SEQS - 1, 1)
            dve.wait_ge(sem["logits_kept"], SEQS)

            tb = [P, TILES, E]
            dve.wait_ge(sem["consts_pool"], 2)
            link(v.reduce_max(top[:], logits, AX_X))
            v.tensor_tensor(route_a, logits, top[:].unsqueeze(2).to_broadcast(tb),
                            ALU.is_equal).then_inc(sem["routed"], 1)
            dve.wait_ge(sem["routed"], 1)
            link(v.tensor_tensor(route_a, route_a, rev[:].unsqueeze(1).to_broadcast(tb), ALU.mult))
            link(v.reduce_max(cum[:, 0, :], route_a, AX_X))
            link(v.tensor_tensor(one_hot[:], rev[:].unsqueeze(1).to_broadcast(tb),
                                 cum[:, 0, :].unsqueeze(2).to_broadcast(tb), ALU.is_equal))
            v.tensor_copy(one_hot_b[:], one_hot[:]).then_inc(sem["onehot_ready"], 1)
            dve.wait_ge(sem["tanh_done"], 1)
            link(v.tensor_scalar(weight[:], weight[:], 0.5, 0.5, ALU.mult, ALU.add))
            dve.wait_ge(sem["counts_done"], 1)
            before = ps[:, 0, :].rearrange("p (t e) -> p t e", e=E)
            total = ps[:, 1, :].rearrange("p (t e) -> p t e", e=E)
            for e in range(E):
                last = v.tensor_tensor_scan(cum[:, e, :], ones64[:], total[:, :, e], 0.0, ALU.mult, ALU.add)
            link(last)
            count, tiles, ends, base = (small[:, n] for n in (4, 5, 6, 7))
            link(v.tensor_copy(count, cum[:, :, TILES - 1]))
            link(v.tensor_tensor(by_e, count.unsqueeze(2).to_broadcast([P, E, TILES]),
                                 iota_t[:].unsqueeze(1).to_broadcast([P, E, TILES]), ALU.is_gt))
            link(v.reduce_sum(tiles, by_e, AX_X))
            link(v.tensor_tensor_scan(ends, ones64[:, 0:E], tiles, 0.0, ALU.mult, ALU.add))
            link(v.tensor_tensor(base, ends, tiles, ALU.subtract))
            link(v.tensor_scalar(base, base, float(P), None, ALU.mult))
            link(v.tensor_tensor(route_a, cum.rearrange("p e t -> p t e"), total, ALU.subtract))
            link(v.tensor_tensor(route_a, route_a, before, ALU.add))
            link(v.tensor_tensor(route_a, route_a, base.unsqueeze(1).to_broadcast(tb), ALU.add))
            link(v.tensor_tensor(route_a, route_a, one_hot[:], ALU.mult))
            link(v.reduce_sum(top[:], route_a, AX_X))
            link(v.tensor_copy(position[:], top[:]))
            tokens, pads_before = small[:, 9], small[:, 10]
            link(v.tensor_tensor_scan(tokens, ones64[:, 0:E], count, 0.0, ALU.mult, ALU.add))
            link(v.tensor_tensor(tokens, tokens, count, ALU.subtract))
            link(v.tensor_tensor(pads_before, base, tokens, ALU.subtract))
            eb = [P, E, E]
            begun, place = by_e[:, :, 0:E], small[:, 11]
            link(v.tensor_tensor(begun, small[:, 0].unsqueeze(2).to_broadcast(eb),
                                 pads_before.unsqueeze(1).to_broadcast(eb), ALU.is_ge))
            link(v.tensor_tensor(begun, begun, count.unsqueeze(1).to_broadcast(eb), ALU.mult))
            link(v.reduce_sum(place, begun, AX_X))
            link(v.tensor_tensor(place, place, small[:, 0], ALU.add))
            link(v.tensor_copy(pad_position[:], place))
            link(v.tensor_tensor(cmp_f, iota_f[:].unsqueeze(2).to_broadcast([P, FT, E]),
                                 ends.unsqueeze(1).to_broadcast([P, FT, E]), ALU.is_ge))
            link(v.reduce_sum(iota_f[:], cmp_f, AX_X))
            link(v.tensor_scalar(iota_f[:], iota_f[:], float(E - 1), None, ALU.min))
            digit = iota_f[:].rearrange("p (k t) -> p t k", t=4)
            word = digit[:, 3]
            for t in (2, 1, 0):
                link(v.scalar_tensor_tensor(out=word, in0=word, scalar=float(E), in1=digit[:, t], op0=ALU.mult,
                                            op1=ALU.add))
            v.tensor_copy(experts_word[:], word).then_inc(sem["positions_ready"], 1)

            def scale(i, b, first=False):
                dve.wait_ge(sem[f"xn_again{b}"], 8 * (i - b) + 16)
                if not first:
                    dve.wait_ge(sem[f"scattered{b}"], 32 * (i - b))
                w = weight[:, bass.ds(i * QT, QT)].unsqueeze(2).to_broadcast([P, QT, D])
                v.tensor_tensor(x_in[:, b], xn[:, b], w, ALU.mult).then_inc(sem["scaled"], 1)

            scale(0, 0, first=True)
            scale(1, 1, first=True)
            dve.wait_ge(sem["weights_loaded"], 16 * 8)
            split(lambda h: w_gu[:, h], stage[:, 0:E * DC * 2 * I]).then_inc(sem["weights_split"], 1)
            split(lambda h: w_dn[:, h], stage[:, E * DC * 2 * I:]).then_inc(sem["weights_split"], 1)

            def next_lo(job, ch):
                dve.wait_ge(sem["next_hi"], job + 1)
                v.tensor_tensor(xt[0][:, 1, ch], ps[:, 7, :], xt[0][:, 0, ch].bitcast(F32), ALU.subtract).then_inc(
                    sem["next_lo"], 1)

            def part_lo(w, c, n):
                hi, lo = (1, 0) if n == 0 else (2, 3)
                dve.wait_ge(sem["parts_hi"], 2 * w + n + 1)
                v.scalar_tensor_tensor(out=parts[:, lo].bitcast(F32R), in0=ps[:, 7, :],
                                       scalar=b_qk[:, 2 * n + c:2 * n + c + 1], in1=parts[:, hi], op0=ALU.add,
                                       op1=ALU.subtract).then_inc(sem["parts_lo"], 1)

            def stage_values(seq, n, first=False):
                dve.wait_ge(sem["v_done"], 2 * seq + n + 1)
                if n == 0 and not first:
                    dve.wait_ge(sem["v_copied"], 2 * seq)
                bias = b_v[:].rearrange("p (h d) -> p h d", d=HD).unsqueeze(1).to_broadcast([P, 2, HEADS, HD])
                v.tensor_tensor(v_stage[:, 2 * n:2 * n + 2], ps[:, 7, :].rearrange("p (t h d) -> p t h d", t=2, d=HD),
                                bias, ALU.add).then_inc(sem["v_staged"], 1)

            dve.wait_ge(sem["small_loaded"], 96)
            scale(2, 0)
            next_lo(0, 0)
            scale(3, 1)
            next_lo(1, 1)
            scale(4, 0)
            part_lo(0, 0, 0)
            scale(5, 1)
            part_lo(0, 0, 1)
            scale(6, 0)
            stage_values(0, 0, first=True)
            scale(7, 1)
            stage_values(0, 1)
            scale(8, 0)
            part_lo(1, 1, 0)
            scale(9, 1)
            part_lo(1, 1, 1)

            def row_max(w, n):
                head, tile = n // 4, n % 4
                lo, span = key_span(tile)
                first = 1 if tile == 0 else 0
                dve.wait_ge(sem["s_done"], 32 * w + n + 1)
                carried(dve)
                v.tensor_tensor_reduce(out=ps[:, n % 3, 0:span * P], in0=ps[:, n % 3, 0:span * P],
                                       in1=mask[:, first:first + span].rearrange("p b k -> p (b k)"),
                                       scale=-1.0, scalar=-NEG, op0=ALU.add, op1=ALU.min,
                                       accum_out=neg_max[:, head // 4, tile, head % 4:head % 4 + 1]).then_inc(
                    sem["s_maxed"], 1)

            def split_maxima(w, g):
                m = 2 * w + g
                dve.wait_ge(sem["s_maxed"], 32 * w + 16 * g + 16)
                if not isinstance(m, int) or m > 0:
                    dve.wait_ge(sem["max_turned"], m)
                v.tensor_copy(max_parts[:, :, :, 0].bitcast(F32R), neg_max[:, g]).then_inc(sem["max_hi"], 1)
                dve.wait_ge(sem["max_hi"], m + 1)
                v.tensor_tensor(max_parts[:, :, :, 1].bitcast(F32R), neg_max[:, g], max_parts[:, :, :, 0],
                                ALU.subtract).then_inc(sem["max_lo"], 1)

            def evacuate_maxima(w, g):
                m = 2 * w + g
                dve.wait_ge(sem["max_turned"], m + 1)
                if not isinstance(m, int) or m > 0:
                    dve.wait_ge(sem[f"m_ready{1 - g}"], 64 * (w + g))
                v.tensor_copy(max_t[:], ps[0:8, 7, :]).then_inc(sem["max_evacuated"], 1)

            for seq in range(10, SEQS):
                scale(seq, seq % 2)
                share = UNIT_HEADS * QT / (SEQS - 10)
                for n in range(int(share * (seq - 10)), int(share * (seq - 9))):
                    row_max(0, n)
                    if n == 19:
                        split_maxima(0, 0)
                    if n == 23:
                        evacuate_maxima(0, 0)
            split_maxima(0, 1)
            evacuate_maxima(0, 1)

            def two_banks(b):
                return ps[:, b:b + 2, :].rearrange("p b (t n) -> p (b t) n", t=2)

            def experts_lo(k, b):
                dve.wait_ge(sem["experts_hi"], k + 1)
                v.tensor_tensor(xt[b][:, 1], ps[:, 0:2, :], xt[b][:, 0].bitcast(F32), ALU.subtract).then_inc(
                    sem["experts_lo"], 1)

            def hid_lo(k):
                dve.wait_ge(sem["hid_hi"], k + 1)
                v.tensor_tensor(hid_t[:, 1], ps[:, 4, :], hid_t[:, 0].bitcast(F32), ALU.subtract).then_inc(sem["hid_lo"], 1)

            def gate(k, first=False):
                dve.wait_ge(sem["tanh_g_done"], k + 1)
                v.scalar_tensor_tensor(out=act_g, in0=tanh_g, scalar=1.0, in1=two_banks(2)[:, :, 0:I], op0=ALU.add,
                                       op1=ALU.mult).then_inc(sem["act_g_done"], 1)
                dve.wait_ge(sem["act_g_done"], k + 1)
                if not first:
                    dve.wait_ge(sem["hid_turned"], k)
                v.scalar_tensor_tensor(out=hid, in0=act_g, scalar=0.5, in1=two_banks(2)[:, :, I:2 * I], op0=ALU.mult,
                                       op1=ALU.mult).then_inc(sem["hid_done"], 1)

            def result(k, b, first=False):
                dve.wait_ge(sem["tanh_y_done"], k + 1)
                if not first:
                    dve.wait_ge(sem[f"y_stored{b}"], 8 * (k - b))
                v.scalar_tensor_tensor(out=y_out[b], in0=tanh_y, scalar=1.0, in1=two_banks(5), op0=ALU.add,
                                       op1=ALU.mult).then_inc(sem["y_ready"], 1)

            experts_lo(0, 0)
            experts_lo(1, 1)
            gate(0, first=True)
            experts_lo(2, 0)
            hid_lo(0)
            gate(1)
            result(0, 0, first=True)
            experts_lo(3, 1)
            hid_lo(1)
            with dve.Fori(1, FG // 2 - 1) as pair:
                for b in range(2):
                    k = 2 * pair + b
                    gate(k)
                    result(k - 1, 1 - b)
                    experts_lo(k + 2, b)
                    hid_lo(k)
            gate(FG - 2)
            result(FG - 3, 1)
            hid_lo(FG - 2)
            gate(FG - 1)
            result(FG - 2, 0)
            hid_lo(FG - 1)
            result(FG - 1, 1)

            def step(i, c, has):
                u = has.u

                for n in range(8):
                    if has.maxima:
                        for item in range(4 * n, 4 * n + 3):
                            row_max(u + 1, item)
                    if has.project and n == 0:
                        part_lo(u + 2, c, 0)
                    if has.maxima_end and n == 1:
                        evacuate_maxima(u, 1)
                    if has.project and n == 2:
                        part_lo(u + 2, c, 1)
                    if has.maxima and n == 4:
                        evacuate_maxima(u + 1, 0)
                    if has.maxima:
                        row_max(u + 1, 4 * n + 3)
                    if has.maxima and n == 3:
                        split_maxima(u + 1, 0)
                    if has.maxima and n == 7:
                        split_maxima(u + 1, 1)
                    if has.project and c == 0 and n in (3, 5):
                        stage_values(i + 1, n // 5)
                    if has.turn and n in (3, 5):
                        next_lo(2 * (i + 2) + n // 5, n // 5)
                    kind, t = OUTPUT_JOBS[c].get(n, none)
                    done = 4 * (i - 1) + t if kind and has.output else 0
                    if kind == "turn" and has.output:
                        view = ps[:, 3, :].rearrange("p (h d) -> p h d", d=32)
                        dve.wait_ge(sem["raw_turned"], done + 1)
                        v.reciprocal(recip[:], view[:, :, HD]).then_inc(sem["recip_done"], 1)
                        dve.wait_ge(sem["recip_done"], done + 1)
                        if t == 0 and later(i, 2):
                            dve.wait_ge(sem["ctx_turned"], done)
                        v.tensor_tensor(ctx_n[:, t], view[:, :, 0:HD],
                                        recip[:].unsqueeze(2).to_broadcast([P, HEADS, HD]), ALU.mult).then_inc(
                            sem["ctx_done"], 1)
                    if kind == "back" and has.output:
                        dve.wait_ge(sem["ctx_hi"], done + 1)
                        v.tensor_tensor(ctx_t[:, 1], ps[:, 3, 0:DC * P].rearrange("p (c t) -> p c t", c=DC),
                                        ctx_t[:, 0].bitcast(F32), ALU.subtract).then_inc(sem["ctx_lo"], 1)
                    if kind == "out" and has.output:
                        dve.wait_ge(sem["o_done"], done + 1)
                        dve.wait_ge(sem["residual_ready"], done + 1)
                        v.tensor_tensor(s_sum[:], ps[:, 3, 0:D], xn[:, 0, t], ALU.add).then_inc(sem["sum_done"], 1)
                        dve.wait_ge(sem["sum_done"], done + 1)
                        if t == 0:
                            dve.wait_ge(sem["y_gathered"], 64 * i)
                            if later(i, 2):
                                dve.wait_ge(sem["out_stored"], 16 * (i - 1))
                        v.scalar_tensor_tensor(out=gated[:, t], in0=y_in[:, t], scalar=0.5, in1=s_sum[:], op0=ALU.mult,
                                               op1=ALU.mult).then_inc(sem["gated_done"], 1)

            attention(dve, step)

        @block.tensor
        def _(pe):
            mm = nc.tensor.matmul
            tr = nc.tensor.transpose

            pe.wait_ge(sem["consts_pool"], 2)

            def turn(i, b, first=False):
                pe.wait_ge(sem["xn_done"], i + 1)
                if not first:
                    pe.wait_ge(sem["rows_lo"], i - 1)
                for c in range(DC):
                    for t in range(QT):
                        last = tr(ps[:, 2 * b + c, t * P:(t + 1) * P], xn[:, b, t, c * P:(c + 1) * P], ident[:])
                last.then_inc(sem["rows_turned"], 1)

            def gate_logits(i, b, first=False):
                pe.wait_ge(sem["rows_lo"], i + 1)
                if not first:
                    pe.wait_ge(sem["logits_copied"], i - 1)
                product(ps[0:E, 4 + b, :], lambda a, c: w_gl[:, a, c, :], lambda a, c: xt[b][:, a, c, :], DC, mm).then_inc(
                    sem["logits_done"], 1)

            def logits_back(i, b, first=False):
                pe.wait_ge(sem["logits_copied"], i + 1)
                carried(pe)
                if not first:
                    pe.wait_ge(sem["logits_kept"], i - 1)
                    carried(pe)
                for t in range(QT):
                    last = tr(ps[:, 6 + b, t * E:(t + 1) * E], logits_t[0:E, b, t * P:(t + 1) * P], ident[0:E, 0:E])
                last.then_inc(sem["logits_turned"], 1)

            turn(0, 0, first=True)
            turn(1, 1, first=True)
            pe.wait_ge(sem["weights_split"], 1)
            gate_logits(0, 0, first=True)
            turn(2, 0)
            logits_back(0, 0, first=True)
            gate_logits(1, 1, first=True)
            turn(3, 1)
            logits_back(1, 1, first=True)
            gate_logits(2, 0)
            with pe.Fori(2, SEQS // 2) as pair:
                turn(2 * pair, 0)
                logits_back(2 * pair - 2, 0)
                gate_logits(2 * pair - 1, 1)
                turn(2 * pair + 1, 1)
                logits_back(2 * pair - 1, 1)
                gate_logits(2 * pair, 0)
            logits_back(SEQS - 2, 0)
            gate_logits(SEQS - 1, 1)
            logits_back(SEQS - 1, 1)

            pe.wait_ge(sem["onehot_ready"], 1)
            oh = one_hot_b[:].rearrange("p t e -> p (t e)")
            mm(ps[:, 0, :], upper_b[:], oh, start=True, stop=True)
            mm(ps[:, 1, :], ones_b[:], oh, start=True, stop=True).then_inc(sem["counts_done"], 1)

            def turn_next(job, ch):
                if ch == 0:
                    pe.wait_ge(sem["next_loaded"], 8 * (job + 2))
                for t in range(QT):
                    last = tr(ps[:, 7, t * P:(t + 1) * P], x_next[:, t, ch * P:(ch + 1) * P], ident[:])
                last.then_inc(sem["next_turned"], 1)

            def project(w, c, n):
                off = n * D + c * P
                product(ps[:, 7, :], lambda a, ch: w_qkv[:, a, ch, off:off + P],
                        lambda a, ch: xt[0][:, a, ch, :], DC, mm).then_inc(sem["proj_done"], 1)

            def project_values(seq, n):
                for h in range(2):
                    t = 2 * n + h
                    last = product(ps[:, 7, h * D:(h + 1) * D], lambda a, ch: xt[0][:, a, ch, t * P:(t + 1) * P],
                                   lambda a, ch: w_qkv[:, a, ch, 2 * D:3 * D], DC, mm)
                last.then_inc(sem["v_done"], 1)

            pe.wait_ge(sem["weights_split"], 3)
            turn_next(0, 0)
            pe.wait_ge(sem["next_lo"], 1)
            turn_next(1, 1)
            pe.wait_ge(sem["next_lo"], 2)
            project(0, 0, 0)
            pe.wait_ge(sem["parts_lo"], 1)
            project(0, 0, 1)
            pe.wait_ge(sem["parts_lo"], 2)
            project_values(0, 0)
            pe.wait_ge(sem["v_staged"], 1)
            project_values(0, 1)
            pe.wait_ge(sem["v_staged"], 2)
            project(1, 1, 0)
            pe.wait_ge(sem["parts_lo"], 3)
            project(1, 1, 1)

            def scores(w, c, n, first_keys=None):
                head, tile = n // 4, n % 4
                pair, j = head // 2, head % 2
                lo, span = key_span(tile)
                if not isinstance(w, int) or 32 * w + n >= 3:
                    pe.wait_ge(sem["s_maxed"], 32 * w + (n - 2 if n >= 2 else n - 1))
                keys = first_keys or k_stack[c]
                mm(ps[:, n % 3, 0:span * P], q_stack[c][KEY_ROWS, PAIRS * j + pair, tile * P:(tile + 1) * P],
                   keys[KEY_ROWS, pair, lo * P:(lo + span) * P], start=True, stop=True).then_inc(sem["s_done"], 1)

            def turn_maxima(w, g):
                pe.wait_ge(sem["max_lo"], 2 * w + g + 1)
                for t in range(QT):
                    last = tr(ps[0:8, 7, t * P:(t + 1) * P], max_parts[:, t].rearrange("p h l -> p (h l)"), ident[:])
                last.then_inc(sem["max_turned"], 1)

            pe.wait_ge(sem["positions_ready"], 1)
            pe.wait_ge(sem["first_stack_ready"], 128)
            for n in range(UNIT_HEADS * QT):
                scores(0, 0, n, k_first)
                if n == 21:
                    pe.wait_ge(sem["parts_lo"], 4)
                    turn_maxima(0, 0)
            pe.wait_ge(sem["max_evacuated"], 1)
            turn_maxima(0, 1)
            pe.wait_ge(sem["s_maxed"], UNIT_HEADS * QT)

            pe.wait_ge(sem["weights_split"], 5)

            def front_turn(k, b, first=False):
                pe.wait_ge(sem[f"experts_in{b}"], 8 * (k - b) + 16)
                if not first:
                    pe.wait_ge(sem["experts_lo"], k)
                for c in range(DC):
                    for t in range(4):
                        last = tr(ps[:, c, t * P:(t + 1) * P], xs[b][:, t, c * P:(c + 1) * P], ident[:])
                last.then_inc(sem["experts_turned"], 1)

            def experts_of(k):
                word = pe.value_load(experts_word[0:1, bass.ds(k, 1)], min_val=0, max_val=E ** 4 - 1)
                return [word // E ** t % E for t in range(4)]

            def front_products(k, b, first=False):
                e = experts_of(k)
                pe.wait_ge(sem["experts_lo"], k + 1)
                if not first:
                    pe.wait_ge(sem["hid_done"], k)
                for t in range(4):
                    last = product(ps[:, 2 + t // 2, (t % 2) * 2 * I:(t % 2 + 1) * 2 * I],
                                   lambda a, c: xt[b][:, a, c, t * P:(t + 1) * P],
                                   lambda a, c: w_gu[:, a, bass.ds(e[t] * (DC * 2 * I) + c * 2 * I, 2 * I)], DC, mm)
                last.then_inc(sem["gu_done"], 1)

            def back_turn(k, first=False):
                pe.wait_ge(sem["hid_done"], k + 1)
                if not first:
                    pe.wait_ge(sem["hid_lo"], k)
                for t in range(4):
                    last = tr(ps[:, 4, t * P:(t + 1) * P], hid[:, t, :], ident[:])
                last.then_inc(sem["hid_turned"], 1)

            def back_products(k, first=False):
                e = experts_of(k)
                pe.wait_ge(sem["hid_lo"], k + 1)
                if not first:
                    pe.wait_ge(sem["y_ready"], k)
                for t in range(4):
                    last = product(ps[:, 5 + t // 2, (t % 2) * D:(t % 2 + 1) * D],
                                   lambda a, c: hid_t[:, a, t * P:(t + 1) * P],
                                   lambda a, c: w_dn[:, a, bass.ds(e[t] * D, D)], 1, mm)
                last.then_inc(sem["y_done"], 1)

            front_turn(0, 0, first=True)
            front_turn(1, 1)
            front_products(0, 0, first=True)
            front_turn(2, 0)
            back_turn(0, first=True)
            front_products(1, 1)
            back_products(0, first=True)
            front_turn(3, 1)
            back_turn(1)
            with pe.Fori(1, FG // 2 - 1) as pair:
                for b in range(2):
                    k = 2 * pair + b
                    front_products(k, b)
                    back_products(k - 1)
                    front_turn(k + 2, b)
                    back_turn(k)
            for b, k in enumerate((FG - 2, FG - 1)):
                front_products(k, b)
                back_products(k - 1)
                back_turn(k)
            back_products(FG - 1)

            pe.wait_ge(sem["hid_done"], FG)

            def step(i, c, has):
                u = has.u

                def spare_job(n):
                    if has.project and n == 0:
                        if c == 0:
                            pe.wait_ge(sem["next_lo"], 2 * (i + 2))
                        else:
                            pe.wait_ge(sem["v_staged"], 2 * (i + 2))
                        project(u + 2, c, 0)
                    if has.maxima_end and n == 1:
                        if has.project:
                            pe.wait_ge(sem["parts_lo"], 2 * (u + 2) + 1)
                        else:
                            pe.wait_ge(sem["max_evacuated"], 2 * u + 1)
                        turn_maxima(u, 1)
                    if has.project and n == 2:
                        if has.maxima_end:
                            pe.wait_ge(sem["max_evacuated"], 2 * u + 2)
                        else:
                            pe.wait_ge(sem["parts_lo"], 2 * (u + 2) + 1)
                        project(u + 2, c, 1)
                    if has.project and c == 0 and n == 3:
                        pe.wait_ge(sem["parts_lo"], 2 * (u + 2) + 2)
                        project_values(i + 1, 0)
                    if has.turn and n == 3:
                        pe.wait_ge(sem["parts_lo"], 2 * (u + 2) + 2)
                        turn_next(2 * (i + 2), 0)
                    if has.maxima and n == 4:
                        if has.project and c == 0:
                            pe.wait_ge(sem["v_staged"], 2 * (i + 1) + 1)
                        elif has.turn:
                            pe.wait_ge(sem["next_lo"], 2 * (i + 2) + 1)
                        elif has.project:
                            pe.wait_ge(sem["parts_lo"], 2 * (u + 2) + 2)
                        else:
                            pe.wait_ge(sem["max_evacuated"], 2 * u + 2)
                        turn_maxima(u + 1, 0)
                    if has.project and c == 0 and n == 5:
                        if has.maxima:
                            pe.wait_ge(sem["max_evacuated"], 2 * (u + 1) + 1)
                        else:
                            pe.wait_ge(sem["v_staged"], 2 * (i + 1) + 1)
                        project_values(i + 1, 1)
                    if has.turn and n == 5:
                        if has.maxima:
                            pe.wait_ge(sem["max_evacuated"], 2 * (u + 1) + 1)
                        else:
                            pe.wait_ge(sem["next_lo"], 2 * (i + 2) + 1)
                        turn_next(2 * (i + 2) + 1, 1)

                def output_job(n):
                    kind, t = OUTPUT_JOBS[c].get(n, none)
                    if not kind or not has.output:
                        return
                    done = 4 * (i - 1) + t
                    if kind == "turn":
                        if t == 0:
                            pe.wait_ge(sem["raw_done"], 4 * i)
                            if later(i, 2):
                                pe.wait_ge(sem["sum_done"], done)
                        else:
                            pe.wait_ge(sem["ctx_done"], done)
                        for g in range(4):
                            last = tr(ps[:, 3, g * P:(g + 1) * P], raw[:, g, t * P:(t + 1) * P], ident[:])
                        last.then_inc(sem["raw_turned"], 1)
                    elif kind == "back":
                        if t == 0:
                            pe.wait_ge(sem["ctx_done"], 4 * i)
                        else:
                            pe.wait_ge(sem["sum_done"], done)
                        flat = ctx_n[:, t].rearrange("p h d -> p (h d)")
                        for ch in range(DC):
                            last = tr(ps[:, 3, ch * P:(ch + 1) * P], flat[:, ch * P:(ch + 1) * P], ident[:])
                        last.then_inc(sem["ctx_turned"], 1)
                    else:
                        pe.wait_ge(sem["ctx_lo"], done + 1)
                        product(ps[:, 3, 0:D], lambda a, ch: ctx_t[:, a, ch, :], lambda a, ch: w_o[:, a, ch, :], DC,
                                mm).then_inc(sem["o_done"], 1)

                def scores_t(n, h):
                    g, item = n // 4, n % 4
                    lo, span = key_span(item)
                    pair, j = 2 * g + h // 2, h % 2
                    e = 4 * n + h
                    if item == 0 and h == 0:
                        pe.wait_ge(sem[f"m_ready{g}"], 64 * (u + 1))
                        if isinstance(u, int) and u == 0:
                            pe.wait_ge(sem[f"stack_ready{g}"], 32)
                    if not isinstance(i, int) or 32 * u + e >= 2:
                        pe.wait_ge(sem["ex_done"], 32 * u + e - 1)
                    mm(ps[:, 4 + e % 2, 0:span * P], k_stack[c][0:MAX_ROWS.stop, pair, item * P:(item + 1) * P],
                       q_stack[c][0:MAX_ROWS.stop, PAIRS * j + pair, lo * P:(lo + span) * P], start=True,
                       stop=True).then_inc(sem["st_done"], 1)

                def context(w, half, n):
                    g, item = n // 4, n % 4
                    lo, span = key_span(item)
                    pe.wait_ge(sem["masked"], 8 * w + n + 1)
                    if item == 0:
                        if not isinstance(i, int) or 2 * w + g > 0:
                            pe.wait_ge(sem["raw_done"], 2 * w + g)
                        if g == 0:
                            pe.wait_ge(sem["v_copied"], w + 1)
                    for h in range(4):
                        last = mm(ps[32 * h:32 * h + 32, 6, lo * P:(lo + span) * P], v_aug[half][:, item, 4 * g + h, :],
                                  probs[:, item, h, 0:span * P], start=(item == 0), stop=(item == QT - 1),
                                  tile_position=(0, 32 * h), skip_group_check=True)
                    last.then_inc(sem["pv_done"], 1)

                def score_items(n, h):
                    if has.probs:
                        scores_t(n, h)
                    if has.maxima:
                        if n % 4 == 0 and h == 0:
                            if isinstance(u, int) and u == 0:
                                pe.wait_ge(sem["first_queries_ready"], 64)
                            pe.wait_ge(sem[f"stack_ready{n // 4}"], 64 * (u + 1))
                        scores(u + 1, 1 - c, 4 * n + h)

                if c == 0 and later(i, 0) and not later(i, 1):
                    pe.wait_ge(sem["y_ready"], FG)
                for n in range(8):
                    score_items(n, 0)
                    score_items(n, 1)
                    spare_job(n)
                    score_items(n, 2)
                    score_items(n, 3)
                    if n == 0 and has.probs_end:
                        context(u - 1, 1 - c, 7)
                    elif n > 0 and has.probs:
                        context(u, c, n - 1)
                    output_job(n)

            pe.wait_ge(sem["ones_ready"], 1)
            attention(pe, step)


def kernel(**inputs):
    import numpy as np
    import concourse.bacc as bacc
    from concourse.bass_utils import run_bass_kernel_spmd

    get = {k: np.asarray(v) for k, v in inputs.items()}

    def by_unit(a):
        qk, v = a[:512], a[512:]
        qk = qk.reshape((2, 2, 4, 2, 16) + a.shape[1:])
        qk = np.moveaxis(qk, 2, 4).reshape((512,) + a.shape[1:])
        return np.concatenate([qk, v])

    arrays = {
        "x": get["L0_attn_x"],
        "w_qkv_t": by_unit(get["L0_attn_w_in"]).T,
        "b_in": by_unit(get["L0_attn_b_in"]),
        "w_out_t": get["L0_attn_w_out"].T,
        "b_out": get["L0_attn_b_out"],
        "gate_t": get["L0_ffn_gate_w"].T,
        "w_gate_t": get["L0_ffn_w_gate"].transpose(0, 2, 1),
        "w_up_t": get["L0_ffn_w_up"].transpose(0, 2, 1),
        "w_down_t": get["L0_ffn_w_down"].transpose(0, 2, 1),
    }
    arrays = {k: np.ascontiguousarray(v) for k, v in arrays.items()}
    nc = bacc.Bacc("TRN2", target_bir_lowering=False, num_devices=1)
    args = [nc.dram_tensor(k, list(a.shape), mybir.dt.from_np(a.dtype), kind="ExternalInput").ap()
            for k, a in arrays.items()]
    shape = list(arrays["x"].shape)
    args.append(nc.dram_tensor("out", shape, F32, kind="ExternalOutput").ap())
    build(nc, *args)
    r = run_bass_kernel_spmd(nc, [arrays], core_ids=[0])
    return r.results[0]["out"]
```
